# Optimizing a Trainium2 kernel written in Bass

```python
import numpy as np
import jax
import jax.numpy as jnp

def _softmax(x, axis=-1):
    return jax.nn.softmax(x, axis=axis)

def _gelu(x):
    return jax.nn.gelu(x, approximate=True)

def _silu(x):
    return jax.nn.silu(x)

def _sigmoid(x):
    return jax.nn.sigmoid(x)

def _layernorm(x, axis=-1, eps=1e-05):
    m = jnp.mean(x, axis=axis, keepdims=True)
    v = jnp.var(x, axis=axis, keepdims=True)
    return (x - m) / jnp.sqrt(v + eps)

def _scatter_add(tgt, idx, src, axis=0):
    return tgt.at[idx].add(src)

def _segment_sum(src, seg, n):
    return jax.ops.segment_sum(src, seg, n)
kernel_name = 'mk_macaron_d4_jaxref_r8_f071fb'

def setup_inputs(seed: int=0):
    np.random.seed(seed)
    _w = jnp.asarray

    def _L0_attn_setup():
        import jax, jax.numpy as jnp
        import numpy as np
        import math
        B, L, HID, NH = (4, 512, 128, 8)
        DH = HID // NH
        THETA = 10000.0

        def _rope_tables(seq_len, dh):
            half = dh // 2
            inv_freq = 1.0 / THETA ** (jnp.arange(half, dtype=jnp.float32) / half)
            freqs = jnp.arange(seq_len, dtype=jnp.float32)[:, None] * inv_freq[None, :]
            return (jnp.cos(freqs), jnp.sin(freqs))

        def _apply_rope(x, cos, sin):
            half = x.shape[-1] // 2
            x1, x2 = (x[..., :half], x[..., half:2 * half])
            c = cos[None, None]
            s = sin[None, None]
            return jnp.concatenate([x1 * c - x2 * s, x1 * s + x2 * c], axis=-1)
        key = jax.random.key(seed)
        ks = jax.random.split(key, 9)

        def xav(k, sh):
            lim = math.sqrt(6.0 / (sh[0] + sh[1]))
            return jax.random.uniform(k, sh, jnp.float32, -lim, lim)
        return {'x': jax.random.normal(ks[0], (B, L, HID), jnp.float32), 'norm_w': jnp.ones((HID,), jnp.float32), 'Wq': xav(ks[1], (HID, HID)), 'Wk': xav(ks[2], (HID, HID)), 'Wv': xav(ks[3], (HID, HID)), 'Wbeta': xav(ks[4], (NH, HID)), 'bbeta': jnp.full((NH,), 2.0, jnp.float32), 'Wig': xav(ks[5], (NH, HID)), 'big': jnp.zeros((NH,), jnp.float32), 'Wog': xav(ks[6], (NH, HID)), 'bog': jnp.zeros((NH,), jnp.float32), 'Wout': xav(ks[7], (HID, HID)), 'bout': jnp.zeros((HID,), jnp.float32)}
    _L0_attn_in = _L0_attn_setup()

    def _L0_ffn_setup():
        import jax, jax.numpy as jnp
        import numpy as np
        DIM = 128
        DEPTH = 2
        HEADS = 8
        DIM_HEAD = 64
        WINDOW = 64
        INNER = HEADS * DIM_HEAD
        HID = int(DIM * 4 * 2 / 3)
        B, N = (2, 1024)
        QK_SCALE = 8.0

        def shift_token(t):
            t1, t2 = jnp.split(t, 2, axis=-1)
            t2 = jnp.pad(t2, ((0, 0), (1, 0), (0, 0)))[:, :-1]
            return jnp.concatenate([t1, t2], axis=-1)

        def l2norm(t):
            return t / jnp.clip(jnp.linalg.norm(t, axis=-1, keepdims=True), 1e-12)

        def rotate_half(x):
            x1, x2 = jnp.split(x, 2, axis=-1)
            return jnp.concatenate([-x2, x1], axis=-1)

        def rotary_xpos(q, k):
            n = q.shape[-2]
            half_idx = jnp.arange(0, DIM_HEAD, 2, dtype=jnp.float32)
            inv_freq = 1.0 / 10000.0 ** (half_idx / DIM_HEAD)
            t = jnp.arange(n, dtype=jnp.float32)
            freqs = t[:, None] * inv_freq[None, :]
            freqs = jnp.concatenate([freqs, freqs], axis=-1)
            base = (half_idx + 0.4 * DIM_HEAD) / (1.4 * DIM_HEAD)
            power = (t - n // 2) / float(WINDOW // 2)
            scale = base[None, :] ** power[:, None]
            scale = jnp.concatenate([scale, scale], axis=-1)
            cos, sin = (jnp.cos(freqs), jnp.sin(freqs))
            q = q * cos * scale + rotate_half(q) * sin * scale
            k = k * cos / scale + rotate_half(k) * sin / scale
            return (q, k)

        def local_attention(q, k, v):
            b, h, n, d = q.shape
            w = n // WINDOW
            bq = q.reshape(b, h, w, WINDOW, d) * QK_SCALE
            bk = k.reshape(b, h, w, WINDOW, d)
            bv = v.reshape(b, h, w, WINDOW, d)

            def look_around(t):
                p = jnp.pad(t, ((0, 0), (0, 0), (1, 0), (0, 0), (0, 0)))
                return jnp.concatenate([p[:, :, :w], p[:, :, 1:]], axis=3)
            bk, bv = (look_around(bk), look_around(bv))
            bt = jnp.arange(n).reshape(w, WINDOW)
            btp = jnp.pad(bt, ((1, 0), (0, 0)), constant_values=-1)
            btk = jnp.concatenate([btp[:w], btp[1:]], axis=1)
            sim = jnp.einsum('bhwid,bhwjd->bhwij', bq, bk)
            i = bt[:, :, None]
            j = btk[:, None, :]
            mask = (i < j) | (i > j + WINDOW) | (j == -1)
            sim = jnp.where(mask, -jnp.finfo(sim.dtype).max, sim)
            attn = jax.nn.softmax(sim, axis=-1)
            out = jnp.einsum('bhwij,bhwjd->bhwid', attn, bv)
            return out.reshape(b, h, n, d)

        def _layer(x, wqkv, qs, ksc, wo, lg, lb, w1, b1, w2, b2):
            b, n, _ = x.shape
            h = shift_token(x)
            qkv = h @ wqkv
            q, k, v = jnp.split(qkv, 3, axis=-1)
            to_heads = lambda t: t.reshape(b, n, HEADS, DIM_HEAD).transpose(0, 2, 1, 3)
            q, k, v = (to_heads(q), to_heads(k), to_heads(v))
            q = l2norm(q) * qs
            k = l2norm(k) * ksc
            q, k = rotary_xpos(q, k)
            o = local_attention(q, k, v)
            o = o.transpose(0, 2, 1, 3).reshape(b, n, INNER)
            x = x + o @ wo
            h = shift_token(x)
            mu = h.mean(-1, keepdims=True)
            var = h.var(-1, keepdims=True)
            h = (h - mu) / jnp.sqrt(var + 1e-05) * lg + lb
            h = h @ w1 + b1
            a, g = jnp.split(h, 2, axis=-1)
            h = a * jax.nn.gelu(g, approximate=False)
            x = x + h @ w2 + b2
            return x
        key = jax.random.key(seed)
        ks = jax.random.split(key, 6)
        return {'x': jax.random.normal(ks[0], (B, N, DIM), jnp.float32), 'wqkv': jax.random.normal(ks[1], (DEPTH, DIM, 3 * INNER), jnp.float32) * 0.02, 'q_scale': jnp.ones((DEPTH, DIM_HEAD), jnp.float32), 'k_scale': jnp.ones((DEPTH, DIM_HEAD), jnp.float32), 'wo': jax.random.normal(ks[2], (DEPTH, INNER, DIM), jnp.float32) * 0.02, 'ln_g': jnp.ones((DEPTH, DIM), jnp.float32), 'ln_b': jnp.zeros((DEPTH, DIM), jnp.float32), 'w1': jax.random.normal(ks[3], (DEPTH, DIM, 2 * HID), jnp.float32) * 0.02, 'b1': jnp.zeros((DEPTH, 2 * HID), jnp.float32), 'w2': jax.random.normal(ks[4], (DEPTH, HID, DIM), jnp.float32) * 0.02, 'b2': jnp.zeros((DEPTH, DIM), jnp.float32)}
    _L0_ffn_in = _L0_ffn_setup()

    def _L1_attn_setup():
        import jax, jax.numpy as jnp
        import numpy as np
        H = 16
        ROPE_BASE = 10000.0

        def _rotate_half(x):
            d = x.shape[-1]
            return jnp.concatenate((-x[..., d // 2:], x[..., :d // 2]), axis=-1)
        key = jax.random.key(seed)
        ks = jax.random.split(key, 9)
        B, S, E = (4, 256, 128)
        s = 0.02
        return {'x': jax.random.normal(ks[0], (B, S, E), dtype=jnp.float32), 'wq': jax.random.normal(ks[1], (E, E), dtype=jnp.float32) * s, 'bq': jax.random.normal(ks[2], (E,), dtype=jnp.float32) * s, 'wk': jax.random.normal(ks[3], (E, E), dtype=jnp.float32) * s, 'bk': jax.random.normal(ks[4], (E,), dtype=jnp.float32) * s, 'wv': jax.random.normal(ks[5], (E, E), dtype=jnp.float32) * s, 'bv': jax.random.normal(ks[6], (E,), dtype=jnp.float32) * s, 'wo': jax.random.normal(ks[7], (E, E), dtype=jnp.float32) * s, 'bo': jax.random.normal(ks[8], (E,), dtype=jnp.float32) * s}
    _L1_attn_in = _L1_attn_setup()

    def _L1_ffn_setup():
        import jax, jax.numpy as jnp
        import numpy as np
        D_IN, D_HID = (128, 512)

        def _ternary(key, shape):
            return jax.random.randint(key, shape, -1, 2).astype(jnp.float32)

        def _tlin(x, w, s):
            return jnp.einsum('bsi,oi->bso', x, w) * s
        key = jax.random.key(seed)
        ks = jax.random.split(key, 12)
        inv = lambda fan: 1.0 / np.sqrt(fan).astype(np.float32)
        return {'x': jax.random.normal(ks[0], (4, 256, D_IN), dtype=jnp.float32), 'w1_w': _ternary(ks[1], (D_HID, D_IN)), 'w1_s': jax.random.uniform(ks[2], (D_HID,), dtype=jnp.float32) * inv(D_IN), 'w2_w': _ternary(ks[3], (D_HID, D_IN)), 'w2_s': jax.random.uniform(ks[4], (D_HID,), dtype=jnp.float32) * inv(D_IN), 'h1_w': _ternary(ks[5], (D_HID, D_HID)), 'h1_s': jax.random.uniform(ks[6], (D_HID,), dtype=jnp.float32) * inv(D_HID), 'h2_w': _ternary(ks[7], (D_HID, D_HID)), 'h2_s': jax.random.uniform(ks[8], (D_HID,), dtype=jnp.float32) * inv(D_HID), 'w3_w': _ternary(ks[9], (D_IN, D_HID)), 'w3_s': jax.random.uniform(ks[10], (D_IN,), dtype=jnp.float32) * inv(D_HID)}
    _L1_ffn_in = _L1_ffn_setup()

    def _L2_attn_setup():
        import jax, jax.numpy as jnp
        import numpy as np
        EPS = 1e-05
        WINDOW = 32
        N_HEADS = 16
        key = jax.random.key(seed)
        k1, k2, k3 = jax.random.split(key, 3)
        B, S, D = (2, 256, 128)
        x = jax.random.normal(k1, (B, S, D), dtype=jnp.float32)
        gamma = jnp.ones((D,), dtype=jnp.float32)
        beta = jnp.zeros((D,), dtype=jnp.float32)
        W_qkv = jax.random.normal(k2, (3 * D, D), dtype=jnp.float32) * (1.0 / np.sqrt(D))
        W_out = jax.random.normal(k3, (D, D), dtype=jnp.float32) * (1.0 / np.sqrt(D))
        return {'x': x, 'gamma': gamma, 'beta': beta, 'W_qkv': W_qkv, 'W_out': W_out}
    _L2_attn_in = _L2_attn_setup()

    def _L2_ffn_setup():
        import jax, jax.numpy as jnp
        import numpy as np
        BLOCK = 16
        _GRID = jnp.array([0.0, 0.5, 1.0, 1.5, 2.0, 3.0, 4.0, 6.0], dtype=jnp.float32)
        _MID = jnp.array([0.25, 0.75, 1.25, 1.75, 2.5, 3.5, 5.0], dtype=jnp.float32)

        def fp4_quant_dequant(x):
            shape = x.shape
            xb = x.reshape(shape[:-1] + (shape[-1] // BLOCK, BLOCK))
            scale = jnp.max(jnp.abs(xb), axis=-1, keepdims=True) / 6.0
            scale = jnp.maximum(scale, jnp.float32(1e-12))
            xn = xb / scale
            idx = jnp.searchsorted(_MID, jnp.abs(xn))
            q = _GRID[idx] * jnp.sign(xn) * scale
            return q.reshape(shape)

        def fp4_linear(x, w):
            xq = fp4_quant_dequant(x)
            wq = fp4_quant_dequant(w)
            return jnp.einsum('bsk,nk->bsn', xq, wq)
        key = jax.random.key(seed)
        k1, k2, k3, k4 = jax.random.split(key, 4)
        H, I = (128, 352)
        x = jax.random.normal(k1, (4, 512, H), dtype=jnp.float32)
        w_gate = jax.random.normal(k2, (I, H), dtype=jnp.float32) * 0.02
        w_up = jax.random.normal(k3, (I, H), dtype=jnp.float32) * 0.02
        w_down = jax.random.normal(k4, (H, I), dtype=jnp.float32) * 0.02
        return {'x': x, 'w_gate': w_gate, 'w_up': w_up, 'w_down': w_down}
    _L2_ffn_in = _L2_ffn_setup()

    def _L3_attn_setup():
        import jax, jax.numpy as jnp
        import numpy as np
        B, T, D, H = (4, 256, 128, 16)
        HD = D // H
        MIX = 0.05

        def _deltanet_forward(x, Wq, Wk, Wv, Wo, Wb, Wfd, bfd, Wsd, bsd, Wg):
            b, t, dm = x.shape

            def heads(W):
                return (x @ W.T).reshape(b, t, H, HD).transpose(0, 2, 1, 3)
            q = jax.nn.silu(heads(Wq))
            k = jax.nn.silu(heads(Wk))
            v = jax.nn.silu(heads(Wv))
            beta = jax.nn.sigmoid(x @ Wb.T).transpose(0, 2, 1)
            fd = jax.nn.sigmoid(x @ Wfd.T + bfd).transpose(0, 2, 1)
            sd = jax.nn.sigmoid(x @ Wsd.T + bsd).transpose(0, 2, 1)
            qT = jnp.moveaxis(q, 2, 0)
            kT = jnp.moveaxis(k, 2, 0)
            vT = jnp.moveaxis(v, 2, 0)
            bT = jnp.moveaxis(beta, 2, 0)
            fT = jnp.moveaxis(fd, 2, 0)
            sT = jnp.moveaxis(sd, 2, 0)

            def step(carry, inp):
                Sf, Ss = carry
                qt, kt, vt, bt, ft, st = inp
                Sf = Sf * ft[..., None]
                Ss = Ss * st[..., None]
                o = 0.5 * qt * (Sf + Ss)
                upd = bt[..., None] * kt * vt
                Sf = Sf + upd
                Ss = Ss + upd
                Sf_new = Sf + MIX * Ss
                Ss = Ss + MIX * Sf
                return ((Sf_new, Ss), o)
            S0 = jnp.zeros((b, H, HD), x.dtype)
            _, oT = jax.lax.scan(step, (S0, S0), (qT, kT, vT, bT, fT, sT))
            o = jnp.moveaxis(oT, 0, 2)
            o = o.transpose(0, 2, 1, 3).reshape(b, t, dm)
            g = jax.nn.sigmoid(x @ Wg.T)
            return o * g @ Wo.T
        key = jax.random.key(seed)
        ks = jax.random.split(key, 10)
        s = 0.02
        return {'x': jax.random.normal(ks[0], (B, T, D), jnp.float32), 'Wq': jax.random.normal(ks[1], (D, D), jnp.float32) * s, 'Wk': jax.random.normal(ks[2], (D, D), jnp.float32) * s, 'Wv': jax.random.normal(ks[3], (D, D), jnp.float32) * s, 'Wo': jax.random.normal(ks[4], (D, D), jnp.float32) * s, 'Wb': jax.random.normal(ks[5], (H, D), jnp.float32) * s, 'Wfd': jax.random.normal(ks[6], (H, D), jnp.float32) * s, 'bfd': jnp.zeros((H,), jnp.float32), 'Wsd': jax.random.normal(ks[7], (H, D), jnp.float32) * s, 'bsd': jnp.zeros((H,), jnp.float32), 'Wg': jax.random.normal(ks[8], (D, D), jnp.float32) * s}
    _L3_attn_in = _L3_attn_setup()

    def _L3_ffn_setup():
        import jax, jax.numpy as jnp
        import numpy as np
        D_IN, D_HID = (128, 512)

        def _ternary(key, shape):
            return jax.random.randint(key, shape, -1, 2).astype(jnp.float32)

        def _tlin(x, w, s):
            return jnp.einsum('bsi,oi->bso', x, w) * s
        key = jax.random.key(seed)
        ks = jax.random.split(key, 12)
        inv = lambda fan: 1.0 / np.sqrt(fan).astype(np.float32)
        return {'x': jax.random.normal(ks[0], (4, 256, D_IN), dtype=jnp.float32), 'w1_w': _ternary(ks[1], (D_HID, D_IN)), 'w1_s': jax.random.uniform(ks[2], (D_HID,), dtype=jnp.float32) * inv(D_IN), 'w2_w': _ternary(ks[3], (D_HID, D_IN)), 'w2_s': jax.random.uniform(ks[4], (D_HID,), dtype=jnp.float32) * inv(D_IN), 'h1_w': _ternary(ks[5], (D_HID, D_HID)), 'h1_s': jax.random.uniform(ks[6], (D_HID,), dtype=jnp.float32) * inv(D_HID), 'h2_w': _ternary(ks[7], (D_HID, D_HID)), 'h2_s': jax.random.uniform(ks[8], (D_HID,), dtype=jnp.float32) * inv(D_HID), 'w3_w': _ternary(ks[9], (D_IN, D_HID)), 'w3_s': jax.random.uniform(ks[10], (D_IN,), dtype=jnp.float32) * inv(D_HID)}
    _L3_ffn_in = _L3_ffn_setup()
    _d = {'L0_attn_x': _L0_attn_in['x'], 'L0_attn_norm_w': _L0_attn_in['norm_w'], 'L0_attn_Wq': _L0_attn_in['Wq'], 'L0_attn_Wk': _L0_attn_in['Wk'], 'L0_attn_Wv': _L0_attn_in['Wv'], 'L0_attn_Wbeta': _L0_attn_in['Wbeta'], 'L0_attn_bbeta': _L0_attn_in['bbeta'], 'L0_attn_Wig': _L0_attn_in['Wig'], 'L0_attn_big': _L0_attn_in['big'], 'L0_attn_Wog': _L0_attn_in['Wog'], 'L0_attn_bog': _L0_attn_in['bog'], 'L0_attn_Wout': _L0_attn_in['Wout'], 'L0_attn_bout': _L0_attn_in['bout'], 'L0_ffn_wqkv': _L0_ffn_in['wqkv'], 'L0_ffn_q_scale': _L0_ffn_in['q_scale'], 'L0_ffn_k_scale': _L0_ffn_in['k_scale'], 'L0_ffn_wo': _L0_ffn_in['wo'], 'L0_ffn_ln_g': _L0_ffn_in['ln_g'], 'L0_ffn_ln_b': _L0_ffn_in['ln_b'], 'L0_ffn_w1': _L0_ffn_in['w1'], 'L0_ffn_b1': _L0_ffn_in['b1'], 'L0_ffn_w2': _L0_ffn_in['w2'], 'L0_ffn_b2': _L0_ffn_in['b2'], 'L1_attn_wq': _L1_attn_in['wq'], 'L1_attn_bq': _L1_attn_in['bq'], 'L1_attn_wk': _L1_attn_in['wk'], 'L1_attn_bk': _L1_attn_in['bk'], 'L1_attn_wv': _L1_attn_in['wv'], 'L1_attn_bv': _L1_attn_in['bv'], 'L1_attn_wo': _L1_attn_in['wo'], 'L1_attn_bo': _L1_attn_in['bo'], 'L1_ffn_w1_w': _L1_ffn_in['w1_w'], 'L1_ffn_w1_s': _L1_ffn_in['w1_s'], 'L1_ffn_w2_w': _L1_ffn_in['w2_w'], 'L1_ffn_w2_s': _L1_ffn_in['w2_s'], 'L1_ffn_h1_w': _L1_ffn_in['h1_w'], 'L1_ffn_h1_s': _L1_ffn_in['h1_s'], 'L1_ffn_h2_w': _L1_ffn_in['h2_w'], 'L1_ffn_h2_s': _L1_ffn_in['h2_s'], 'L1_ffn_w3_w': _L1_ffn_in['w3_w'], 'L1_ffn_w3_s': _L1_ffn_in['w3_s'], 'L2_attn_gamma': _L2_attn_in['gamma'], 'L2_attn_beta': _L2_attn_in['beta'], 'L2_attn_W_qkv': _L2_attn_in['W_qkv'], 'L2_attn_W_out': _L2_attn_in['W_out'], 'L2_ffn_w_gate': _L2_ffn_in['w_gate'], 'L2_ffn_w_up': _L2_ffn_in['w_up'], 'L2_ffn_w_down': _L2_ffn_in['w_down'], 'L3_attn_Wq': _L3_attn_in['Wq'], 'L3_attn_Wk': _L3_attn_in['Wk'], 'L3_attn_Wv': _L3_attn_in['Wv'], 'L3_attn_Wo': _L3_attn_in['Wo'], 'L3_attn_Wb': _L3_attn_in['Wb'], 'L3_attn_Wfd': _L3_attn_in['Wfd'], 'L3_attn_bfd': _L3_attn_in['bfd'], 'L3_attn_Wsd': _L3_attn_in['Wsd'], 'L3_attn_bsd': _L3_attn_in['bsd'], 'L3_attn_Wg': _L3_attn_in['Wg'], 'L3_ffn_w1_w': _L3_ffn_in['w1_w'], 'L3_ffn_w1_s': _L3_ffn_in['w1_s'], 'L3_ffn_w2_w': _L3_ffn_in['w2_w'], 'L3_ffn_w2_s': _L3_ffn_in['w2_s'], 'L3_ffn_h1_w': _L3_ffn_in['h1_w'], 'L3_ffn_h1_s': _L3_ffn_in['h1_s'], 'L3_ffn_h2_w': _L3_ffn_in['h2_w'], 'L3_ffn_h2_s': _L3_ffn_in['h2_s'], 'L3_ffn_w3_w': _L3_ffn_in['w3_w'], 'L3_ffn_w3_s': _L3_ffn_in['w3_s']}
    _x0 = _d['L0_attn_x']
    _d['L0_attn_x'] = jax.random.normal(jax.random.fold_in(jax.random.key(seed), 1), (2, 1024, 128), dtype=_x0.dtype)
    del _x0
    return _d

def reference(L0_attn_x, L0_attn_norm_w, L0_attn_Wq, L0_attn_Wk, L0_attn_Wv, L0_attn_Wbeta, L0_attn_bbeta, L0_attn_Wig, L0_attn_big, L0_attn_Wog, L0_attn_bog, L0_attn_Wout, L0_attn_bout, L0_ffn_wqkv, L0_ffn_q_scale, L0_ffn_k_scale, L0_ffn_wo, L0_ffn_ln_g, L0_ffn_ln_b, L0_ffn_w1, L0_ffn_b1, L0_ffn_w2, L0_ffn_b2, L1_attn_wq, L1_attn_bq, L1_attn_wk, L1_attn_bk, L1_attn_wv, L1_attn_bv, L1_attn_wo, L1_attn_bo, L1_ffn_w1_w, L1_ffn_w1_s, L1_ffn_w2_w, L1_ffn_w2_s, L1_ffn_h1_w, L1_ffn_h1_s, L1_ffn_h2_w, L1_ffn_h2_s, L1_ffn_w3_w, L1_ffn_w3_s, L2_attn_gamma, L2_attn_beta, L2_attn_W_qkv, L2_attn_W_out, L2_ffn_w_gate, L2_ffn_w_up, L2_ffn_w_down, L3_attn_Wq, L3_attn_Wk, L3_attn_Wv, L3_attn_Wo, L3_attn_Wb, L3_attn_Wfd, L3_attn_bfd, L3_attn_Wsd, L3_attn_bsd, L3_attn_Wg, L3_ffn_w1_w, L3_ffn_w1_s, L3_ffn_w2_w, L3_ffn_w2_s, L3_ffn_h1_w, L3_ffn_h1_s, L3_ffn_h2_w, L3_ffn_h2_s, L3_ffn_w3_w, L3_ffn_w3_s):

    def _L0_attn_ref(x, norm_w, Wq, Wk, Wv, Wbeta, bbeta, Wig, big, Wog, bog, Wout, bout):
        import jax, jax.numpy as jnp
        import numpy as np
        import math
        B, L, HID, NH = (4, 512, 128, 8)
        DH = HID // NH
        THETA = 10000.0

        def _rope_tables(seq_len, dh):
            half = dh // 2
            inv_freq = 1.0 / THETA ** (jnp.arange(half, dtype=jnp.float32) / half)
            freqs = jnp.arange(seq_len, dtype=jnp.float32)[:, None] * inv_freq[None, :]
            return (jnp.cos(freqs), jnp.sin(freqs))

        def _apply_rope(x, cos, sin):
            half = x.shape[-1] // 2
            x1, x2 = (x[..., :half], x[..., half:2 * half])
            c = cos[None, None]
            s = sin[None, None]
            return jnp.concatenate([x1 * c - x2 * s, x1 * s + x2 * c], axis=-1)
        Bq, Lq, _ = x.shape
        h = x * jax.lax.rsqrt(jnp.mean(x * x, axis=-1, keepdims=True) + 1e-06) * norm_w

        def heads(W):
            return jnp.einsum('bld,ed->ble', h, W).reshape(Bq, Lq, NH, DH).transpose(0, 2, 1, 3)
        q, k, v = (heads(Wq), heads(Wk), heads(Wv))
        cos, sin = _rope_tables(Lq, DH)
        q = _apply_rope(q, cos, sin)
        k = _apply_rope(k, cos, sin)

        def gate(W, b):
            return jax.nn.sigmoid(jnp.einsum('bld,hd->blh', h, W) + b).transpose(0, 2, 1)
        beta, ig, og = (gate(Wbeta, bbeta), gate(Wig, big), gate(Wog, bog))
        scale = 1.0 / math.sqrt(DH)
        qT = q.transpose(2, 0, 1, 3)
        kT = k.transpose(2, 0, 1, 3)
        vT = v.transpose(2, 0, 1, 3)
        fT = beta.transpose(2, 0, 1)
        gT = ig.transpose(2, 0, 1)
        oT = og.transpose(2, 0, 1)
        M0 = jnp.zeros((Bq, NH, DH, DH), x.dtype)

        def step(M, inp):
            q_t, k_t, v_t, f_t, g_t, o_t = inp
            M = M * f_t[..., None, None] + g_t[..., None, None] * scale * (k_t[..., :, None] * v_t[..., None, :])
            y_t = jnp.einsum('bhd,bhde->bhe', q_t, M) * o_t[..., None]
            return (M, y_t)
        _, yT = jax.lax.scan(step, M0, (qT, kT, vT, fT, gT, oT))
        y = yT.transpose(1, 0, 2, 3).reshape(Bq, Lq, HID)
        return jnp.einsum('bld,ed->ble', y, Wout) + bout

    def _L0_ffn_ref(x, wqkv, q_scale, k_scale, wo, ln_g, ln_b, w1, b1, w2, b2):
        import jax, jax.numpy as jnp
        import numpy as np
        DIM = 128
        DEPTH = 2
        HEADS = 8
        DIM_HEAD = 64
        WINDOW = 64
        INNER = HEADS * DIM_HEAD
        HID = int(DIM * 4 * 2 / 3)
        B, N = (2, 1024)
        QK_SCALE = 8.0

        def shift_token(t):
            t1, t2 = jnp.split(t, 2, axis=-1)
            t2 = jnp.pad(t2, ((0, 0), (1, 0), (0, 0)))[:, :-1]
            return jnp.concatenate([t1, t2], axis=-1)

        def l2norm(t):
            return t / jnp.clip(jnp.linalg.norm(t, axis=-1, keepdims=True), 1e-12)

        def rotate_half(x):
            x1, x2 = jnp.split(x, 2, axis=-1)
            return jnp.concatenate([-x2, x1], axis=-1)

        def rotary_xpos(q, k):
            n = q.shape[-2]
            half_idx = jnp.arange(0, DIM_HEAD, 2, dtype=jnp.float32)
            inv_freq = 1.0 / 10000.0 ** (half_idx / DIM_HEAD)
            t = jnp.arange(n, dtype=jnp.float32)
            freqs = t[:, None] * inv_freq[None, :]
            freqs = jnp.concatenate([freqs, freqs], axis=-1)
            base = (half_idx + 0.4 * DIM_HEAD) / (1.4 * DIM_HEAD)
            power = (t - n // 2) / float(WINDOW // 2)
            scale = base[None, :] ** power[:, None]
            scale = jnp.concatenate([scale, scale], axis=-1)
            cos, sin = (jnp.cos(freqs), jnp.sin(freqs))
            q = q * cos * scale + rotate_half(q) * sin * scale
            k = k * cos / scale + rotate_half(k) * sin / scale
            return (q, k)

        def local_attention(q, k, v):
            b, h, n, d = q.shape
            w = n // WINDOW
            bq = q.reshape(b, h, w, WINDOW, d) * QK_SCALE
            bk = k.reshape(b, h, w, WINDOW, d)
            bv = v.reshape(b, h, w, WINDOW, d)

            def look_around(t):
                p = jnp.pad(t, ((0, 0), (0, 0), (1, 0), (0, 0), (0, 0)))
                return jnp.concatenate([p[:, :, :w], p[:, :, 1:]], axis=3)
            bk, bv = (look_around(bk), look_around(bv))
            bt = jnp.arange(n).reshape(w, WINDOW)
            btp = jnp.pad(bt, ((1, 0), (0, 0)), constant_values=-1)
            btk = jnp.concatenate([btp[:w], btp[1:]], axis=1)
            sim = jnp.einsum('bhwid,bhwjd->bhwij', bq, bk)
            i = bt[:, :, None]
            j = btk[:, None, :]
            mask = (i < j) | (i > j + WINDOW) | (j == -1)
            sim = jnp.where(mask, -jnp.finfo(sim.dtype).max, sim)
            attn = jax.nn.softmax(sim, axis=-1)
            out = jnp.einsum('bhwij,bhwjd->bhwid', attn, bv)
            return out.reshape(b, h, n, d)

        def _layer(x, wqkv, qs, ksc, wo, lg, lb, w1, b1, w2, b2):
            b, n, _ = x.shape
            h = shift_token(x)
            qkv = h @ wqkv
            q, k, v = jnp.split(qkv, 3, axis=-1)
            to_heads = lambda t: t.reshape(b, n, HEADS, DIM_HEAD).transpose(0, 2, 1, 3)
            q, k, v = (to_heads(q), to_heads(k), to_heads(v))
            q = l2norm(q) * qs
            k = l2norm(k) * ksc
            q, k = rotary_xpos(q, k)
            o = local_attention(q, k, v)
            o = o.transpose(0, 2, 1, 3).reshape(b, n, INNER)
            x = x + o @ wo
            h = shift_token(x)
            mu = h.mean(-1, keepdims=True)
            var = h.var(-1, keepdims=True)
            h = (h - mu) / jnp.sqrt(var + 1e-05) * lg + lb
            h = h @ w1 + b1
            a, g = jnp.split(h, 2, axis=-1)
            h = a * jax.nn.gelu(g, approximate=False)
            x = x + h @ w2 + b2
            return x
        for l in range(DEPTH):
            x = _layer(x, wqkv[l], q_scale[l], k_scale[l], wo[l], ln_g[l], ln_b[l], w1[l], b1[l], w2[l], b2[l])
        return x

    def _L1_attn_ref(x, wq, bq, wk, bk, wv, bv, wo, bo):
        import jax, jax.numpy as jnp
        import numpy as np
        H = 16
        ROPE_BASE = 10000.0

        def _rotate_half(x):
            d = x.shape[-1]
            return jnp.concatenate((-x[..., d // 2:], x[..., :d // 2]), axis=-1)
        B, S, E = x.shape
        D = E // H

        def proj(w, b):
            return (x @ w.T + b).reshape(B, S, H, D).transpose(0, 2, 1, 3)
        q = proj(wq, bq)
        k = proj(wk, bk)
        v = proj(wv, bv)
        inv_freq = 1.0 / ROPE_BASE ** (jnp.arange(0, D, 2, dtype=jnp.float32) / D)
        freqs = jnp.arange(S, dtype=jnp.float32)[:, None] * inv_freq[None, :]
        cos = jnp.repeat(jnp.cos(freqs), 2, axis=-1)[None, None]
        sin = jnp.repeat(jnp.sin(freqs), 2, axis=-1)[None, None]
        q = q * cos + _rotate_half(q) * sin
        k = k * cos + _rotate_half(k) * sin
        scale = D ** (-0.5)
        scores = jnp.einsum('bhqd,bhkd->bhqk', q, k) * scale
        attn = jax.nn.softmax(scores, axis=-1)
        out = jnp.einsum('bhqk,bhkd->bhqd', attn, v)
        out = out.transpose(0, 2, 1, 3).reshape(B, S, E)
        return out @ wo.T + bo

    def _L1_ffn_ref(x, w1_w, w1_s, w2_w, w2_s, h1_w, h1_s, h2_w, h2_s, w3_w, w3_s):
        import jax, jax.numpy as jnp
        import numpy as np
        D_IN, D_HID = (128, 512)

        def _ternary(key, shape):
            return jax.random.randint(key, shape, -1, 2).astype(jnp.float32)

        def _tlin(x, w, s):
            return jnp.einsum('bsi,oi->bso', x, w) * s
        h = jax.nn.silu(_tlin(x, w1_w, w1_s)) * _tlin(x, w2_w, w2_s)
        h = jax.nn.gelu(_tlin(h, h1_w, h1_s), approximate=False)
        h = jax.nn.gelu(_tlin(h, h2_w, h2_s), approximate=False)
        return _tlin(h, w3_w, w3_s)

    def _L2_attn_ref(x, gamma, beta, W_qkv, W_out):
        import jax, jax.numpy as jnp
        import numpy as np
        EPS = 1e-05
        WINDOW = 32
        N_HEADS = 16
        B, S, D = x.shape
        H = N_HEADS
        hd = D // H
        scale = 1.0 / np.sqrt(hd)
        residual = x
        mu = jnp.mean(x, axis=-1, keepdims=True)
        var = jnp.var(x, axis=-1, keepdims=True)
        xn = (x - mu) * jax.lax.rsqrt(var + EPS) * gamma + beta
        qkv = jnp.einsum('bsd,ed->bse', xn, W_qkv)
        qkv = qkv.reshape(B, S, 3, H, hd)
        q, k, v = (qkv[:, :, 0], qkv[:, :, 1], qkv[:, :, 2])
        scores = jnp.einsum('bqhd,bkhd->bhqk', q, k) * scale
        row = jnp.arange(S)[:, None]
        col = jnp.arange(S)[None, :]
        mask = (col <= row) & (col >= row - WINDOW)
        scores = jnp.where(mask[None, None], scores, -jnp.inf)
        attn = jax.nn.softmax(scores, axis=-1)
        out = jnp.einsum('bhqk,bkhd->bqhd', attn, v).reshape(B, S, D)
        out = jnp.einsum('bsd,ed->bse', out, W_out)
        return out + residual

    def _L2_ffn_ref(x, w_gate, w_up, w_down):
        import jax, jax.numpy as jnp
        import numpy as np
        BLOCK = 16
        _GRID = jnp.array([0.0, 0.5, 1.0, 1.5, 2.0, 3.0, 4.0, 6.0], dtype=jnp.float32)
        _MID = jnp.array([0.25, 0.75, 1.25, 1.75, 2.5, 3.5, 5.0], dtype=jnp.float32)

        def fp4_quant_dequant(x):
            shape = x.shape
            xb = x.reshape(shape[:-1] + (shape[-1] // BLOCK, BLOCK))
            scale = jnp.max(jnp.abs(xb), axis=-1, keepdims=True) / 6.0
            scale = jnp.maximum(scale, jnp.float32(1e-12))
            xn = xb / scale
            idx = jnp.searchsorted(_MID, jnp.abs(xn))
            q = _GRID[idx] * jnp.sign(xn) * scale
            return q.reshape(shape)

        def fp4_linear(x, w):
            xq = fp4_quant_dequant(x)
            wq = fp4_quant_dequant(w)
            return jnp.einsum('bsk,nk->bsn', xq, wq)
        gate = fp4_linear(x, w_gate)
        y = fp4_linear(x, w_up)
        h = jax.nn.silu(gate) * y
        return fp4_linear(h, w_down)

    def _L3_attn_ref(x, Wq, Wk, Wv, Wo, Wb, Wfd, bfd, Wsd, bsd, Wg):
        import jax, jax.numpy as jnp
        import numpy as np
        B, T, D, H = (4, 256, 128, 16)
        HD = D // H
        MIX = 0.05

        def _deltanet_forward(x, Wq, Wk, Wv, Wo, Wb, Wfd, bfd, Wsd, bsd, Wg):
            b, t, dm = x.shape

            def heads(W):
                return (x @ W.T).reshape(b, t, H, HD).transpose(0, 2, 1, 3)
            q = jax.nn.silu(heads(Wq))
            k = jax.nn.silu(heads(Wk))
            v = jax.nn.silu(heads(Wv))
            beta = jax.nn.sigmoid(x @ Wb.T).transpose(0, 2, 1)
            fd = jax.nn.sigmoid(x @ Wfd.T + bfd).transpose(0, 2, 1)
            sd = jax.nn.sigmoid(x @ Wsd.T + bsd).transpose(0, 2, 1)
            qT = jnp.moveaxis(q, 2, 0)
            kT = jnp.moveaxis(k, 2, 0)
            vT = jnp.moveaxis(v, 2, 0)
            bT = jnp.moveaxis(beta, 2, 0)
            fT = jnp.moveaxis(fd, 2, 0)
            sT = jnp.moveaxis(sd, 2, 0)

            def step(carry, inp):
                Sf, Ss = carry
                qt, kt, vt, bt, ft, st = inp
                Sf = Sf * ft[..., None]
                Ss = Ss * st[..., None]
                o = 0.5 * qt * (Sf + Ss)
                upd = bt[..., None] * kt * vt
                Sf = Sf + upd
                Ss = Ss + upd
                Sf_new = Sf + MIX * Ss
                Ss = Ss + MIX * Sf
                return ((Sf_new, Ss), o)
            S0 = jnp.zeros((b, H, HD), x.dtype)
            _, oT = jax.lax.scan(step, (S0, S0), (qT, kT, vT, bT, fT, sT))
            o = jnp.moveaxis(oT, 0, 2)
            o = o.transpose(0, 2, 1, 3).reshape(b, t, dm)
            g = jax.nn.sigmoid(x @ Wg.T)
            return o * g @ Wo.T
        return _deltanet_forward(x, Wq, Wk, Wv, Wo, Wb, Wfd, bfd, Wsd, bsd, Wg)

    def _L3_ffn_ref(x, w1_w, w1_s, w2_w, w2_s, h1_w, h1_s, h2_w, h2_s, w3_w, w3_s):
        import jax, jax.numpy as jnp
        import numpy as np
        D_IN, D_HID = (128, 512)

        def _ternary(key, shape):
            return jax.random.randint(key, shape, -1, 2).astype(jnp.float32)

        def _tlin(x, w, s):
            return jnp.einsum('bsi,oi->bso', x, w) * s
        h = jax.nn.silu(_tlin(x, w1_w, w1_s)) * _tlin(x, w2_w, w2_s)
        h = jax.nn.gelu(_tlin(h, h1_w, h1_s), approximate=False)
        h = jax.nn.gelu(_tlin(h, h2_w, h2_s), approximate=False)
        return _tlin(h, w3_w, w3_s)
    x = L0_attn_x
    x = x + 0.5 * _L0_ffn_ref(_layernorm(x, axis=-1), L0_ffn_wqkv, L0_ffn_q_scale, L0_ffn_k_scale, L0_ffn_wo, L0_ffn_ln_g, L0_ffn_ln_b, L0_ffn_w1, L0_ffn_b1, L0_ffn_w2, L0_ffn_b2)
    x = x + _L0_attn_ref(_layernorm(x, axis=-1), L0_attn_norm_w, L0_attn_Wq, L0_attn_Wk, L0_attn_Wv, L0_attn_Wbeta, L0_attn_bbeta, L0_attn_Wig, L0_attn_big, L0_attn_Wog, L0_attn_bog, L0_attn_Wout, L0_attn_bout)
    x = x + 0.5 * _L0_ffn_ref(_layernorm(x, axis=-1), L0_ffn_wqkv, L0_ffn_q_scale, L0_ffn_k_scale, L0_ffn_wo, L0_ffn_ln_g, L0_ffn_ln_b, L0_ffn_w1, L0_ffn_b1, L0_ffn_w2, L0_ffn_b2)
    x = x + 0.5 * _L1_ffn_ref(_layernorm(x, axis=-1), L1_ffn_w1_w, L1_ffn_w1_s, L1_ffn_w2_w, L1_ffn_w2_s, L1_ffn_h1_w, L1_ffn_h1_s, L1_ffn_h2_w, L1_ffn_h2_s, L1_ffn_w3_w, L1_ffn_w3_s)
    x = x + _L1_attn_ref(_layernorm(x, axis=-1), L1_attn_wq, L1_attn_bq, L1_attn_wk, L1_attn_bk, L1_attn_wv, L1_attn_bv, L1_attn_wo, L1_attn_bo)
    x = x + 0.5 * _L1_ffn_ref(_layernorm(x, axis=-1), L1_ffn_w1_w, L1_ffn_w1_s, L1_ffn_w2_w, L1_ffn_w2_s, L1_ffn_h1_w, L1_ffn_h1_s, L1_ffn_h2_w, L1_ffn_h2_s, L1_ffn_w3_w, L1_ffn_w3_s)
    x = x + 0.5 * _L2_ffn_ref(_layernorm(x, axis=-1), L2_ffn_w_gate, L2_ffn_w_up, L2_ffn_w_down)
    x = x + _L2_attn_ref(_layernorm(x, axis=-1), L2_attn_gamma, L2_attn_beta, L2_attn_W_qkv, L2_attn_W_out)
    x = x + 0.5 * _L2_ffn_ref(_layernorm(x, axis=-1), L2_ffn_w_gate, L2_ffn_w_up, L2_ffn_w_down)
    x = x + 0.5 * _L3_ffn_ref(_layernorm(x, axis=-1), L3_ffn_w1_w, L3_ffn_w1_s, L3_ffn_w2_w, L3_ffn_w2_s, L3_ffn_h1_w, L3_ffn_h1_s, L3_ffn_h2_w, L3_ffn_h2_s, L3_ffn_w3_w, L3_ffn_w3_s)
    x = x + _L3_attn_ref(_layernorm(x, axis=-1), L3_attn_Wq, L3_attn_Wk, L3_attn_Wv, L3_attn_Wo, L3_attn_Wb, L3_attn_Wfd, L3_attn_bfd, L3_attn_Wsd, L3_attn_bsd, L3_attn_Wg)
    x = x + 0.5 * _L3_ffn_ref(_layernorm(x, axis=-1), L3_ffn_w1_w, L3_ffn_w1_s, L3_ffn_w2_w, L3_ffn_w2_s, L3_ffn_h1_w, L3_ffn_h1_s, L3_ffn_h2_w, L3_ffn_h2_s, L3_ffn_w3_w, L3_ffn_w3_s)
    return x

_drawn_inputs = setup_inputs


def setup_inputs(seed=0):
    import zlib

    import numpy as np

    out = dict(_drawn_inputs(seed))
    spreads = {'L0_attn_norm_w': (1.0, 0.2),
     'L0_attn_bbeta': (2.0, 0.2),
     'L0_attn_big': (0.0, 0.1),
     'L0_attn_bog': (0.0, 0.1),
     'L0_attn_bout': (0.0, 0.1),
     'L0_ffn_q_scale': (1.0, 0.2),
     'L0_ffn_k_scale': (1.0, 0.2),
     'L0_ffn_ln_g': (1.0, 0.2),
     'L0_ffn_ln_b': (0.0, 0.1),
     'L0_ffn_b1': (0.0, 0.1),
     'L0_ffn_b2': (0.0, 0.1),
     'L2_attn_gamma': (1.0, 0.2),
     'L2_attn_beta': (0.0, 0.1),
     'L3_attn_bfd': (0.0, 0.1),
     'L3_attn_bsd': (0.0, 0.1)}
    factors = {}
    for name, (base, spread) in spreads.items():
        noise = np.random.default_rng([zlib.crc32(name.encode()), seed]).standard_normal(out[name].shape)
        drawn = base * np.exp(spread * noise) if base else spread * noise
        out[name] = jnp.asarray(drawn.astype(out[name].dtype))
    for name, factor in factors.items():
        out[name] = (out[name] * factor).astype(out[name].dtype)
    return out
```

```python
from contextlib import ExitStack

import concourse.bass as bass
from concourse import mybir

ALU = mybir.AluOpType
ACT = mybir.ActivationFunctionType
AX = mybir.AxisListType
F32 = mybir.dt.float32
BF16 = mybir.dt.bfloat16

P = 128
BATCH, SEQ = 2, 1024
TOKENS = BATCH * SEQ
TILES = TOKENS // P
SEQ_TILES = SEQ // P
CHUNK = 512
CHUNKS = TOKENS // CHUNK
PER_CHUNK = CHUNK // P
BANK = 512

LA_HEADS, LA_DIM, LA_WIN = 8, 64, 64
LA_INNER = LA_HEADS * LA_DIM
GLU_HID = 341
GLU_PARTS = [(m * P, min(P, GLU_HID - m * P)) for m in range(-(-GLU_HID // P))]
TF_HID = 512
TF_PARTS = TF_HID // P
GA_HEADS, GA_DIM = 8, 16
FA_HEADS, FA_DIM = 16, 8
WA_WIN = 32
BAND = P + WA_WIN
Q4_HID, Q4_BLOCK = 352, 16
Q4_PARTS = [(m * P, min(P, Q4_HID - m * P)) for m in range(-(-Q4_HID // P))]
RA_HEADS, RA_DIM, RA_MIX = 16, 8, 0.05
RA_STEP = 32
RA_SEG = TOKENS // RA_STEP

L0_FFN = []
for _l in range(2):
    L0_FFN += [(f"wqkv{_l}", 3 * LA_INNER), (f"wo{_l}", LA_INNER), (f"w1{_l}", 2 * GLU_HID),
               (f"w2{_l}", len(GLU_PARTS) * P), (f"qs{_l}", LA_DIM), (f"ks{_l}", LA_DIM),
               (f"lg{_l}", 1), (f"lb{_l}", 1), (f"b1a{_l}", len(GLU_PARTS)), (f"b1g{_l}", len(GLU_PARTS)),
               (f"b2{_l}", P)]
L0_FFN += [("cq", SEQ_TILES * LA_DIM), ("ck", SEQ_TILES * LA_DIM),
           ("sq", SEQ_TILES * LA_DIM), ("sk", SEQ_TILES * LA_DIM)]
L0_ATTN = [("wq", 256), ("wqs", 256), ("wk", 256), ("wks", 256), ("wvg", P + 3 * GA_HEADS),
           ("wout", P), ("bg", 3 * GA_HEADS), ("bout", P), ("nw", 1), ("cos", SEQ), ("sin", SEQ), ("upper", P),
           ("diag", 2 * 64)]
TERNARY = [("w1", TF_HID), ("w2", TF_HID), ("h1", TF_PARTS * TF_HID), ("h2", TF_PARTS * TF_HID),
           ("w3", TF_PARTS * P), ("s1", TF_PARTS), ("s2", TF_PARTS), ("t1", TF_PARTS), ("t2", TF_PARTS), ("s3", P)]
L1_ATTN = [("wq", P), ("wqs", P), ("wk", P), ("wks", P), ("wv", P), ("wo", P), ("bq", 1), ("bqs", 1),
           ("bk", 1), ("bks", 1), ("bv", P), ("bo", P), ("cos", SEQ), ("sin", SEQ)]
L2_FFN = [("wg", 3 * P), ("wu", 3 * P), ("wd", Q4_HID)]
L2_ATTN = [("wq", P), ("wk", P), ("wv", P), ("wout", P), ("gamma", 1), ("beta", 1)]
L3_ATTN = [("wq", P), ("wk", P), ("wv", P), ("wg", P), ("wb", P), ("wfd", P), ("wsd", P), ("wo", P),
           ("bfd", 1), ("bsd", 1)]
CONSTANTS = [("ident", P)]
MASKS = [("ident", P), ("local", TILES * P), ("causal", P), ("band_q", SEQ_TILES * BAND), ("band_k", BAND)]
L2_FFN_HELD = sum(n for _, n in L2_FFN) + 2 * Q4_HID + len(Q4_PARTS) * P
AREA_A = sum(n for _, n in L0_FFN)
AREA_B = sum(n for _, n in TERNARY)
LAYOUTS = {"L0_ffn": L0_FFN, "L0_attn": L0_ATTN, "L1_ffn": TERNARY, "L1_attn": L1_ATTN, "L2_ffn": L2_FFN,
           "L2_attn": L2_ATTN, "L3_ffn": TERNARY, "L3_attn": L3_ATTN}


def columns(layout):
    at, out = 0, {}
    for name, n in layout:
        out[name] = (at, n)
        at += n
    return out


class Tally:

    def __init__(self, handle):
        self.handle, self.done = handle, 0


class Steps:

    def __init__(self, engine, tally, per_turn=0, turn=None):
        self.engine, self.tally, self.per_turn, self.made = engine, tally, per_turn, 0
        self.start = tally.done if turn is None else tally.done + turn * per_turn

    def __call__(self, instruction):
        self.made += 1
        instruction.then_inc(self.tally.handle, 1)
        self.engine.wait_ge(self.tally.handle, self.start + self.made)

    def close(self, turns=1):
        assert not self.per_turn or self.made == self.per_turn, self.made
        self.tally.done += self.made * turns


class Core:

    def __init__(self, nc, ctx):
        self.nc, self.ctx, self.tallies, self.made = nc, ctx, {}, 0
        self.weights_quantised = False
        sb = lambda name, shape, dt=F32: ctx.enter_context(nc.sbuf_tensor(name, shape, dt))
        self.x = sb("x", [P, TILES, P])
        self.y = sb("y", [P, TILES, P])
        self.zt = sb("zt", [P, 64 + TOKENS + 64])
        self.ident = sb("ident", [P, P])
        self.masks = sb("masks", [P, sum(n for _, n in MASKS)], BF16)
        self.stats = sb("stats", [P, TILES, 6])
        self.moments = sb("moments", [P, TILES, 2])
        self.spread = sb("spread", [P, TILES])
        self.rstd = sb("rstd", [P, TILES])
        self.minus_half = sb("minus_half", [P, TILES])
        self.areas = [sb("area_a", [P, AREA_A]), sb("area_b", [P, AREA_B])]
        self.psum = ctx.enter_context(nc.psum_tensor("psum", [P, 8, BANK], F32))
        self.mask_at = columns(MASKS)

    def sem(self, name):
        if name not in self.tallies:
            self.tallies[name] = Tally(self.ctx.enter_context(self.nc.semaphore(name)))
        return self.tallies[name]

    def fresh(self, name):
        self.made += 1
        return f"{name}_{self.made}"

    def mask(self, name):
        at, n = self.mask_at[name]
        return self.masks[:, at:at + n]

    def weights(self, area, layout):
        where = columns(layout)
        return lambda name: self.areas[area][:, where[name][0]:where[name][0] + where[name][1]]


def need(engine, tally, n):
    engine.wait_ge(tally.handle, tally.done + n)



def normalise_block(core, source, out, eps, evacuate=None, rms=False, only_transpose=False):
    nc, psum = core.nc, core.psum
    chain, done_pow, normed, turned, taken = (core.sem(n) for n in (
        "vector_chain", "rstd_ready", "tile_normalised", "bank_transposed", "bank_evacuated"))
    scalar_chain = core.sem("scalar_chain")
    with nc.Block() as block:
        if not only_transpose:
            @block.vector
            def _(dve):
                with dve.Fori(0, TILES) as i:
                    nc.vector.bn_stats(core.stats[:, i, :], source[:, i, :]).then_inc(chain.handle, 1)
                dve.wait_ge(chain.handle, chain.done + TILES)
                for i in range(TILES):
                    nc.vector.bn_aggr(core.moments[:, i, :], core.stats[:, i, :]).then_inc(chain.handle, 1)
                dve.wait_ge(chain.handle, chain.done + 2 * TILES)
                chain.done += 2 * TILES
                link = Steps(dve, chain)
                if rms:
                    link(nc.vector.tensor_tensor(core.spread[:], core.moments[:, :, 0], core.moments[:, :, 0], ALU.mult))
                    link(nc.vector.tensor_tensor(core.spread[:], core.spread[:], core.moments[:, :, 1], ALU.add))
                    nc.vector.tensor_scalar(core.spread[:], core.spread[:], eps, None, ALU.add).then_inc(done_pow.handle, 1)
                else:
                    nc.vector.tensor_scalar(core.spread[:], core.moments[:, :, 1], eps, None, ALU.add).then_inc(done_pow.handle, 1)
                link.close()
                need(dve, done_pow, 2)
                with dve.Fori(0, TILES) as i:
                    if rms:
                        nc.vector.tensor_scalar(out[:, i, :], source[:, i, :], core.rstd[:, bass.ds(i, 1)], None,
                                                ALU.mult).then_inc(normed.handle, 1)
                    else:
                        nc.vector.tensor_scalar(out[:, i, :], source[:, i, :], core.moments[:, i, 0:1],
                                                core.rstd[:, bass.ds(i, 1)], ALU.subtract, ALU.mult).then_inc(normed.handle, 1)

            @block.gpsimd
            def _(pool):
                need(pool, done_pow, 1)
                nc.gpsimd.tensor_tensor(core.rstd[:], core.spread[:], core.minus_half[:], ALU.pow).then_inc(done_pow.handle, 1)

        if evacuate is None:
            @block.sync
            def _(sp):
                need(sp, normed, TILES)

        @block.tensor
        def _(pe):
            if evacuate is None:
                return
            for g in range(CHUNKS):
                if g >= 2:
                    need(pe, taken, g - 1)
                for j in range(PER_CHUNK):
                    if not only_transpose:
                        need(pe, normed, PER_CHUNK * g + j + 1)
                    last = nc.tensor.transpose(psum[:, g % 2, j * P:(j + 1) * P], out[:, PER_CHUNK * g + j, :], core.ident[:])
                last.then_inc(turned.handle, 1)

        @block.scalar
        def _(act):
            if evacuate is None:
                return
            for g in range(CHUNKS):
                need(act, turned, g + 1)
                for ins in evacuate(g, psum[:, g % 2, :]):
                    last = ins
                last.then_inc(taken.handle, 1)
    if not only_transpose:
        done_pow.done += 2
        normed.done += TILES
    if evacuate is not None:
        turned.done += CHUNKS
        taken.done += CHUNKS


def tokens_product(core, weights, take, offset=0):
    nc, psum, zt = core.nc, core.psum, core.zt
    made, taken, chain = core.sem("tokens_product"), core.sem("tokens_product_taken"), core.sem("vector_chain")
    width = weights.shape[1]
    per = BANK // width if BANK % width == 0 else 2
    banks = -(-PER_CHUNK // per)
    with nc.Block() as block:
        @block.tensor
        def _(pe):
            for g in range(CHUNKS):
                if g >= 2:
                    need(pe, taken, g - 1)
                for j in range(PER_CHUNK):
                    at = offset + (g * PER_CHUNK + j) * P
                    last = nc.tensor.matmul(psum[:, g % 2 * banks + j // per, j % per * width:(j % per + 1) * width],
                                            zt[:, at:at + P], weights, start=True, stop=True)
                last.then_inc(made.handle, 1)

        @block.vector
        def _(dve):
            link = Steps(dve, chain)
            for g in range(CHUNKS):
                need(dve, made, g + 1)
                got = psum[:, g % 2 * banks:(g % 2 + 1) * banks, 0:min(per, PER_CHUNK) * width].rearrange("p b (j n) -> p (b j) n", n=width) \
                    if per * width == BANK else psum[:, g % 2 * banks:(g % 2 + 1) * banks, 0:per * width].rearrange("p b (j n) -> p b j n", n=width)
                take(g, got, link).then_inc(taken.handle, 1)
            link.close()
    made.done += CHUNKS
    taken.done += CHUNKS


def add_to_x(core, bias=None, also=None):
    nc, x = core.nc, core.x

    def take(g, got, link):
        tiles = slice(g * PER_CHUNK, (g + 1) * PER_CHUNK)
        if bias is not None:
            link(nc.vector.tensor_tensor(x[:, tiles, :], x[:, tiles, :], bias.unsqueeze(1).to_broadcast([P, PER_CHUNK, P]), ALU.add))
        if also is not None:
            link(nc.vector.tensor_tensor(x[:, tiles, :], x[:, tiles, :], also[:, tiles, :], ALU.add))
        return nc.vector.tensor_tensor(x[:, tiles, :], got, x[:, tiles, :], ALU.add)
    return take


def rotated_product(core, pairs, cos, sin):
    nc, psum, zt = core.nc, core.psum, core.zt
    made, turned, chain = core.sem("rotary_product"), core.sem("rotary_taken"), core.sem("vector_chain")
    with ExitStack() as ctx:
        part_a = ctx.enter_context(nc.sbuf_tensor(core.fresh("rotary_a"), [P, 2, CHUNK], F32))
        part_b = ctx.enter_context(nc.sbuf_tensor(core.fresh("rotary_b"), [P, 2, CHUNK], F32))
        R = len(pairs)
        with nc.Block() as block:
            @block.tensor
            def _(pe):
                with pe.Fori(0, CHUNKS) as c:
                    for r, (_, wa, _, wb, _) in enumerate(pairs):
                        if r >= 2:
                            pe.wait_ge(turned.handle, turned.done + c * R + r - 1)
                        tokens = zt[:, bass.ds(c * CHUNK, CHUNK)]
                        nc.tensor.matmul(psum[:, 2 * (r % 2), :], wa, tokens, start=True, stop=True)
                        nc.tensor.matmul(psum[:, 2 * (r % 2) + 1, :], wb, tokens, start=True, stop=True).then_inc(made.handle, 1)
                    pe.wait_ge(turned.handle, turned.done + (c + 1) * R)

            @block.vector
            def _(dve):
                with dve.Fori(0, CHUNKS) as c:
                    link = Steps(dve, chain, R, c)
                    for r, (out, _, ba, _, bb) in enumerate(pairs):
                        dve.wait_ge(made.handle, made.done + c * R + r + 1)
                        for bank, part, bias, table in ((0, part_a, ba, cos), (1, part_b, bb, sin)):
                            at = table[:, bass.ds((c % (SEQ // CHUNK)) * CHUNK, CHUNK)]
                            got = psum[:, 2 * (r % 2) + bank, :]
                            if bias is None:
                                last = nc.vector.tensor_tensor(part[:, r % 2, :], got, at, ALU.mult)
                            else:
                                last = nc.vector.scalar_tensor_tensor(out=part[:, r % 2, :], in0=got, scalar=bias, in1=at,
                                                                      op0=ALU.add, op1=ALU.mult)
                        link(last)
                        nc.vector.tensor_tensor(out[:, bass.ds(c * CHUNK, CHUNK)], part_a[:, r % 2, :], part_b[:, r % 2, :],
                                                ALU.add).then_inc(turned.handle, 1)
                    dve.wait_ge(turned.handle, turned.done + (c + 1) * R)
                link.close(CHUNKS)
        made.done += R * CHUNKS
        turned.done += R * CHUNKS


def plain(core):
    def evacuate(g, bank):
        yield core.nc.scalar.copy(core.zt[:, g * CHUNK:(g + 1) * CHUNK], bank)
    return evacuate


def affine(core, scale, bias):
    def evacuate(g, bank):
        yield core.nc.scalar.activation(core.zt[:, g * CHUNK:(g + 1) * CHUNK], bank, ACT.Identity, bias=bias, scale=scale)
    return evacuate


def ternary_ffn(core, area):
    nc, psum, x, zt = core.nc, core.psum, core.x, core.zt
    w = core.weights(area, TERNARY)
    normalise_block(core, x, core.y, 1e-5, plain(core))
    up, silu, gated, hid, acted, low, added = (core.sem(n) for n in (
        "tf_up_product", "tf_silu", "tf_gated", "tf_hidden_product", "tf_gelu", "tf_out_product", "tf_added"))
    chain = core.sem("vector_chain")
    M = TF_PARTS
    with ExitStack() as ctx:
        sb = lambda name, shape: ctx.enter_context(nc.sbuf_tensor(core.fresh(name), shape, F32))
        ha, hb = sb("hidden_a", [P, 2, M, CHUNK]), sb("hidden_b", [P, 2, M, CHUNK])
        gate, scaled = sb("gate", [P, 2, CHUNK]), sb("scaled", [P, PER_CHUNK, P])
        with nc.Block() as block:
            @block.tensor
            def _(pe):
                with pe.Fori(0, CHUNKS // 2) as i:
                    for c in range(2):
                        for m in range(M):
                            n = c * M + m
                            if n >= 2:
                                pe.wait_ge(gated.handle, gated.done + i * 2 * M + n - 1)
                            tokens = zt[:, bass.ds(i * 2 * CHUNK + c * CHUNK, CHUNK)]
                            nc.tensor.matmul(psum[:, n % 2, :], w("w1")[:, m * P:(m + 1) * P], tokens, start=True, stop=True)
                            nc.tensor.matmul(psum[:, 2 + n % 2, :], w("w2")[:, m * P:(m + 1) * P], tokens,
                                             start=True, stop=True).then_inc(up.handle, 1)
                    for step, (name, src) in enumerate((("h1", ha), ("h2", hb))):
                        for c in range(2):
                            if step == 0:
                                pe.wait_ge(gated.handle, gated.done + i * 2 * M + (c + 1) * M)
                            else:
                                pe.wait_ge(acted.handle, acted.done + i * 4 * M + (c + 1) * M)
                            for m in range(M):
                                n = step * 2 * M + c * M + m
                                if n >= 2:
                                    pe.wait_ge(acted.handle, acted.done + i * 4 * M + n - 1)
                                for k in range(M):
                                    last = nc.tensor.matmul(psum[:, 4 + n % 2, :], w(name)[:, k * TF_HID + m * P:k * TF_HID + (m + 1) * P],
                                                            src[:, c, k, :], start=(k == 0), stop=(k == M - 1))
                                last.then_inc(hid.handle, 1)
                    for c in range(2):
                        pe.wait_ge(acted.handle, acted.done + i * 4 * M + (2 + c + 1) * M)
                        for j in range(PER_CHUNK):
                            for k in range(M):
                                last = nc.tensor.matmul(psum[:, 6 + c, j * P:(j + 1) * P], ha[:, c, k, j * P:(j + 1) * P],
                                                        w("w3")[:, k * P:(k + 1) * P], start=(k == 0), stop=(k == M - 1))
                        last.then_inc(low.handle, 1)
                    pe.wait_ge(added.handle, added.done + (i + 1) * 2)

            @block.scalar
            def _(act):
                with act.Fori(0, CHUNKS // 2) as i:
                    for n in range(2 * M):
                        act.wait_ge(up.handle, up.done + i * 2 * M + n + 1)
                        if n >= 2:
                            act.wait_ge(gated.handle, gated.done + i * 2 * M + n - 1)
                        nc.scalar.activation(gate[:, n % 2, :], psum[:, n % 2, :], ACT.Silu,
                                             scale=w("s1")[:, n % M:n % M + 1]).then_inc(silu.handle, 1)
                    for step, (dst, scale) in enumerate(((hb, "t1"), (ha, "t2"))):
                        for c in range(2):
                            for m in range(M):
                                n = step * 2 * M + c * M + m
                                act.wait_ge(hid.handle, hid.done + i * 4 * M + n + 1)
                                nc.scalar.activation(dst[:, c, m, :], psum[:, 4 + n % 2, :], ACT.Gelu,
                                                     scale=w(scale)[:, m:m + 1]).then_inc(acted.handle, 1)

            @block.vector
            def _(dve):
                with dve.Fori(0, CHUNKS // 2) as i:
                    link = Steps(dve, chain, 2, i)
                    for n in range(2 * M):
                        dve.wait_ge(silu.handle, silu.done + i * 2 * M + n + 1)
                        nc.vector.scalar_tensor_tensor(out=ha[:, n // M, n % M, :], in0=psum[:, 2 + n % 2, :],
                                                       scalar=w("s2")[:, n % M:n % M + 1], in1=gate[:, n % 2, :],
                                                       op0=ALU.mult, op1=ALU.mult).then_inc(gated.handle, 1)
                    for c in range(2):
                        dve.wait_ge(low.handle, low.done + i * 2 + c + 1)
                        link(nc.vector.tensor_tensor(scaled[:], psum[:, 6 + c, :].rearrange("p (j n) -> p j n", j=PER_CHUNK),
                                                     w("s3").unsqueeze(1).to_broadcast([P, PER_CHUNK, P]), ALU.mult))
                        tiles = x[:, bass.ds(i * 2 * PER_CHUNK + c * PER_CHUNK, PER_CHUNK), :]
                        nc.vector.scalar_tensor_tensor(out=tiles, in0=scaled[:], scalar=0.5, in1=tiles,
                                                       op0=ALU.mult, op1=ALU.add).then_inc(added.handle, 1)
                        dve.wait_ge(added.handle, added.done + i * 2 + c + 1)
                link.close(CHUNKS // 2)
        turns = CHUNKS // 2
        for tally, n in ((up, 2 * M), (silu, 2 * M), (gated, 2 * M), (hid, 4 * M), (acted, 4 * M), (low, 2), (added, 2)):
            tally.done += n * turns



def shifted(core):
    half, zt = P // 2, core.zt

    def evacuate(g, bank):
        at = 64 + g * CHUNK
        n = CHUNK - 1 if (g + 1) * CHUNK % SEQ == 0 else CHUNK
        yield core.nc.scalar.copy(zt[0:half, at:at + CHUNK], bank[0:half, :])
        yield core.nc.scalar.copy(zt[half:P, at + 1:at + 1 + n], bank[half:P, 0:n])
    return evacuate


def first_tokens(core):
    cleared = core.sem("first_token_cleared")
    with core.nc.Block() as block:
        @block.gpsimd
        def _(pool):
            for b in range(BATCH):
                core.nc.gpsimd.memset(core.zt[P // 2:P, 64 + b * SEQ:65 + b * SEQ], 0.0).then_inc(cleared.handle, 1)
    cleared.done += BATCH


def local_attention(core, w, layer):
    nc, psum, y, zt = core.nc, core.psum, core.y, core.zt
    H, D, W = LA_HEADS, LA_DIM, LA_WIN
    names = ("la_tokens_staged", "la_qk_product", "la_v_product", "la_squared", "la_square_sums", "la_norms", "la_rotated",
             "la_qk_turned", "la_q_evacuated", "la_scores", "la_shifted_scores", "la_probs", "la_probs_turned",
             "la_probs_evacuated", "la_v_evacuated", "la_values", "la_values_normed", "la_values_turned",
             "la_values_evacuated", "la_out_product", "la_added", "la_tables")
    (staged, qk_ready, v_ready, squared, sums, norms, rotated, qk_turned, q_taken, scores, shifted_s, probs, p_turned,
     p_taken, v_taken, values, o_normed, o_turned, o_taken, out_ready, added, tables) = (core.sem(n) for n in names)
    chain, chain_act = core.sem("vector_chain"), core.sem("scalar_chain")
    wq = w(f"wqkv{layer}")
    wo = w(f"wo{layer}").rearrange("p (k n) -> p k n", k=LA_INNER // P)
    with ExitStack() as ctx:
        sb = lambda name, shape, dt=F32: ctx.enter_context(nc.sbuf_tensor(core.fresh(name), shape, dt))
        direct = sb("direct", [P, 2, TILES, D])
        cross = sb("cross", [P, 2, TILES, D])
        window = sb("window", [P, W + P])
        squares = sb("squares", [P, 2 * H, D])
        square_sum = sb("square_sum", [P, 2 * H])
        norm = sb("norm", [P, 2 * H])
        turn_a, turn_b = sb("turn_a", [P, 2 * H, D]), sb("turn_b", [P, 2 * H, D])
        qk = sb("qk", [P, 2 * H, D])
        q_t = sb("q_t", [P, H // 2, P])
        k_t = sb("k_t", [P, H // 2, W + P])
        v = sb("v", [P, 2, H, D + 1])
        top = sb("top", [P, H])
        shifted_scores, prob = sb("shifted_scores", [P, H, P]), sb("prob", [P, H, P])
        prob_t = sb("prob_t", [P, H, P])
        rec = sb("rec", [P, H])
        o = sb("o", [P, H, D])
        o_t = sb("o_t", [P, LA_INNER // P, P])
        score_banks, qk_banks, v_banks, turn_banks = psum[:, 0:2, :], psum[:, 2:4, :], psum[:, 4:6, :], psum[:, 6:8, :]

        def heads_of(banks):
            return banks.rearrange("p b (h n) -> p (b h) n", h=H // 2)

        with nc.Block() as block:
            @block.vector
            def _(dve):
                for s, (name, scale) in enumerate((("q", f"qs{layer}"), ("k", f"ks{layer}"))):
                    learned = w(scale).rearrange("p (a d) -> p a d", a=2)
                    for b in range(BATCH):
                        tiles = slice(b * SEQ_TILES, (b + 1) * SEQ_TILES)
                        nc.vector.tensor_tensor(direct[:, s, tiles, :], w("c" + name).rearrange("p (t d) -> p t d", d=D),
                                                w(scale).unsqueeze(1).to_broadcast([P, SEQ_TILES, D]),
                                                ALU.mult).then_inc(tables.handle, 1)
                        for a in range(2):
                            half = slice(a * D // 2, (a + 1) * D // 2)
                            nc.vector.tensor_tensor(cross[:, s, tiles, half],
                                                    w("s" + name).rearrange("p (t d) -> p t d", d=D)[:, :, half],
                                                    learned[:, 1 - a, :].unsqueeze(1).to_broadcast([P, SEQ_TILES, D // 2]),
                                                    ALU.mult).then_inc(tables.handle, 1)

            @block.gpsimd
            def _(pool):
                nc.gpsimd.memset(v[:], 1.0).then_inc(tables.handle, 1)
                nc.gpsimd.memset(k_t[:], 0.0).then_inc(tables.handle, 1)
        tables.done += 14

        def pool_first(pool, n, opening):
            if not opening:
                pool.wait_ge(v_ready.handle, v_ready.done + n)
            nc.gpsimd.tensor_copy(window[:], zt[:, bass.ds(n * P, W + P)]).then_inc(staged.handle, 1)
            pool.wait_ge(sums.handle, sums.done + n + 1)
            nc.gpsimd.tensor_tensor(norm[:], square_sum[:], core.minus_half[:], ALU.pow).then_inc(norms.handle, 1)

        def pe_project(pe, n, opening, then_scores=False):
            pe.wait_ge(staged.handle, staged.done + n + 1)
            if not opening:
                pe.wait_ge(rotated.handle, rotated.done + n)
                pe.wait_ge(v_taken.handle, v_taken.done + n)
            nc.tensor.matmul(qk_banks[:, 0, :], window[:, W:W + P], wq[:, 0:LA_INNER], start=True, stop=True)
            nc.tensor.matmul(qk_banks[:, 1, :], window[:, W:W + P], wq[:, LA_INNER:2 * LA_INNER],
                             start=True, stop=True).then_inc(qk_ready.handle, 1)
            for a in range(2):
                if a and then_scores:
                    pe.wait_ge(q_taken.handle, q_taken.done + n)
                last = nc.tensor.matmul(v_banks[:, a, :], window[:, a * W:a * W + P], wq[:, 2 * LA_INNER:], start=True, stop=True)
            last.then_inc(v_ready.handle, 1)

        def pe_turn_qk(pe, n, opening):
            pe.wait_ge(rotated.handle, rotated.done + n + 1)
            if not opening:
                pe.wait_ge(added.handle, added.done + n)
            for s in range(2):
                for k in range(H // 2):
                    last = nc.tensor.transpose(turn_banks[:, s, k * P:(k + 1) * P],
                                               qk[:, s * H + 2 * k:s * H + 2 * k + 2, :], core.ident[:])
            last.then_inc(qk_turned.handle, 1)

        def pe_scores(pe, n):
            for s in range(2):
                rows = slice(D * s, D * s + D)
                for h in range(H // 2):
                    for a in range(2):
                        nc.tensor.matmul(score_banks[a * W:(a + 1) * W, s, h * P:(h + 1) * P],
                                         q_t[rows, h, a * W:(a + 1) * W], k_t[rows, h, a * W:a * W + P],
                                         start=(h == 0), stop=False, skip_group_check=True)
            for s in range(2):
                last = nc.tensor.matmul(score_banks[:, s, :], core.mask("ident"),
                                        core.mask("local").rearrange("p (t k) -> p t k", k=P)[:, bass.ds(n, 1), :].to_broadcast([P, H // 2, P]),
                                        start=False, stop=True, skip_group_check=True)
            last.then_inc(scores.handle, 1)

        def pe_values(pe, n):
            pe.wait_ge(probs.handle, probs.done + n + 1)
            for h in range(H):
                last = nc.tensor.transpose(heads_of(turn_banks)[:, h, :], prob[:, h, :], core.ident[:])
            last.then_inc(p_turned.handle, 1)
            pe.wait_ge(p_taken.handle, p_taken.done + n + 1)
            for h in range(H):
                for a in range(2):
                    last = nc.tensor.matmul(score_banks[a * W:(a + 1) * W, h // 4, (h % 4) * (D + 1):(h % 4 + 1) * (D + 1)],
                                            prob_t[:, h, a * W:(a + 1) * W], v[:, a, 2 * (h % 4) + h // 4, :], start=True, stop=True,
                                            skip_group_check=True)
            last.then_inc(values.handle, 1)
            pe.wait_ge(o_normed.handle, o_normed.done + n + 1)
            for k in range(LA_INNER // P):
                last = nc.tensor.transpose(turn_banks[:, 0, k * P:(k + 1) * P], o[:, 2 * k:2 * k + 2, :], core.ident[:])
            last.then_inc(o_turned.handle, 1)
            pe.wait_ge(o_taken.handle, o_taken.done + n + 1)
            for k in range(LA_INNER // P):
                last = nc.tensor.matmul(turn_banks[:, 1, 0:P], o_t[:, k, :], wo[:, k, :], start=(k == 0), stop=(k == LA_INNER // P - 1))
            last.then_inc(out_ready.handle, 1)

        def act_square(act, n):
            act.wait_ge(qk_ready.handle, qk_ready.done + n + 1)
            nc.scalar.activation(squares[:], heads8(qk_banks), ACT.Square).then_inc(squared.handle, 1)

        def heads8(banks):
            return banks.rearrange("p b (h d) -> p (b h) d", d=D)

        def act_take_v(act, n):
            act.wait_ge(v_ready.handle, v_ready.done + n + 1)
            nc.scalar.copy(v[:, :, :, 0:D], v_banks.rearrange("p a (h d) -> p a h d", d=D)).then_inc(v_taken.handle, 1)

        def act_take_qk(act, n, turn):
            act.wait_ge(qk_turned.handle, qk_turned.done + n + 1)
            link = Steps(act, chain_act, 1, turn)
            link(nc.scalar.copy(k_t[:, :, 0:W], k_t[:, :, P:P + W]))
            nc.scalar.copy(q_t[:], turn_banks[:, 0, :].rearrange("p (k n) -> p k n", k=H // 2))
            nc.scalar.copy(k_t[:, :, W:W + P], turn_banks[:, 1, :].rearrange("p (k n) -> p k n", k=H // 2)).then_inc(q_taken.handle, 1)
            return link

        def act_second(act, n, take_next_v):
            act.wait_ge(shifted_s.handle, shifted_s.done + n + 1)
            nc.scalar.activation(prob[:], shifted_scores[:], ACT.Exp, scale=8.0).then_inc(probs.handle, 1)
            act.wait_ge(p_turned.handle, p_turned.done + n + 1)
            nc.scalar.copy(prob_t[:], heads_of(turn_banks)).then_inc(p_taken.handle, 1)
            act.wait_ge(values.handle, values.done + n + 1)
            if take_next_v:
                act_take_v(act, n + 1)
            act.wait_ge(o_turned.handle, o_turned.done + n + 1)
            nc.scalar.copy(o_t[:], turn_banks[:, 0, :].rearrange("p (k n) -> p k n", k=LA_INNER // P)).then_inc(o_taken.handle, 1)

        FIRST, SECOND = 3, 2

        def dve_first(dve, n, link):
            dve.wait_ge(squared.handle, squared.done + n + 1)
            link(nc.vector.tensor_reduce(square_sum[:], squares[:], AX.X, ALU.add))
            nc.vector.tensor_scalar(square_sum[:], square_sum[:], 1e-24, None, ALU.max).then_inc(sums.handle, 1)
            nc.vector.tensor_tensor(turn_a[:].rearrange("p (s h) d -> p s h d", s=2), qk_banks.rearrange("p s (h d) -> p s h d", d=D),
                                    direct[:, :, bass.ds(n, 1), :].to_broadcast([P, 2, H, D]), ALU.mult)
            for s in range(2):
                partner = qk_banks[:, s, :].rearrange("p (h a d) -> p h a d", h=H, a=2)[:, :, ::-1, :]
                last = nc.vector.tensor_tensor(turn_b[:, s * H:(s + 1) * H, :].rearrange("p h (a d) -> p h a d", a=2), partner,
                                               cross[:, s, bass.ds(n, 1), :].to_broadcast([P, H, D]).rearrange("p h (a d) -> p h a d", a=2),
                                               ALU.mult)
            link(last)
            link(nc.vector.tensor_tensor(turn_a[:], turn_a[:], turn_b[:], ALU.add))

        def dve_norm_qk(dve, n):
            dve.wait_ge(norms.handle, norms.done + n + 1)
            nc.vector.tensor_tensor(qk[:], turn_a[:], norm[:].unsqueeze(2).to_broadcast([P, 2 * H, D]), ALU.mult).then_inc(rotated.handle, 1)

        def dve_softmax(dve, n, link):
            dve.wait_ge(scores.handle, scores.done + n + 1)
            link(nc.vector.tensor_reduce(top[:], heads_of(score_banks), AX.X, ALU.max))
            nc.vector.tensor_tensor(shifted_scores[:], heads_of(score_banks), top[:].unsqueeze(2).to_broadcast([P, H, P]),
                                    ALU.subtract).then_inc(shifted_s.handle, 1)

        def dve_values(dve, n, link):
            dve.wait_ge(values.handle, values.done + n + 1)
            got = score_banks[:, :, 0:4 * (D + 1)].rearrange("p b (h e) -> p b h e", e=D + 1)
            link(nc.vector.reciprocal(rec[:].rearrange("p (b h) -> p b h", b=2), got[:, :, :, D]))
            nc.vector.tensor_tensor(o[:].rearrange("p (h b) d -> p b h d", b=2), got[:, :, :, 0:D],
                                    rec[:].rearrange("p (b h) -> p b h", b=2).unsqueeze(3).to_broadcast([P, 2, 4, D]),
                                    ALU.mult).then_inc(o_normed.handle, 1)

        def dve_add(dve, n):
            dve.wait_ge(out_ready.handle, out_ready.done + n + 1)
            tile = y[:, bass.ds(n, 1), :]
            nc.vector.tensor_tensor(tile, turn_banks[:, 1, 0:P].unsqueeze(1), tile, ALU.add).then_inc(added.handle, 1)

        with nc.Block() as block:
            @block.gpsimd
            def _(pool):
                pool_first(pool, 0, True)
                with pool.Fori(1, TILES) as n:
                    pool_first(pool, n, False)

            @block.tensor
            def _(pe):
                pe_project(pe, 0, True)
                pe_turn_qk(pe, 0, True)
                with pe.Fori(0, TILES - 1) as n:
                    pe_project(pe, n + 1, False, then_scores=True)
                    pe_scores(pe, n)
                    pe_values(pe, n)
                    pe_turn_qk(pe, n + 1, False)
                need(pe, q_taken, TILES)
                pe_scores(pe, TILES - 1)
                pe_values(pe, TILES - 1)

            @block.scalar
            def _(act):
                act_square(act, 0)
                act_take_v(act, 0)
                act_take_qk(act, 0, 0)
                with act.Fori(0, TILES - 1) as n:
                    act_square(act, n + 1)
                    act_second(act, n, True)
                    link = act_take_qk(act, n + 1, n + 1)
                act_second(act, TILES - 1, False)
                link.close(TILES)

            @block.vector
            def _(dve):
                link = Steps(dve, chain)
                dve_first(dve, 0, link)
                dve_norm_qk(dve, 0)
                link.close()
                with dve.Fori(0, TILES - 1) as n:
                    link = Steps(dve, chain, FIRST + SECOND, n)
                    dve_softmax(dve, n, link)
                    dve_first(dve, n + 1, link)
                    dve_values(dve, n, link)
                    dve_norm_qk(dve, n + 1)
                    dve_add(dve, n)
                link.close(TILES - 1)
                link = Steps(dve, chain)
                dve_softmax(dve, TILES - 1, link)
                dve_values(dve, TILES - 1, link)
                dve_add(dve, TILES - 1)
                link.close()
        for tally in (staged, qk_ready, v_ready, squared, sums, norms, rotated, qk_turned, q_taken, scores, shifted_s, probs,
                      p_turned, p_taken, v_taken, values, o_normed, o_turned, o_taken, out_ready, added):
            tally.done += TILES


def glu(core, w, layer):
    nc, psum, y, zt = core.nc, core.psum, core.y, core.zt
    up, act_done, gated, low, added = (core.sem(n) for n in ("glu_up_product", "glu_gelu", "glu_gated", "glu_out_product", "glu_added"))
    chain = core.sem("vector_chain")
    M = len(GLU_PARTS)
    w1, w2 = w(f"w1{layer}"), w(f"w2{layer}")
    with ExitStack() as ctx:
        sb = lambda name, shape: ctx.enter_context(nc.sbuf_tensor(core.fresh(name), shape, F32))
        hidden, gate, summed = sb("hidden", [P, 2, M, CHUNK]), sb("glu_gate", [P, 2, CHUNK]), sb("summed", [P, PER_CHUNK, P])
        with nc.Block() as block:
            @block.tensor
            def _(pe):
                with pe.Fori(0, CHUNKS // 2) as i:
                    for c in range(2):
                        for m, (at, rows) in enumerate(GLU_PARTS):
                            n = c * M + m
                            if n >= 2:
                                pe.wait_ge(gated.handle, gated.done + i * 2 * M + n - 1)
                            tokens = zt[:, bass.ds(i * 2 * CHUNK + c * CHUNK, CHUNK)]
                            nc.tensor.matmul(psum[0:rows, n % 2, :], w1[:, at:at + rows], tokens, start=True, stop=True)
                            nc.tensor.matmul(psum[0:rows, 2 + n % 2, :], w1[:, GLU_HID + at:GLU_HID + at + rows], tokens,
                                             start=True, stop=True).then_inc(up.handle, 1)
                    for c in range(2):
                        pe.wait_ge(gated.handle, gated.done + i * 2 * M + (c + 1) * M)
                        for j in range(PER_CHUNK):
                            for m, (at, rows) in enumerate(GLU_PARTS):
                                last = nc.tensor.matmul(psum[:, 4 + c, j * P:(j + 1) * P], hidden[0:rows, c, m, j * P:(j + 1) * P],
                                                        w2[0:rows, m * P:(m + 1) * P], start=(m == 0), stop=(m == M - 1))
                        last.then_inc(low.handle, 1)
                    pe.wait_ge(added.handle, added.done + (i + 1) * 2)

            @block.scalar
            def _(act):
                with act.Fori(0, CHUNKS // 2) as i:
                    for n in range(2 * M):
                        rows = GLU_PARTS[n % M][1]
                        act.wait_ge(up.handle, up.done + i * 2 * M + n + 1)
                        if n >= 2:
                            act.wait_ge(gated.handle, gated.done + i * 2 * M + n - 1)
                        nc.scalar.activation(gate[0:rows, n % 2, :], psum[0:rows, 2 + n % 2, :], ACT.Gelu,
                                             bias=w(f"b1g{layer}")[0:rows, n % M:n % M + 1]).then_inc(act_done.handle, 1)

            @block.vector
            def _(dve):
                with dve.Fori(0, CHUNKS // 2) as i:
                    link = Steps(dve, chain, 2, i)
                    for n in range(2 * M):
                        rows = GLU_PARTS[n % M][1]
                        dve.wait_ge(act_done.handle, act_done.done + i * 2 * M + n + 1)
                        nc.vector.scalar_tensor_tensor(out=hidden[0:rows, n // M, n % M, :], in0=psum[0:rows, n % 2, :],
                                                       scalar=w(f"b1a{layer}")[0:rows, n % M:n % M + 1], in1=gate[0:rows, n % 2, :],
                                                       op0=ALU.add, op1=ALU.mult).then_inc(gated.handle, 1)
                    for c in range(2):
                        dve.wait_ge(low.handle, low.done + i * 2 + c + 1)
                        link(nc.vector.tensor_tensor(summed[:], psum[:, 4 + c, :].rearrange("p (j n) -> p j n", j=PER_CHUNK),
                                                     w(f"b2{layer}").unsqueeze(1).to_broadcast([P, PER_CHUNK, P]), ALU.add))
                        tiles = y[:, bass.ds(i * 2 * PER_CHUNK + c * PER_CHUNK, PER_CHUNK), :]
                        nc.vector.tensor_tensor(tiles, summed[:], tiles, ALU.add).then_inc(added.handle, 1)
                        dve.wait_ge(added.handle, added.done + i * 2 + c + 1)
                link.close(CHUNKS // 2)
        turns = CHUNKS // 2
        for tally, n in ((up, 2 * M), (act_done, 2 * M), (gated, 2 * M), (low, 2), (added, 2)):
            tally.done += n * turns


def unshift(core, out):
    nc, psum = core.nc, core.psum
    turned, taken = core.sem("bank_transposed"), core.sem("bank_evacuated")
    with nc.Block() as block:
        @block.tensor
        def _(pe):
            for g in range(CHUNKS):
                if g >= 2:
                    need(pe, taken, g - 1)
                for j in range(PER_CHUNK):
                    at = 64 + g * CHUNK + j * P
                    last = nc.tensor.transpose(psum[:, g % 2, j * P:(j + 1) * P], core.zt[:, at:at + P], core.ident[:])
                last.then_inc(turned.handle, 1)

        @block.scalar
        def _(act):
            for g in range(CHUNKS):
                need(act, turned, g + 1)
                nc.scalar.copy(out[:, g * PER_CHUNK:(g + 1) * PER_CHUNK, :],
                               psum[:, g % 2, :].rearrange("p (j n) -> p j n", j=PER_CHUNK)).then_inc(taken.handle, 1)
    turned.done += CHUNKS
    taken.done += CHUNKS


def l0_ffn(core, area):
    nc, x, y = core.nc, core.x, core.y
    w = core.weights(area, L0_FFN)
    summed = core.sem("residual_added")
    for layer in range(2):
        first_tokens(core)
        normalise_block(core, x, y, 1e-5, shifted(core), only_transpose=(layer == 1))
        local_attention(core, w, layer)
        first_tokens(core)
        normalise_block(core, x, y, 1e-5, shifted(core), only_transpose=True)
        with ExitStack() as ctx:
            tokens = ctx.enter_context(nc.sbuf_tensor(core.fresh("shifted_tokens"), [P, TILES, P], F32))
            normed = ctx.enter_context(nc.sbuf_tensor(core.fresh("normed_tokens"), [P, TILES, P], F32))
            unshift(core, tokens)
            normalise_block(core, tokens, normed, 1e-5, affine(core, w(f"lg{layer}"), w(f"lb{layer}")))
        glu(core, w, layer)
    with nc.Block() as block:
        @block.vector
        def _(dve):
            for g in range(CHUNKS):
                tiles = slice(g * PER_CHUNK, (g + 1) * PER_CHUNK)
                nc.vector.scalar_tensor_tensor(out=x[:, tiles, :], in0=y[:, tiles, :], scalar=0.5, in1=x[:, tiles, :],
                                               op0=ALU.mult, op1=ALU.add).then_inc(summed.handle, 1)
    summed.done += CHUNKS



def l0_attn(core, area):
    nc, psum, x, y, zt = core.nc, core.psum, core.x, core.y, core.zt
    H, D, G = GA_HEADS, GA_DIM, 2
    R = H // G
    w = core.weights(area, L0_ATTN)
    chain, gates_done = core.sem("vector_chain"), core.sem("ga_gate_exps")
    names = ("ga_staged", "ga_products", "ga_decays", "ga_weighted", "ga_values", "ga_state")
    staged, products, decays, weighted, values, state_done = (core.sem(n) for n in names)
    with ExitStack() as ctx:
        sb = lambda name, shape, dt=F32: ctx.enter_context(nc.sbuf_tensor(core.fresh(name), shape, dt))
        normed = sb("rms_tokens", [P, TILES, P])
        normalise_block(core, x, y, 1e-5)
        normalise_block(core, y, normed, 1e-6, affine(core, w("nw"), 0.0), rms=True)
        q_t, k_t = sb("ga_q_t", [P, G, TOKENS]), sb("ga_k_t", [P, G, TOKENS])
        pairs = [(out[:, g, :], w(a)[:, g * P:(g + 1) * P], None, w(b)[:, g * P:(g + 1) * P], None)
                 for out, a, b in ((q_t, "wq", "wqs"), (k_t, "wk", "wks")) for g in range(G)]
        rotated_product(core, pairs, w("cos"), w("sin"))
        values_in = sb("ga_v", [P, TILES, H, D])
        gate = sb("ga_gate", [P, TILES, 3 * H])
        log_f = sb("ga_log_f", [P, TILES, 2, R, G])
        magnitude, soft = sb("ga_magnitude", [P, TILES, H]), sb("ga_soft", [P, TILES, H])
        out_gate = sb("ga_out_gate", [P, TILES, H])

        def take(g, got, link):
            n = slice(g * PER_CHUNK, (g + 1) * PER_CHUNK)
            split = lambda t, m: t[:, n, :].rearrange("p (b j) m -> p b j m", b=2)
            v = values_in[:, n, :, :].rearrange("p (b j) h d -> p b j (h d)", b=2)
            nc.vector.tensor_copy(v, got[:, :, 0:2, 0:P])
            return nc.vector.tensor_tensor(split(gate, 3 * H), got[:, :, 0:2, P:P + 3 * H],
                                           w("bg").unsqueeze(1).unsqueeze(1).to_broadcast([P, 2, 2, 3 * H]), ALU.add)
        tokens_product(core, w("wvg"), take)
        with nc.Block() as block:
            @block.scalar
            def _(act):
                act_chain = core.sem("scalar_chain")
                link = Steps(act, act_chain)
                link(nc.scalar.activation(magnitude[:], gate[:, :, 0:H], ACT.Abs))
                link(nc.scalar.activation(magnitude[:], magnitude[:], ACT.Exp, scale=-1.0))
                nc.scalar.activation(out_gate[:], gate[:, :, 2 * H:], ACT.Exp, scale=-1.0).then_inc(gates_done.handle, 1)
                nc.scalar.activation(gate[:, :, H:2 * H], gate[:, :, H:2 * H], ACT.Exp, scale=-1.0).then_inc(gates_done.handle, 1)
                nc.scalar.activation(soft[:], magnitude[:], ACT.Ln, bias=1.0).then_inc(gates_done.handle, 1)
                link.close()

            @block.vector
            def _(dve):
                need(dve, gates_done, 3)
                link = Steps(dve, chain)
                for t in (out_gate[:], gate[:, :, H:2 * H]):
                    link(nc.vector.tensor_scalar(t, t, 1.0, None, ALU.add))
                    link(nc.vector.reciprocal(t, t))
                link(nc.vector.tensor_scalar(gate[:, :, H:2 * H], gate[:, :, H:2 * H], 1.0 / 4.0, None, ALU.mult))
                for n in range(2):
                    tiles = slice(n * SEQ_TILES, (n + 1) * SEQ_TILES)
                    nc.vector.tensor_tensor(values_in[:, tiles, :, :], values_in[:, tiles, :, :],
                                            gate[:, tiles, H:2 * H].unsqueeze(3).to_broadcast([P, SEQ_TILES, H, D]),
                                            ALU.mult).then_inc(gates_done.handle, 1)
                for r in range(R):
                    ins = nc.vector.scalar_tensor_tensor(
                        out=log_f[:, :, 0, r, :], in0=gate[:, :, 0:H].rearrange("p t (g r) -> p t g r", g=G)[:, :, :, r], scalar=0.0,
                        in1=soft[:].rearrange("p t (g r) -> p t g r", g=G)[:, :, :, r], op0=ALU.min, op1=ALU.subtract)
                link(ins)
                nc.vector.tensor_scalar(log_f[:, :, 1, :, :].rearrange("p t r g -> p t (r g)"),
                                        log_f[:, :, 0, :, :].rearrange("p t r g -> p t (r g)"), -1.0, None,
                                        ALU.mult).then_inc(gates_done.handle, 1)
                need(dve, gates_done, 6)
                link.close()
        gates_done.done += 6

        q_s, k_s = sb("ga_q", [P, 2, G, P]), sb("ga_k", [P, 2, G, P])
        f_s = sb("ga_f", [P, 2, 2, R, G])
        f_rows = sb("ga_f_rows", [P, 2, G, R * 32])
        v_s = sb("ga_vs", [P, 2, H, D])
        decay = sb("ga_decay", [P, 2, R, G, P])
        exps = sb("ga_exps", [P, 2, 2 * H + G])
        weights = sb("ga_weights", [P, 2, R, G, P])
        k_tok = sb("ga_k_tok", [P, 2, G, R, 32])
        inter, intra, block_u = sb("ga_inter", [P, H, D]), sb("ga_intra", [P, H, D]), sb("ga_block", [P, G, 64])
        state = sb("ga_state_m", [P, G, 64])
        o = normed
        YB, SB = psum[:, 6, :], psum[:, 7, :]
        ones_col = w("upper")[:, P - 1:P]
        TURNS = TILES // 2
        with nc.Block() as block:
            def each(engine, body):
                with engine.Fori(0, BATCH) as b:
                    body(b, None, -1)
                    with engine.Fori(0, SEQ_TILES // 2) as i:
                        for p in range(2):
                            body(b, b * SEQ_TILES + i * 2 + p, p)

            @block.gpsimd
            def _(pool):
                def body(b, n, p):
                    if n is None:
                        return
                    pool.wait_ge(state_done.handle, state_done.done + n + b + 1)
                    nc.gpsimd.tensor_copy(q_s[:, p], q_t[:, :, bass.ds(n * P, P)])
                    nc.gpsimd.tensor_copy(k_s[:, p], k_t[:, :, bass.ds(n * P, P)])
                    nc.gpsimd.tensor_copy(f_s[:, p].rearrange("p s r g -> p (s r g)").unsqueeze(1),
                                          log_f[:].rearrange("p t s r g -> p t (s r g)")[:, bass.ds(n, 1), :])
                    nc.gpsimd.tensor_copy(f_rows[:, p].rearrange("p g (r d) -> p g r d", r=R),
                                          log_f[:, :, 0, :, :].rearrange("p t r g -> p t g r")[:, bass.ds(n, 1), :, :]
                                          .rearrange("p t g r -> p (t g) r").unsqueeze(3).to_broadcast([P, G, R, 32]))
                    nc.gpsimd.tensor_copy(v_s[:, p].rearrange("p h d -> p (h d)").unsqueeze(1),
                                          values_in[:].rearrange("p t h d -> p t (h d)")[:, bass.ds(n, 1), :]).then_inc(staged.handle, 1)
                each(pool, body)

            @block.tensor
            def _(pe):
                def body(b, n, p):
                    if n is None:
                        return
                    pe.wait_ge(staged.handle, staged.done + n + 1)
                    for g in range(G):
                        nc.tensor.transpose(SB[:, P + g * P:P + (g + 1) * P], k_s[:, p, g, :], core.ident[:])
                    lf, nlf = f_s[:, p, 0].rearrange("p r g -> p (r g)"), f_s[:, p, 1].rearrange("p r g -> p (r g)")
                    nc.tensor.matmul(YB[:, 256:264], w("upper"), lf, start=True, stop=True)
                    nc.tensor.matmul(YB[:, 264:272], ones_col.to_broadcast([P, P]), lf, start=True, stop=False)
                    nc.tensor.matmul(YB[:, 264:272], w("upper"), nlf, start=False, stop=True)
                    for g in range(G):
                        nc.tensor.matmul(YB[:, 272 + g:273 + g], f_rows[:, p, g, :], ones_col,
                                         start=True, stop=True)
                    for k in range(2):
                        for a in range(4):
                            nc.tensor.matmul(psum[:, 4 + k, a * P:(a + 1) * P], lf[:, 4 * k + a:4 * k + a + 1].to_broadcast([P, P]), w("upper"),
                                             start=(a == 0), stop=False, skip_group_check=True)
                        nc.tensor.matmul(psum[:, 4 + k, :], w("upper"), nlf[:, 4 * k:4 * k + 4].unsqueeze(2).to_broadcast([P, 4, P]),
                                         start=False, stop=False, skip_group_check=True)
                        last = nc.tensor.matmul(psum[:, 4 + k, :], core.mask("ident"), core.mask("causal").unsqueeze(1).to_broadcast([P, 4, P]),
                                                start=False, stop=True, skip_group_check=True)
                    last.then_inc(products.handle, 1)
                    for g in range(G):
                        for r in range(R):
                            rows = slice(32 * r, 32 * r + D)
                            last = nc.tensor.matmul(psum[:, r, g * P:(g + 1) * P], k_s[rows, p, g, :], q_s[rows, p, g, :],
                                                    start=True, stop=True, skip_group_check=True)
                    last.then_inc(products.handle, 1)
                    pe.wait_ge(weighted.handle, weighted.done + n * 2 + 2)
                    for h in range(H):
                        nc.tensor.matmul(YB[:, h * D:(h + 1) * D], weights[:, p, h % R, h // R, :], v_s[:, p, h, :], start=True, stop=True)
                    for g in range(G):
                        nc.tensor.matmul(YB[:, P + g * 64:P + (g + 1) * 64], q_s[:, p, g, :], state[:, g, :], start=True, stop=True)
                    for g in range(G):
                        last = nc.tensor.matmul(SB[:, g * 64:(g + 1) * 64], k_tok[:, p, g].rearrange("p r d -> p (r d)"),
                                                v_s[:, p, g * R:(g + 1) * R, :], start=True, stop=True)
                    last.then_inc(values.handle, 1)
                each(pe, body)

            @block.scalar
            def _(act):
                def body(b, n, p):
                    if n is None:
                        return
                    act.wait_ge(products.handle, products.done + n * 2 + 1)
                    nc.scalar.activation(exps[:, p, :], YB[:, 256:274], ACT.Exp)
                    nc.scalar.activation(decay[:, p].rearrange("p r g n -> p (r g n)").rearrange("p (b n) -> p b n", b=2), psum[:, 4:6, :],
                                         ACT.Exp).then_inc(decays.handle, 1)
                each(act, body)

            @block.vector
            def _(dve):
                def body(b, n, p):
                    if n is None:
                        nc.vector.memset(state[:], 0.0).then_inc(state_done.handle, 1)
                        return
                    dve.wait_ge(decays.handle, decays.done + n + 1)
                    nc.vector.tensor_tensor(k_tok[:, p], SB[:, P:3 * P].rearrange("p (g r d) -> p g r d", g=G, r=R),
                                            exps[:, p, H:2 * H].rearrange("p (r g) -> p g r", r=R).unsqueeze(3).to_broadcast([P, G, R, 32]),
                                            ALU.mult).then_inc(weighted.handle, 1)
                    dve.wait_ge(products.handle, products.done + n * 2 + 2)
                    nc.vector.tensor_tensor(weights[:, p].rearrange("p r g n -> p r (g n)"), psum[:, 0:4, 0:G * P],
                                            decay[:, p].rearrange("p r g n -> p r (g n)"), ALU.mult).then_inc(weighted.handle, 1)
                    dve.wait_ge(values.handle, values.done + n + 1)
                    link = Steps(dve, chain, 2, n)
                    nc.vector.tensor_tensor(inter[:].rearrange("p (g r) d -> p g r d", g=G), YB[:, P:2 * P].rearrange("p (g r d) -> p g r d", g=G, r=R),
                                            exps[:, p, 0:H].rearrange("p (r g) -> p g r", r=R).unsqueeze(3).to_broadcast([P, G, R, D]),
                                            ALU.mult)
                    link(nc.vector.tensor_tensor(block_u[:].rearrange("p g m -> p (g m)"), SB[:, 0:P], w("diag"), ALU.mult))
                    nc.vector.tensor_tensor(intra[:].rearrange("p h d -> p (h d)"), YB[:, 0:P], inter[:].rearrange("p h d -> p (h d)"), ALU.add)
                    for g in range(G):
                        last = nc.vector.scalar_tensor_tensor(out=state[:, g, :], in0=state[:, g, :], scalar=exps[:, p, 2 * H + g:2 * H + g + 1],
                                                              in1=block_u[:, g, :], op0=ALU.mult, op1=ALU.add)
                    link(last)
                    nc.vector.tensor_tensor(o[:].rearrange("p t (h d) -> p t h d", h=H)[:, bass.ds(n, 1), :, :], intra[:].unsqueeze(1),
                                                 out_gate[:, bass.ds(n, 1), :].unsqueeze(3).to_broadcast([P, 1, H, D]), ALU.mult).then_inc(state_done.handle, 1)
                each(dve, body)
        chain.done += 2 * TILES
        for tally, n in ((staged, 1), (products, 2), (decays, 1), (weighted, 2), (values, 1), (state_done, 1)):
            tally.done += n * TILES
        state_done.done += BATCH
        normalise_block(core, x, o, 1e-5, plain(core), only_transpose=True)
        tokens_product(core, w("wout"), add_to_x(core, bias=w("bout")))


STACK = 74
MAX_ROWS = 64


class Stacks:

    PARTS = [(a, b) for a in range(3) for b in range(3)]

    def __init__(self, core, ctx, before, behind):
        nc = core.nc
        sb = lambda name, shape, dt: ctx.enter_context(nc.sbuf_tensor(core.fresh(name), shape, dt))
        self.before, self.behind = before, behind
        self.q = sb("stack_q", [P, FA_HEADS, SEQ + behind], BF16)
        self.k = sb("stack_k", [P, FA_HEADS, before + SEQ], BF16)
        self.parts = [[sb(f"part_{n}{i}", [P, SEQ], BF16) for i in range(3)] for n in "qk"]
        self.scratch = nc.dram_tensor(core.fresh("parts_dram"), (2, 3, P, SEQ), BF16).ap()

    def fill(self, core, q, k, b):
        nc = core.nc
        chain, split, placed, cleared = (core.sem(n) for n in ("vector_chain", "parts_split", "parts_placed", "stack_cleared"))
        stored = [core.sem("q_parts_stored"), core.sem("k_parts_stored")]
        with nc.Block() as block:
            @block.vector
            def _(dve):
                link = Steps(dve, chain)
                for src, parts in ((q, self.parts[0]), (k, self.parts[1])):
                    link(nc.vector.tensor_copy(parts[0][:], src))
                    link(nc.vector.tensor_tensor(src, src, parts[0][:], ALU.subtract))
                    link(nc.vector.tensor_copy(parts[1][:], src))
                    nc.vector.tensor_tensor(parts[2][:], src, parts[1][:], ALU.subtract).then_inc(split.handle, 1)
                link.close()

            @block.gpsimd
            def _(pool):
                if b == 0:
                    if self.before:
                        nc.gpsimd.memset(self.k[0:96, :, 0:self.before], 0.0).then_inc(cleared.handle, 1)
                        nc.gpsimd.memset(self.q[0:96, :, SEQ:], 0.0).then_inc(cleared.handle, 1)
                        need(pool, cleared, 2)
                    nc.gpsimd.memset(self.k[MAX_ROWS:MAX_ROWS + 2, :, :], 1.0).then_inc(cleared.handle, 1)
                nc.gpsimd.memset(self.q[MAX_ROWS:MAX_ROWS + 2, :, 0:SEQ], 0.0).then_inc(cleared.handle, 1)

            def place(engine, which, to, at):
                need(engine, split, which + 1)
                for i in range(3):
                    engine.dma_start(self.scratch[which, i], self.parts[which][i][:]).then_inc(stored[which].handle, 16)
                need(engine, stored[which], 48)
                if b == 0 and self.before:
                    need(engine, cleared, 2)
                for n, pair in enumerate(self.PARTS):
                    row = 8 * n + (2 if 8 * n >= MAX_ROWS else 0)
                    engine.dma_start(to[row:row + 8, :, at:at + SEQ],
                                     self.scratch[which, pair[which]].rearrange("(h d) t -> d h t", d=FA_DIM)
                                     ).then_inc(placed.handle, 16)

            @block.sync
            def _(sp):
                place(sp, 0, self.q, 0)
                need(sp, placed, 16 * 2 * len(self.PARTS))

            @block.scalar
            def _(act):
                place(act, 1, self.k, self.before)
        split.done += 2
        for tally in stored:
            tally.done += 48
        cleared.done += 1 if b else 2 + 2 * bool(self.before)
        placed.done += 16 * 2 * len(self.PARTS)


def value_tokens(core, out, weights, bias):
    nc = core.nc
    ones = core.sem("value_ones")
    with nc.Block() as block:
        @block.gpsimd
        def _(pool):
            nc.gpsimd.memset(out, 1.0).then_inc(ones.handle, 1)
    ones.done += 1

    def take(g, got, link):
        to = out[:, g * PER_CHUNK:(g + 1) * PER_CHUNK, :, 0:FA_DIM]
        got = got.rearrange("p j (h d) -> p j h d", h=FA_HEADS)
        if bias is None:
            return nc.vector.tensor_copy(to, got)
        for j in range(PER_CHUNK):
            last = nc.vector.tensor_tensor(to[:, j], got[:, j], bias.rearrange("p (h d) -> p h d", h=FA_HEADS), ALU.add)
        return last
    tokens_product(core, weights, take)


def l1_attn(core, area):
    nc, psum, x, y, zt = core.nc, core.psum, core.x, core.y, core.zt
    w = core.weights(area, L1_ATTN)
    H, D = FA_HEADS, FA_DIM
    base = sum(n for _, n in L1_ATTN)
    q_t, k_t = (core.areas[area][:, base + i * TOKENS:base + (i + 1) * TOKENS] for i in range(2))
    chain = core.sem("vector_chain")
    (max_scores, max_read, tops, tops_turned, rows_ready, rows_placed, scores, probs, used, values, normed) = (
        core.sem(n) for n in ("fa_max_scores", "fa_max_read", "fa_tops", "fa_tops_turned", "fa_rows_split", "fa_rows_placed",
                              "fa_scores", "fa_probs", "fa_probs_used", "fa_values", "fa_normed"))
    with ExitStack() as ctx:
        sb = lambda name, shape, dt=F32: ctx.enter_context(nc.sbuf_tensor(core.fresh(name), shape, dt))
        normalise_block(core, x, y, 1e-5, plain(core))
        rotated_product(core, [(q_t, w("wq"), w("bq"), w("wqs"), w("bqs")), (k_t, w("wk"), w("bk"), w("wks"), w("bks"))],
                        w("cos"), w("sin"))
        v = sb("fa_v", [P, TILES, H, D + 1])
        value_tokens(core, v[:], w("wv"), w("bv"))
        stacks = Stacks(core, ctx, 0, 0)
        prob = sb("fa_prob", [P, 2, SEQ])
        half_top, top = sb("fa_half_top", [P, 2 * SEQ_TILES]), sb("fa_top", [P, SEQ_TILES])
        low = sb("fa_low", [SEQ_TILES, P])
        rows = sb("fa_rows", [SEQ_TILES, 2, P], BF16)
        max_dram = nc.dram_tensor("fa_max_dram", (2, SEQ), BF16).ap()
        rows_stored = core.sem("fa_rows_stored")
        rec = sb("fa_rec", [P, SEQ_TILES])
        T = SEQ_TILES
        q_s = stacks.q[0:STACK].rearrange("p h t -> p (h t)")
        k_s = stacks.k[0:STACK].rearrange("p h t -> p (h t)")
        v_s = v[:].rearrange("p t h e -> p t (h e)")
        for b in range(BATCH):
            stacks.fill(core, q_t[:, b * SEQ:(b + 1) * SEQ], k_t[:, b * SEQ:(b + 1) * SEQ], b)

            def pe_max(pe, a, t):
                for half in range(2):
                    if not (isinstance(a, int) and a == 0 and t == 0):
                        pe.wait_ge(max_read.handle, max_read.done + a * 2 * T + 2 * t + half - 1)
                    nc.tensor.matmul(psum[:, half, :], q_s[:, bass.ds(a * SEQ + t * P, P)], k_s[:, bass.ds(a * SEQ + half * CHUNK, CHUNK)],
                                     start=True, stop=True).then_inc(max_scores.handle, 1)

            def pe_turn_max(pe, a):
                pe.wait_ge(tops.handle, tops.done + a + 1)
                nc.tensor.transpose(psum[0:T, 7, 0:P], top[:], core.ident[:]).then_inc(tops_turned.handle, 1)

            def pe_head(pe, n, ahead, first):
                pe.wait_ge(rows_placed.handle, rows_placed.done + n * 16 + 16)

                def on_values(t):
                    pe.wait_ge(probs.handle, probs.done + n * T + t + 1)
                    if t == 0 and not first:
                        pe.wait_ge(normed.handle, normed.done + n)
                    for s in range(T):
                        last = nc.tensor.matmul(psum[:, 6, s * (D + 1):(s + 1) * (D + 1)], prob[:, t % 2, s * P:(s + 1) * P],
                                                v_s[:, b * T + t, bass.ds(n * (D + 1), D + 1)],
                                                start=(t == 0 and s == 0), stop=(t == T - 1), skip_group_check=True)
                    last.then_inc(used.handle, 1)
                for t in range(T):
                    if t >= 2:
                        pe.wait_ge(probs.handle, probs.done + n * T + t - 1)
                    elif not first:
                        pe.wait_ge(probs.handle, probs.done + n * T + t - 1)
                    for half in range(2):
                        last = nc.tensor.matmul(psum[:, 2 + 2 * (t % 2) + half, :], k_s[:, bass.ds(n * SEQ + t * P, P)],
                                                q_s[:, bass.ds(n * SEQ + half * CHUNK, CHUNK)], start=True, stop=True)
                    last.then_inc(scores.handle, 1)
                    if ahead:
                        pe_max(pe, n + 2, t)
                    if t:
                        on_values(t - 1)
                on_values(T - 1)
                if ahead:
                    pe_turn_max(pe, n + 2)

            def act_head(act, n, first):
                for t in range(T):
                    act.wait_ge(scores.handle, scores.done + n * T + t + 1)
                    if t >= 2 or not first:
                        act.wait_ge(used.handle, used.done + n * T + t - 1)
                    nc.scalar.activation(prob[:, t % 2, :], psum[:, 2 + 2 * (t % 2):4 + 2 * (t % 2), :].rearrange("p a n -> p (a n)"),
                                         ACT.Exp, scale=float(D) ** -0.5).then_inc(probs.handle, 1)

            MAX_STEPS, VALUE_STEPS = 3, 1

            def dve_max(dve, a, link):
                for t in range(T):
                    for half in range(2):
                        dve.wait_ge(max_scores.handle, max_scores.done + a * 2 * T + 2 * t + half + 1)
                        nc.vector.tensor_reduce(half_top[:, 2 * t + half:2 * t + half + 1], psum[:, half, :], AX.X,
                                                ALU.max).then_inc(max_read.handle, 1)
                dve.wait_ge(max_read.handle, max_read.done + (a + 1) * 2 * T)
                nc.vector.tensor_reduce(top[:], half_top[:].rearrange("p (t a) -> p t a", a=2), AX.X, ALU.max, negate=True).then_inc(tops.handle, 1)
                dve.wait_ge(tops_turned.handle, tops_turned.done + a + 1)
                if not (isinstance(a, int) and a == 0):
                    dve.wait_ge(rows_placed.handle, rows_placed.done + a * 16)
                link(nc.vector.tensor_copy(rows[:, 0, :], psum[0:T, 7, 0:P]))
                nc.vector.tensor_tensor(rows[:, 1, :], psum[0:T, 7, 0:P], rows[:, 0, :], ALU.subtract).then_inc(rows_ready.handle, 1)

            def dve_values(dve, n, link):
                dve.wait_ge(used.handle, used.done + (n + 1) * T)
                got = psum[:, 6, 0:T * (D + 1)].rearrange("p (t e) -> p t e", e=D + 1)
                link(nc.vector.reciprocal(rec[:], got[:, :, D]))
                nc.vector.tensor_tensor(y[:, b * T:(b + 1) * T, bass.ds(n * D, D)], got[:, :, 0:D], rec[:].unsqueeze(2).to_broadcast([P, T, D]),
                                        ALU.mult).then_inc(normed.handle, 1)

            def sp_rows(sp, a, first):
                sp.wait_ge(rows_ready.handle, rows_ready.done + a + 1)
                if not first:
                    sp.wait_ge(rows_placed.handle, rows_placed.done + a * 16)
                sp.dma_start(max_dram.rearrange("i (q t) -> q i t", t=P), rows[:]).then_inc(rows_stored.handle, 16)
                sp.wait_ge(rows_stored.handle, rows_stored.done + (a + 1) * 16)
                sp.dma_start(stacks.q[MAX_ROWS:MAX_ROWS + 2, :, :].rearrange("p h t -> p (h t)")[:, bass.ds(a * SEQ, SEQ)],
                             max_dram).then_inc(rows_placed.handle, 16)

            with nc.Block() as block:
                @block.tensor
                def _(pe):
                    for a in range(2):
                        for t in range(T):
                            pe_max(pe, a, t)
                        pe_turn_max(pe, a)
                    pe_head(pe, 0, True, True)
                    with pe.Fori(1, H - 2) as n:
                        pe_head(pe, n, True, False)
                    for n in (H - 2, H - 1):
                        pe_head(pe, n, False, False)

                @block.scalar
                def _(act):
                    act_head(act, 0, True)
                    with act.Fori(1, H) as n:
                        act_head(act, n, False)

                @block.vector
                def _(dve):
                    link = Steps(dve, chain)
                    for a in range(2):
                        dve_max(dve, a, link)
                    link.close()
                    with dve.Fori(0, H - 2) as n:
                        link = Steps(dve, chain, 2, n)
                        dve_max(dve, n + 2, link)
                        dve_values(dve, n, link)
                    link.close(H - 2)
                    link = Steps(dve, chain)
                    for n in (H - 2, H - 1):
                        dve_values(dve, n, link)
                    link.close()

                @block.sync
                def _(sp):
                    sp_rows(sp, 0, True)
                    for a in range(1, H):
                        sp_rows(sp, a, False)
            for tally, n in ((max_scores, 2 * T), (max_read, 2 * T), (tops, 1), (tops_turned, 1), (rows_ready, 1), (rows_placed, 16), (rows_stored, 16),
                             (scores, T), (probs, T), (used, T), (normed, 1)):
                tally.done += n * H
        normalise_block(core, x, y, 1e-5, plain(core), only_transpose=True)
        tokens_product(core, w("wo"), add_to_x(core, bias=w("bo")))


I32 = mybir.dt.int32
QUANT_STEPS = 14


def quantise(nc, link, source, out, tmp, ready=None):
    n = source.shape[1]
    blocks = lambda t: t[:, 0:n].rearrange("p (b e) -> p b e", e=Q4_BLOCK)
    nb = n // Q4_BLOCK
    biggest, scale, inverse = (t[:, 0:nb] for t in tmp["small"])
    scaled, size, high, low = (t[:, 0:n] for t in tmp["wide"])
    spread = lambda t: t.unsqueeze(2).to_broadcast([P, nb, Q4_BLOCK])
    link(nc.vector.tensor_reduce(biggest, blocks(source), AX.X, ALU.max, apply_absolute_value=True))
    link(nc.vector.tensor_scalar(scale, biggest, 1.0 / 6.0, 1e-12, ALU.mult, ALU.max))
    link(nc.vector.reciprocal(inverse, scale))
    link(nc.vector.tensor_tensor(blocks(scaled), blocks(source), spread(inverse), ALU.mult))
    link(nc.vector.tensor_scalar(size.bitcast(I32), scaled.bitcast(I32), 0x7FFFFFFF, None, ALU.bitwise_and))
    link(nc.vector.tensor_scalar(high, size, 5.0, 2.0, ALU.is_gt, ALU.mult))
    for mid in (3.5, 2.5):
        link(nc.vector.scalar_tensor_tensor(out=high, in0=size, scalar=mid, in1=high, op0=ALU.is_gt, op1=ALU.add))
    link(nc.vector.tensor_scalar(low, size, 1.75, None, ALU.is_gt))
    for mid in (1.25, 0.75, 0.25):
        link(nc.vector.scalar_tensor_tensor(out=low, in0=size, scalar=mid, in1=low, op0=ALU.is_gt, op1=ALU.add))
    link(nc.vector.scalar_tensor_tensor(out=high, in0=low, scalar=0.5, in1=high, op0=ALU.mult, op1=ALU.add))
    link(nc.vector.scalar_tensor_tensor(out=low.bitcast(I32), in0=scaled.bitcast(I32), scalar=-2147483648, in1=high.bitcast(I32),
                                        op0=ALU.bitwise_and, op1=ALU.bitwise_or))
    last = nc.vector.tensor_tensor(blocks(out), blocks(low), spread(scale), ALU.mult)
    link(last) if ready is None else last.then_inc(ready.handle, 1)


def l2_ffn(core, area):
    nc, psum, x, y, zt = core.nc, core.psum, core.x, core.y, core.zt
    w = core.weights(area, L2_FFN)
    chain = core.sem("vector_chain")
    base = sum(n for _, n in L2_FFN)
    gate_up = core.areas[area][:, base:base + 2 * Q4_HID]
    down = core.areas[area][:, base + 2 * Q4_HID:base + 2 * Q4_HID + 3 * P]
    turned, taken = core.sem("bank_transposed"), core.sem("bank_evacuated")
    products, silu, gated, ready, h_turned, h_taken, out_made, added = (core.sem(n) for n in (
        "q4_up_product", "q4_silu", "q4_gated", "q4_hidden_quantised", "q4_hidden_turned", "q4_hidden_taken",
        "q4_out_product", "q4_added"))
    WIDE = PER_CHUNK * Q4_HID
    with ExitStack() as ctx:
        sb = lambda name, shape, dt=F32: ctx.enter_context(nc.sbuf_tensor(core.fresh(name), shape, dt))
        tmp = {"small": [sb(f"q4_small{i}", [P, WIDE // Q4_BLOCK]) for i in range(3)],
               "wide": [sb(f"q4_wide{i}", [P, WIDE]) for i in range(4)]}
        if not core.weights_quantised:
            core.weights_quantised = True
            dequant = sb("q4_weights", [P, 6 * P + Q4_HID])
            with nc.Block() as block:
                @block.vector
                def _(dve):
                    link = Steps(dve, chain)
                    packed = core.areas[area][:, 0:base]
                    quantise(nc, link, packed, dequant, tmp)
                    link.close()
            with nc.Block() as block:
                @block.tensor
                def _(pe):
                    for s in range(2):
                        for m, (at, rows) in enumerate(Q4_PARTS):
                            last = nc.tensor.transpose(psum[:, s, at:at + rows], dequant[0:rows, (3 * s + m) * P:(3 * s + m + 1) * P],
                                                       core.ident[0:rows, 0:rows])
                    for m, (at, rows) in enumerate(Q4_PARTS):
                        last = nc.tensor.transpose(psum[0:rows, 2, m * P:(m + 1) * P], dequant[:, 6 * P + at:6 * P + at + rows], core.ident[:])
                    last.then_inc(turned.handle, 1)

                @block.scalar
                def _(act):
                    need(act, turned, 1)
                    nc.scalar.copy(gate_up.rearrange("p (s n) -> p s n", s=2), psum[:, 0:2, 0:Q4_HID]).then_inc(taken.handle, 1)
                    for m, (at, rows) in enumerate(Q4_PARTS):
                        nc.scalar.copy(down[0:rows, m * P:(m + 1) * P], psum[0:rows, 2, m * P:(m + 1) * P]).then_inc(taken.handle, 1)
            turned.done += 1
            taken.done += 4
        normalise_block(core, x, y, 1e-5)
        with nc.Block() as block:
            @block.vector
            def _(dve):
                link = Steps(dve, chain)
                half = TOKENS // 2
                flat = y[:].rearrange("p t d -> p (t d)")
                for b in range(2):
                    quantise(nc, link, flat[:, b * half:(b + 1) * half], flat[:, b * half:(b + 1) * half], tmp)
                link.close()
        normalise_block(core, x, y, 1e-5, plain(core), only_transpose=True)
        act_gate = sb("q4_gate", [P, 2, Q4_HID])
        hidden = sb("q4_hidden", [P, PER_CHUNK, Q4_HID])
        hidden_q = sb("q4_hidden_q", [P, PER_CHUNK, Q4_HID])
        hidden_t = sb("q4_hidden_t", [P, 3, CHUNK])
        with nc.Block() as block:
            @block.tensor
            def _(pe):
                def up(c):
                    for j in range(PER_CHUNK):
                        n = c * PER_CHUNK + j
                        if n >= 2:
                            need(pe, gated, n - 1)
                        for s in range(2):
                            last = nc.tensor.matmul(psum[:, 2 * (n % 2) + s, 0:Q4_HID], zt[:, n * P:(n + 1) * P],
                                                    gate_up[:, s * Q4_HID:(s + 1) * Q4_HID], start=True, stop=True)
                        last.then_inc(products.handle, 1)
                for c in range(CHUNKS):
                    up(c)
                    need(pe, ready, c + 1)
                    for m, (at, rows) in enumerate(Q4_PARTS):
                        for j in range(PER_CHUNK):
                            last = nc.tensor.transpose(psum[0:rows, 4 + m, j * P:(j + 1) * P], hidden_q[:, j, at:at + rows], core.ident[:])
                    last.then_inc(h_turned.handle, 1)
                    need(pe, h_taken, 3 * (c + 1))
                    if c >= 1:
                        need(pe, added, c)
                    for j in range(PER_CHUNK):
                        for m, (at, rows) in enumerate(Q4_PARTS):
                            last = nc.tensor.matmul(psum[:, 7, j * P:(j + 1) * P], hidden_t[0:rows, m, j * P:(j + 1) * P],
                                                    down[0:rows, m * P:(m + 1) * P], start=(m == 0), stop=(m == 2))
                    last.then_inc(out_made.handle, 1)

            @block.scalar
            def _(act):
                for c in range(CHUNKS):
                    for j in range(PER_CHUNK):
                        n = c * PER_CHUNK + j
                        need(act, products, n + 1)
                        if n >= 2:
                            need(act, gated, n - 1)
                        nc.scalar.activation(act_gate[:, n % 2, :], psum[:, 2 * (n % 2), 0:Q4_HID], ACT.Silu).then_inc(silu.handle, 1)
                    need(act, h_turned, c + 1)
                    for m, (at, rows) in enumerate(Q4_PARTS):
                        nc.scalar.copy(hidden_t[0:rows, m, :], psum[0:rows, 4 + m, :]).then_inc(h_taken.handle, 1)

            @block.vector
            def _(dve):
                with dve.Fori(0, CHUNKS) as c:
                    for j in range(PER_CHUNK):
                        dve.wait_ge(silu.handle, silu.done + c * PER_CHUNK + j + 1)
                        nc.vector.tensor_tensor(hidden[:, j, :], psum[:, 2 * (j % 2) + 1, 0:Q4_HID], act_gate[:, j % 2, :],
                                                ALU.mult).then_inc(gated.handle, 1)
                    dve.wait_ge(gated.handle, gated.done + (c + 1) * PER_CHUNK)
                    link = Steps(dve, chain, QUANT_STEPS, c)
                    quantise(nc, link, hidden[:].rearrange("p j n -> p (j n)"), hidden_q[:].rearrange("p j n -> p (j n)"), tmp, ready)
                    dve.wait_ge(out_made.handle, out_made.done + c + 1)
                    tiles = x[:, bass.ds(c * PER_CHUNK, PER_CHUNK), :]
                    nc.vector.scalar_tensor_tensor(out=tiles, in0=psum[:, 7, :].rearrange("p (j n) -> p j n", j=PER_CHUNK), scalar=0.5,
                                                   in1=tiles, op0=ALU.mult, op1=ALU.add).then_inc(added.handle, 1)
                link.close(CHUNKS)
        for tally, n in ((products, TILES), (silu, TILES), (gated, TILES), (ready, CHUNKS), (h_turned, CHUNKS),
                         (h_taken, 3 * CHUNKS), (out_made, CHUNKS), (added, CHUNKS)):
            tally.done += n



def l2_attn(core, area):
    nc, psum, x, y, zt = core.nc, core.psum, core.x, core.y, core.zt
    w = core.weights(area, L2_ATTN)
    H, D, T, W = FA_HEADS, FA_DIM, SEQ_TILES, WA_WIN
    GROUP = 3
    GROUPS = [(g, min(GROUP, H - g)) for g in range(0, H, GROUP)]
    FULL = H // GROUP
    chain = core.sem("vector_chain")
    (feature_made, feature_taken, max_scores, tops, tops_turned, rows_ready, rows_stored, rows_placed, scores, probs, values, normed,
     prev_cleared) = (core.sem(n) for n in (
        "wa_feature_product", "wa_feature_taken", "wa_max_scores", "wa_tops", "wa_tops_turned", "wa_rows_split", "wa_rows_stored",
        "wa_rows_placed", "wa_scores", "wa_probs", "wa_values", "wa_normed", "wa_prev_cleared"))
    with ExitStack() as ctx:
        sb = lambda name, shape, dt=F32: ctx.enter_context(nc.sbuf_tensor(core.fresh(name), shape, dt))
        o = sb("wa_tokens", [P, TILES, P])
        normalise_block(core, x, y, 1e-5)
        normalise_block(core, y, o, 1e-5, affine(core, w("gamma"), w("beta")))
        spare = L2_FFN_HELD
        q_t, k_t = (core.areas[0][:, spare + i * TOKENS:spare + (i + 1) * TOKENS] for i in range(2))
        with nc.Block() as block:
            @block.tensor
            def _(pe):
                for n in range(2 * CHUNKS):
                    if n >= 4:
                        need(pe, feature_taken, n - 3)
                    nc.tensor.matmul(psum[:, n % 4, :], w("wq" if n < CHUNKS else "wk"), zt[:, n % CHUNKS * CHUNK:(n % CHUNKS + 1) * CHUNK],
                                     start=True, stop=True).then_inc(feature_made.handle, 1)

            @block.scalar
            def _(act):
                for n in range(2 * CHUNKS):
                    need(act, feature_made, n + 1)
                    to = q_t if n < CHUNKS else k_t
                    nc.scalar.copy(to[:, n % CHUNKS * CHUNK:(n % CHUNKS + 1) * CHUNK], psum[:, n % 4, :]).then_inc(feature_taken.handle, 1)
        feature_made.done += 2 * CHUNKS
        feature_taken.done += 2 * CHUNKS
        v = core.areas[0][:, spare + 2 * TOKENS:spare + 2 * TOKENS + TILES * H * (D + 1)].rearrange("p (t h e) -> p t h e", t=TILES, h=H)
        value_tokens(core, v, w("wv"), None)
        stacks = Stacks(core, ctx, W, W)
        prob = sb("wa_prob", [P, 2, H, BAND])
        top = sb("wa_top", [P, 2, H])
        rows = sb("wa_rows", [H, 2, SEQ], BF16)
        rec = sb("wa_rec", [P, H])
        max_dram = nc.dram_tensor("wa_max_dram", (2, H, SEQ), BF16).ap()
        for b in range(BATCH):
            stacks.fill(core, q_t[:, b * SEQ:(b + 1) * SEQ], k_t[:, b * SEQ:(b + 1) * SEQ], b)
            q_s, k_s = stacks.q[0:STACK], stacks.k[0:STACK]
            with nc.Block() as block:
                @block.tensor
                def _(pe):
                    def tile(t, first):
                        for g, (head, n) in enumerate(GROUPS):
                            if g == 0 and not first:
                                pe.wait_ge(tops.handle, tops.done + t)
                            for h in range(n):
                                nc.tensor.matmul(psum[:, g, h * BAND:(h + 1) * BAND], q_s[:, head + h, bass.ds(t * P, P)],
                                                 k_s[:, head + h, bass.ds(t * P, BAND)], start=(h == 0), stop=False, skip_group_check=True)
                            last = nc.tensor.matmul(psum[:, g, 0:n * BAND], core.mask("ident"),
                                                    core.mask("band_q")[:, bass.ds(t * BAND, BAND)].unsqueeze(1).to_broadcast([P, n, BAND]),
                                                    start=False, stop=True, skip_group_check=True)
                        last.then_inc(max_scores.handle, 1)
                        pe.wait_ge(tops.handle, tops.done + t + 1)
                        nc.tensor.transpose(psum[0:H, 6, 0:P], top[:, 0, :], core.ident[:]).then_inc(tops_turned.handle, 1)
                    tile(0, True)
                    with pe.Fori(1, T) as t:
                        tile(t, False)

                @block.vector
                def _(dve):
                    with dve.Fori(0, T) as t:
                        link = Steps(dve, chain, 2, t)
                        dve.wait_ge(max_scores.handle, max_scores.done + t + 1)
                        nc.vector.tensor_reduce(top[:, 0, 0:FULL * GROUP], psum[:, 0:FULL, 0:GROUP * BAND].rearrange("p g (h k) -> p g h k", k=BAND),
                                                AX.X, ALU.max, negate=True)
                        nc.vector.tensor_reduce(top[:, 0, FULL * GROUP:], psum[:, FULL, 0:BAND], AX.X, ALU.max,
                                                negate=True).then_inc(tops.handle, 1)
                        dve.wait_ge(tops_turned.handle, tops_turned.done + t + 1)
                        link(nc.vector.tensor_copy(rows[:, 0, bass.ds(t * P, P)], psum[0:H, 6, 0:P]))
                        link(nc.vector.tensor_tensor(rows[:, 1, bass.ds(t * P, P)], psum[0:H, 6, 0:P], rows[:, 0, bass.ds(t * P, P)], ALU.subtract))
                    nc.vector.memset(prob[:, 1, :, P:BAND], 0.0).then_inc(rows_ready.handle, 1)
                    link.close(T)

                @block.sync
                def _(sp):
                    need(sp, rows_ready, 1)
                    sp.dma_start(max_dram.rearrange("i h t -> h i t"), rows[:]).then_inc(rows_stored.handle, 16)
                    need(sp, rows_stored, 16)
                    sp.dma_start(stacks.q[MAX_ROWS:MAX_ROWS + 2, :, 0:SEQ], max_dram).then_inc(rows_placed.handle, 16)
                    need(sp, rows_placed, 16)
            for tally, n in ((max_scores, T), (tops, T), (tops_turned, T), (rows_ready, 1), (rows_stored, 16), (rows_placed, 16)):
                tally.done += n
            with nc.Block() as block:
                @block.tensor
                def _(pe):
                    def tile(t, p, first):
                        if not first:
                            pe.wait_ge(probs.handle, probs.done + t)
                        for g, (head, n) in enumerate(GROUPS):
                            for h in range(n):
                                nc.tensor.matmul(psum[:, g, h * BAND:(h + 1) * BAND], k_s[:, head + h, bass.ds(t * P + W, P)],
                                                 q_s[:, head + h, bass.ds(t * P, BAND)], start=(h == 0), stop=False, skip_group_check=True)
                            last = nc.tensor.matmul(psum[:, g, 0:n * BAND], core.mask("ident"), core.mask("band_k").unsqueeze(1).to_broadcast([P, n, BAND]),
                                                    start=False, stop=True, skip_group_check=True)
                        last.then_inc(scores.handle, 1)
                        pe.wait_ge(probs.handle, probs.done + t + 1)
                        if not first:
                            pe.wait_ge(normed.handle, normed.done + t)
                        v_now = v.rearrange("p t h e -> p (t h e)")
                        width = H * (D + 1)
                        for h in range(H):
                            nc.tensor.matmul(psum[:, 6, h * (D + 1):(h + 1) * (D + 1)], prob[:, p, h, 0:P],
                                             v_now[:, bass.ds((b * T + t) * width + h * (D + 1), D + 1)], start=(h == 0), stop=False,
                                             skip_group_check=True)
                        before = (b * T + t - (0 if first else 1)) * width
                        for h in range(H):
                            last = nc.tensor.matmul(psum[0:W, 6, h * (D + 1):(h + 1) * (D + 1)], prob[:, 1 - p, h, P:BAND],
                                                    v_now[:, bass.ds(before + h * (D + 1), D + 1)], start=False, stop=(h == H - 1),
                                                    skip_group_check=True)
                        last.then_inc(values.handle, 1)
                    tile(0, 0, True)
                    tile(1, 1, False)
                    with pe.Fori(1, T // 2) as i:
                        for p in range(2):
                            tile(i * 2 + p, p, False)

                @block.scalar
                def _(act):
                    def tile(t, p, first):
                        act.wait_ge(scores.handle, scores.done + t + 1)
                        if not first:
                            act.wait_ge(values.handle, values.done + t)
                        for g, n in ((0, FULL), (FULL, 1)):
                            heads = GROUP if g == 0 else GROUPS[-1][1]
                            last = nc.scalar.activation(prob[:, p, g * GROUP:g * GROUP + n * heads, :].rearrange("p (g h) k -> p g (h k)", g=n),
                                                        psum[:, g:g + n, 0:heads * BAND], ACT.Exp, scale=float(D) ** -0.5)
                        last.then_inc(probs.handle, 1)
                    tile(0, 0, True)
                    tile(1, 1, False)
                    with act.Fori(1, T // 2) as i:
                        for p in range(2):
                            tile(i * 2 + p, p, False)

                @block.vector
                def _(dve):
                    with dve.Fori(0, T) as t:
                        link = Steps(dve, chain, 1, t)
                        dve.wait_ge(values.handle, values.done + t + 1)
                        got = psum[:, 6, 0:H * (D + 1)].rearrange("p (h e) -> p h e", e=D + 1)
                        link(nc.vector.reciprocal(rec[:], got[:, :, D]))
                        nc.vector.tensor_tensor(o[:].rearrange("p t (h d) -> p t h d", h=H)[:, bass.ds(b * T + t, 1)], got[:, :, 0:D].unsqueeze(1),
                                                rec[:].unsqueeze(1).unsqueeze(3).to_broadcast([P, 1, H, D]), ALU.mult).then_inc(normed.handle, 1)
                    link.close(T)
            for tally, n in ((scores, T), (probs, T), (values, T), (normed, T)):
                tally.done += n
        normalise_block(core, x, o, 1e-5, plain(core), only_transpose=True)
        tokens_product(core, w("wout"), add_to_x(core, also=y))



def l3_attn(core, area):
    nc, psum, x, y, zt = core.nc, core.psum, core.x, core.y, core.zt
    w = core.weights(area, L3_ATTN)
    L, S = RA_STEP, RA_SEG
    K = 3
    chain, made, taken = core.sem("vector_chain"), core.sem("ra_product"), core.sem("ra_activated")
    with ExitStack() as ctx:
        sb = lambda name, shape, dt=F32: ctx.enter_context(nc.sbuf_tensor(core.fresh(name), shape, dt))
        normalise_block(core, x, y, 1e-5, plain(core))
        q, k, v, g, beta = (sb(n, [P, TOKENS]) for n in ("ra_q", "ra_k", "ra_v", "ra_g", "ra_beta"))
        decay = sb("ra_decay_gates", [P, 2, TOKENS])
        runs = [("wq", q[:], ACT.Silu, None), ("wk", k[:], ACT.Silu, None), ("wv", v[:], ACT.Silu, None),
                ("wg", g[:], ACT.Sigmoid, None), ("wb", beta[:], ACT.Sigmoid, None),
                ("wfd", decay[:, 0, :], ACT.Sigmoid, "bfd"), ("wsd", decay[:, 1, :], ACT.Sigmoid, "bsd")]
        N = len(runs)
        with nc.Block() as block:
            @block.tensor
            def _(pe):
                for r, (name, _, _, _) in enumerate(runs):
                    for c in range(CHUNKS):
                        n = r * CHUNKS + c
                        if n >= 4:
                            need(pe, taken, n - 3)
                        nc.tensor.matmul(psum[:, n % 4, :], w(name), zt[:, c * CHUNK:(c + 1) * CHUNK],
                                         start=True, stop=True).then_inc(made.handle, 1)

            @block.scalar
            def _(act):
                for r, (_, out, func, bias) in enumerate(runs):
                    for c in range(CHUNKS):
                        n = r * CHUNKS + c
                        need(act, made, n + 1)
                        nc.scalar.activation(out[:, c * CHUNK:(c + 1) * CHUNK], psum[:, n % 4, :], func,
                                             bias=0.0 if bias is None else w(bias)).then_inc(taken.handle, 1)

            @block.vector
            def _(dve):
                link = Steps(dve, chain)
                need(dve, taken, 3 * CHUNKS)
                link(nc.vector.scalar_tensor_tensor(out=k[:], in0=k[:], scalar=1.0 + RA_MIX, in1=v[:], op0=ALU.mult, op1=ALU.mult))
                need(dve, taken, 4 * CHUNKS)
                nc.vector.scalar_tensor_tensor(out=q[:], in0=q[:], scalar=0.5, in1=g[:], op0=ALU.mult, op1=ALU.mult)
                need(dve, taken, 5 * CHUNKS)
                link(nc.vector.tensor_tensor(k[:], k[:], beta[:], ALU.mult))
                link.close()
        made.done += N * CHUNKS
        taken.done += N * CHUNKS

        states, faded = sb("ra_states", [P, 2, K, S]), sb("ra_faded", [P, 2, K, S])
        read = sb("ra_read", [P, K, S, L])
        starts = sb("ra_starts", [P, 2, S])
        piece = sb("ra_piece", [P, 2, 2, BATCH])
        seg = S // BATCH
        state2 = lambda t: t[:].rearrange("p a k s -> p a (k s)")
        u = k[:].rearrange("p (s l) -> p s l", l=L)
        fades = decay[:].rearrange("p a (s l) -> p a s l", l=L)
        with nc.Block() as block:
            @block.vector
            def _(dve):
                link = Steps(dve, chain)
                link(nc.vector.memset(states[:], 0.0))
                nc.vector.memset(states[:, 0, 1, :], 1.0)
                nc.vector.memset(starts[:], 0.0)
                link(nc.vector.memset(states[:, 1, 2, :], 1.0))
                link.close()
                with dve.Fori(0, L) as t:
                    link = Steps(dve, chain, 3, t)
                    link(nc.vector.tensor_tensor(faded[:], states[:],
                                                 fades[:, :, :, bass.ds(t, 1)].rearrange("p a s l -> p a (s l)").unsqueeze(2)
                                                 .to_broadcast([P, 2, K, S]), ALU.mult))
                    nc.vector.tensor_tensor(read[:, :, :, bass.ds(t, 1)].rearrange("p k s l -> p k (s l)"), faded[:, 0], faded[:, 1], ALU.add)
                    link(nc.vector.scalar_tensor_tensor(out=state2(states), in0=state2(faded)[:, ::-1, :], scalar=RA_MIX,
                                                        in1=state2(faded), op0=ALU.mult, op1=ALU.add))
                    link(nc.vector.tensor_tensor(states[:, :, 0, :], states[:, :, 0, :],
                                                 u[:, :, bass.ds(t, 1)].rearrange("p s l -> p (s l)").unsqueeze(1).to_broadcast([P, 2, S]),
                                                 ALU.add))
                link.close(L)
                ends = states[:].rearrange("p a k (b c) -> p a k b c", b=BATCH)
                at = starts[:, :, 0:S].rearrange("p k (b c) -> p k b c", b=BATCH)
                with dve.Fori(0, seg - 1) as c:
                    link = Steps(dve, chain, 4, c)
                    for a in range(2):
                        last = nc.vector.tensor_tensor(piece[:, a], ends[:, a, 1:3, :, bass.ds(c, 1)].rearrange("p k b c -> p k (b c)"),
                                                       at[:, :, :, bass.ds(c, 1)].rearrange("p k b c -> p k (b c)"), ALU.mult)
                        link(last)
                    link(nc.vector.tensor_tensor(piece[:, :, 0, :], piece[:, :, 0, :], piece[:, :, 1, :], ALU.add))
                    link(nc.vector.tensor_tensor(at[:, :, :, bass.ds(c + 1, 1)].rearrange("p k b c -> p k (b c)"), piece[:, :, 0, :],
                                                 ends[:, :, 0, :, bass.ds(c, 1)].rearrange("p a b c -> p a (b c)"), ALU.add))
                link.close(seg - 1)
                link = Steps(dve, chain)
                flat = lambda t: t.rearrange("p s l -> p (s l)")
                for a in range(2):
                    link(nc.vector.tensor_tensor(read[:, 1 + a], read[:, 1 + a], starts[:, a, 0:S].unsqueeze(2).to_broadcast([P, S, L]), ALU.mult))
                link(nc.vector.tensor_tensor(read[:, 0], read[:, 0], read[:, 1], ALU.add))
                link(nc.vector.tensor_tensor(read[:, 0], read[:, 0], read[:, 2], ALU.add))
                link(nc.vector.tensor_tensor(zt[:, 0:TOKENS], flat(read[:, 0]), q[:], ALU.mult))
                link.close()
        tokens_product(core, w("wo"), add_to_x(core))


def fetch(core, area, source):
    ready = core.sem(f"weights_{'ab'[area]}_arrived")
    with core.nc.Block() as block:
        @block.sync
        def _(sp):
            sp.dma_start(core.areas[area][:, 0:source.shape[1]], source).then_inc(ready.handle, 16)
    ready.done += 16


def arrived(core, area):
    ready = core.sem(f"weights_{'ab'[area]}_arrived")
    with core.nc.Block() as block:
        @block.sync
        def _(sp):
            sp.wait_ge(ready.handle, ready.done)


STAGES = [("L0_ffn", l0_ffn, 0), ("L0_attn", l0_attn, 1), ("L0_ffn", l0_ffn, 0),
          ("L1_ffn", ternary_ffn, 1), ("L1_attn", l1_attn, 0), ("L1_ffn", ternary_ffn, 1),
          ("L2_ffn", l2_ffn, 0), ("L2_attn", l2_attn, 1), ("L2_ffn", l2_ffn, 0),
          ("L3_ffn", ternary_ffn, 1), ("L3_attn", l3_attn, 0), ("L3_ffn", ternary_ffn, 1)]


def macaron_d4(nc, x_in, blobs, out, stages=STAGES):
    with ExitStack() as ctx:
        core = Core(nc, ctx)
        loaded = core.sem("inputs_arrived")
        stored = core.sem("output_stored")
        half = core.sem("constants_set")
        with nc.Block() as block:
            @block.sync
            def _(sp):
                sp.dma_start(core.x[:], x_in.rearrange("b (i p) d -> p (b i) d", p=P)).then_inc(loaded.handle, 16)
                sp.dma_start(core.ident[:], blobs["constants"]).then_inc(loaded.handle, 16)
                sp.wait_ge(loaded.handle, 32)

            @block.gpsimd
            def _(pool):
                pool.dma_start(core.masks[:], blobs["masks"]).then_inc(core.sem("masks_arrived").handle, 16)
                nc.gpsimd.memset(core.minus_half[:], -0.5).then_inc(half.handle, 1)
                nc.gpsimd.memset(core.zt[:], 0.0).then_inc(half.handle, 1)
                pool.wait_ge(core.sem("masks_arrived").handle, 16)
        held = [None, None]

        def fetch_for(n):
            name, _, area = stages[n]
            if held[area] != name:
                fetch(core, area, blobs[name])
                held[area] = name
        fetch_for(0)
        for n, (_, stage, area) in enumerate(stages):
            if n + 1 < len(stages) and stages[n + 1][2] != area:
                fetch_for(n + 1)
            arrived(core, area)
            stage(core, area)
            if n + 1 < len(stages) and stages[n + 1][2] == area:
                fetch_for(n + 1)
        with nc.Block() as block:
            @block.sync
            def _(sp):
                sp.dma_start(out.rearrange("b (i p) d -> p (b i) d", p=P), core.x[:]).then_inc(stored.handle, 16)
                sp.wait_ge(stored.handle, 16)


def _pack(layout, arrays):
    import numpy as np
    cols = []
    for name, n in layout:
        a = arrays[name]
        a = a.reshape(a.shape[0], -1)
        assert a.shape[1] == n, (name, a.shape, n)
        if a.shape[0] < 128:
            a = np.concatenate([a, np.zeros((128 - a.shape[0], n), a.dtype)])
        cols.append(a)
    return np.ascontiguousarray(np.concatenate(cols, axis=1))


def _rows(w, part=128):
    import numpy as np
    n = -(-w.shape[0] // part)
    w = np.concatenate([w, np.zeros((n * part - w.shape[0], w.shape[1]), w.dtype)])
    return w.reshape(n, part, w.shape[1]).transpose(1, 0, 2).reshape(part, -1)


def _all_rows(v):
    import numpy as np
    return np.broadcast_to(v[None, :], (128, v.shape[0]))


def _tables():
    import numpy as np
    f = np.float32
    out = {}
    t = np.arange(1024, dtype=f)
    hi = np.arange(0, 64, 2, dtype=f)
    inv = (f(1.0) / f(10000.0) ** (hi / f(64))).astype(f)
    fr = (t[:, None] * inv[None, :]).astype(f)
    fr = np.concatenate([fr, fr], -1)
    base = ((hi + f(0.4 * 64)) / f(1.4 * 64)).astype(f)
    power = ((t - 512) / f(32)).astype(f)
    scale = (base[None, :] ** power[:, None]).astype(f)
    scale = np.concatenate([scale, scale], -1)
    cos, sin = np.cos(fr), np.sin(fr)
    sign = np.concatenate([-np.ones(32, f), np.ones(32, f)])
    tok = lambda a: a.astype(f).reshape(8, 128, 64).transpose(1, 0, 2).reshape(128, -1)
    out["xpos"] = {"cq": tok(cos * scale), "sq": tok(sin * scale * sign), "ck": tok(cos / scale), "sk": tok(sin / scale * sign)}
    inv = (f(1.0) / f(10000.0) ** (np.arange(8, dtype=f) / f(8))).astype(f)
    fr = (t[:, None] * inv[None, :]).astype(f)
    c = np.zeros((4, 32, 1024), f)
    s = np.zeros((4, 32, 1024), f)
    c[:, :8] = c[:, 8:16] = np.cos(fr).T
    s[:, :8], s[:, 8:16] = -np.sin(fr).T, np.sin(fr).T
    out["ga"] = (c.reshape(128, 1024), s.reshape(128, 1024))
    inv = (f(1.0) / f(10000.0) ** (np.arange(0, 8, 2, dtype=f) / f(8))).astype(f)
    fr = (t[:, None] * inv[None, :]).astype(f)
    c8 = np.repeat(np.cos(fr), 2, -1).T
    s8 = np.repeat(np.sin(fr), 2, -1).T * np.array([-1] * 4 + [1] * 4, f)[:, None]
    out["fa"] = (np.tile(c8, (16, 1)).astype(f), np.tile(s8, (16, 1)).astype(f))
    off = f(-1e30)
    q, k = np.arange(64)[:, None], np.arange(128)[None, :]
    local = np.where((k >= q) & (k <= q + 64), f(0), off).astype(f)
    first = np.where(k < 64, off, local).astype(f)
    masks = np.zeros((128, 16, 128), f)
    for i in range(16):
        masks[:64, i] = first if i % 8 == 0 else local
        masks[64:, i] = local
    j, i = np.arange(128)[:, None], np.arange(128)[None, :]
    causal = np.where(j <= i, f(0), off).astype(f)
    q, k = np.arange(128)[:, None], np.arange(160)[None, :] - 32
    band_q = np.where((k <= q) & (k >= q - 32), f(0), off).astype(f)
    band_q0 = np.where((k <= q) & (k >= q - 32) & (k >= 0), f(0), off).astype(f)
    k, q = np.arange(128)[:, None], np.arange(160)[None, :]
    band_qs = np.concatenate([band_q0] + [band_q] * 7, 1)
    band_k = np.where((k <= q) & (k >= q - 32), f(0), off).astype(f)
    out["masks"] = {"ident": np.eye(128, dtype=f), "local": masks.reshape(128, -1), "causal": causal,
                    "band_q": band_qs, "band_k": band_k}
    out["upper"] = (j <= i).astype(f)
    d = (np.arange(128)[:, None] // 32 == np.arange(64)[None, :] // 16).astype(f)
    out["diag"] = np.concatenate([d, d], 1)
    return out


def _blobs(a):
    import numpy as np
    tb = _tables()
    parts = {}
    r = {}
    for l in range(2):
        w1, w2, b1 = a["L0_ffn_w1"][l], a["L0_ffn_w2"][l], a["L0_ffn_b1"][l]
        col = lambda b: _rows(b[:, None])
        qs, ks = a["L0_ffn_q_scale"][l], a["L0_ffn_k_scale"][l]
        r.update({f"wqkv{l}": a["L0_ffn_wqkv"][l], f"wo{l}": _rows(a["L0_ffn_wo"][l]), f"w1{l}": w1, f"w2{l}": _rows(w2),
                  f"qs{l}": _all_rows(qs), f"ks{l}": _all_rows(ks), f"lg{l}": a["L0_ffn_ln_g"][l][:, None],
                  f"lb{l}": a["L0_ffn_ln_b"][l][:, None], f"b1a{l}": col(b1[:341]), f"b1g{l}": col(b1[341:]),
                  f"b2{l}": _all_rows(a["L0_ffn_b2"][l])})
    r.update(tb["xpos"])
    parts["L0_ffn"] = r

    def spaced(w, swap=False):
        w = w.reshape(8, 16, 128)
        if swap:
            w = np.concatenate([w[:, 8:], w[:, :8]], 1)
        w = np.concatenate([w, np.zeros_like(w)], 1).reshape(256, 128)
        return w.T
    A = "L0_attn_"
    parts["L0_attn"] = {"wq": spaced(a[A + "Wq"]), "wqs": spaced(a[A + "Wq"], True), "wk": spaced(a[A + "Wk"]),
                        "wks": spaced(a[A + "Wk"], True),
                        "wvg": np.concatenate([a[A + "Wv"], a[A + "Wbeta"], a[A + "Wig"], a[A + "Wog"]]).T,
                        "wout": a[A + "Wout"].T, "bg": _all_rows(np.concatenate([a[A + "bbeta"], a[A + "big"], a[A + "bog"]])),
                        "bout": _all_rows(a[A + "bout"]), "nw": a[A + "norm_w"][:, None],
                        "cos": tb["ga"][0], "sin": tb["ga"][1], "upper": tb["upper"], "diag": tb["diag"]}
    for L in ("L1_ffn", "L3_ffn"):
        g = lambda n: a[f"{L}_{n}"]
        col = lambda v: _rows(v[:, None])
        parts[L] = {"w1": g("w1_w").T, "w2": g("w2_w").T, "h1": _rows(g("h1_w").T), "h2": _rows(g("h2_w").T),
                    "w3": _rows(g("w3_w").T), "s1": col(g("w1_s")), "s2": col(g("w2_s")), "t1": col(g("h1_s")),
                    "t2": col(g("h2_s")), "s3": _all_rows(g("w3_s"))}
    swap8 = lambda w: w.reshape(16, 2, 4, -1)[:, ::-1].reshape(128, -1)
    A = "L1_attn_"
    parts["L1_attn"] = {"wq": a[A + "wq"].T, "wqs": swap8(a[A + "wq"]).T, "wk": a[A + "wk"].T, "wks": swap8(a[A + "wk"]).T,
                        "wv": a[A + "wv"].T, "wo": a[A + "wo"].T, "bq": a[A + "bq"][:, None], "bqs": swap8(a[A + "bq"]),
                        "bk": a[A + "bk"][:, None], "bks": swap8(a[A + "bk"]), "bv": _all_rows(a[A + "bv"]),
                        "bo": _all_rows(a[A + "bo"]), "cos": tb["fa"][0], "sin": tb["fa"][1]}
    parts["L2_ffn"] = {"wg": _rows(a["L2_ffn_w_gate"]), "wu": _rows(a["L2_ffn_w_up"]), "wd": a["L2_ffn_w_down"]}
    W = a["L2_attn_W_qkv"]
    parts["L2_attn"] = {"wq": W[:128].T, "wk": W[128:256].T, "wv": W[256:].T, "wout": a["L2_attn_W_out"].T,
                        "gamma": a["L2_attn_gamma"][:, None], "beta": a["L2_attn_beta"][:, None]}
    A = "L3_attn_"
    rep = lambda w: np.repeat(w, 8, axis=0)
    parts["L3_attn"] = {"wq": a[A + "Wq"].T, "wk": a[A + "Wk"].T, "wv": a[A + "Wv"].T, "wg": a[A + "Wg"].T,
                        "wb": rep(a[A + "Wb"]).T, "wfd": rep(a[A + "Wfd"]).T, "wsd": rep(a[A + "Wsd"]).T,
                        "wo": a[A + "Wo"].T, "bfd": rep(a[A + "bfd"])[:, None], "bsd": rep(a[A + "bsd"])[:, None]}
    blobs = {name: _pack(LAYOUTS[name], parts[name]) for name in LAYOUTS}
    blobs["constants"] = np.eye(128, dtype=np.float32)
    blobs["masks"] = _pack(MASKS, tb["masks"])
    return blobs


def kernel(**inputs):
    import numpy as _np
    import concourse.bacc as _bacc
    from concourse import mybir as _mybir
    from concourse.bass_utils import run_bass_kernel_spmd as _run

    nc = _bacc.Bacc("TRN2", target_bir_lowering=False, num_devices=1)
    given = {k: _np.asarray(v) for k, v in inputs.items()}
    arrays = {"in_x": _np.ascontiguousarray(given["L0_attn_x"])}
    arrays.update({f"in_{k}": v for k, v in _blobs(given).items()})
    args = {k: nc.dram_tensor(k, v.shape, _mybir.dt.from_np(v.dtype), kind="ExternalInput").ap() for k, v in arrays.items()}
    out = nc.dram_tensor("out_x", (BATCH, SEQ, P), F32, kind="ExternalOutput").ap()
    macaron_d4(nc, args["in_x"], {k[3:]: v for k, v in args.items()}, out)
    r = _run(nc, [arrays], core_ids=[0])
    return r.results[0]["out_x"]
```

```python
from contextlib import ExitStack

import concourse.bass as bass
from concourse import mybir

ALU = mybir.AluOpType
ACT = mybir.ActivationFunctionType
AX = mybir.AxisListType
F32 = mybir.dt.float32
BF16 = mybir.dt.bfloat16

P = 128
BATCH, SEQ = 2, 1024
TOKENS = BATCH * SEQ
TILES = TOKENS // P
SEQ_TILES = SEQ // P
CHUNK = 512
CHUNKS = TOKENS // CHUNK
PER_CHUNK = CHUNK // P
BANK = 512

LA_HEADS, LA_DIM, LA_WIN = 8, 64, 64
LA_INNER = LA_HEADS * LA_DIM
GLU_HID = 341
GLU_PARTS = [(m * P, min(P, GLU_HID - m * P)) for m in range(-(-GLU_HID // P))]
TF_HID = 512
TF_PARTS = TF_HID // P
GA_HEADS, GA_DIM = 8, 16
FA_HEADS, FA_DIM = 16, 8
WA_WIN = 32
BAND = P + WA_WIN
Q4_HID, Q4_BLOCK = 352, 16
Q4_PARTS = [(m * P, min(P, Q4_HID - m * P)) for m in range(-(-Q4_HID // P))]
RA_HEADS, RA_DIM, RA_MIX = 16, 8, 0.05
RA_STEP = 32
RA_SEG = TOKENS // RA_STEP

L0_FFN = []
for _l in range(2):
    L0_FFN += [(f"wqkv{_l}", 3 * LA_INNER), (f"wo{_l}", LA_INNER), (f"w1{_l}", 2 * GLU_HID),
               (f"w2{_l}", len(GLU_PARTS) * P), (f"qs{_l}", LA_DIM), (f"ks{_l}", LA_DIM),
               (f"lg{_l}", 1), (f"lb{_l}", 1), (f"b1a{_l}", len(GLU_PARTS)), (f"b1g{_l}", len(GLU_PARTS)),
               (f"b2{_l}", P)]
L0_FFN += [("cq", SEQ_TILES * LA_DIM), ("ck", SEQ_TILES * LA_DIM),
           ("sq", SEQ_TILES * LA_DIM), ("sk", SEQ_TILES * LA_DIM)]
L0_ATTN = [("wq", 256), ("wqs", 256), ("wk", 256), ("wks", 256), ("wvg", P + 3 * GA_HEADS),
           ("wout", P), ("bg", 3 * GA_HEADS), ("bout", P), ("nw", 1), ("cos", SEQ), ("sin", SEQ), ("upper", P),
           ("diag", 2 * 64)]
TERNARY = [("w1", TF_HID), ("w2", TF_HID), ("h1", TF_PARTS * TF_HID), ("h2", TF_PARTS * TF_HID),
           ("w3", TF_PARTS * P), ("s1", TF_PARTS), ("s2", TF_PARTS), ("t1", TF_PARTS), ("t2", TF_PARTS), ("s3", P)]
L1_ATTN = [("wq", P), ("wqs", P), ("wk", P), ("wks", P), ("wv", P), ("wo", P), ("bq", 1), ("bqs", 1),
           ("bk", 1), ("bks", 1), ("bv", P), ("bo", P), ("cos", SEQ), ("sin", SEQ)]
L2_FFN = [("wg", 3 * P), ("wu", 3 * P), ("wd", Q4_HID)]
L2_ATTN = [("wq", P), ("wk", P), ("wv", P), ("wout", P), ("gamma", 1), ("beta", 1)]
L3_ATTN = [("wq", P), ("wk", P), ("wv", P), ("wg", P), ("wb", P), ("wfd", P), ("wsd", P), ("wo", P),
           ("bfd", 1), ("bsd", 1)]
CONSTANTS = [("ident", P)]
MASKS = [("ident", P), ("local", TILES * P), ("causal", P), ("band_q", SEQ_TILES * BAND), ("band_k", BAND)]
L2_FFN_HELD = sum(n for _, n in L2_FFN) + 2 * Q4_HID + len(Q4_PARTS) * P
AREA_A = sum(n for _, n in L0_FFN)
AREA_B = sum(n for _, n in TERNARY)
LAYOUTS = {"L0_ffn": L0_FFN, "L0_attn": L0_ATTN, "L1_ffn": TERNARY, "L1_attn": L1_ATTN, "L2_ffn": L2_FFN,
           "L2_attn": L2_ATTN, "L3_ffn": TERNARY, "L3_attn": L3_ATTN}


def columns(layout):
    at, out = 0, {}
    for name, n in layout:
        out[name] = (at, n)
        at += n
    return out


class Tally:

    def __init__(self, handle):
        self.handle, self.done = handle, 0


class Steps:

    def __init__(self, engine, tally, per_turn=0, turn=None):
        self.engine, self.tally, self.per_turn, self.made = engine, tally, per_turn, 0
        self.start = tally.done if turn is None else tally.done + turn * per_turn

    def __call__(self, instruction):
        self.made += 1
        instruction.then_inc(self.tally.handle, 1)
        self.engine.wait_ge(self.tally.handle, self.start + self.made)

    def close(self, turns=1):
        assert not self.per_turn or self.made == self.per_turn, self.made
        self.tally.done += self.made * turns


class Core:

    def __init__(self, nc, ctx):
        self.nc, self.ctx, self.tallies, self.made = nc, ctx, {}, 0
        self.weights_quantised = False
        sb = lambda name, shape, dt=F32: ctx.enter_context(nc.sbuf_tensor(name, shape, dt))
        self.x = sb("x", [P, TILES, P])
        self.y = sb("y", [P, TILES, P])
        self.zt = sb("zt", [P, 64 + TOKENS + 64])
        self.ident = sb("ident", [P, P])
        self.masks = sb("masks", [P, sum(n for _, n in MASKS)], BF16)
        self.stats = sb("stats", [P, TILES, 6])
        self.moments = sb("moments", [P, TILES, 2])
        self.spread = sb("spread", [P, TILES])
        self.rstd = sb("rstd", [P, TILES])
        self.minus_half = sb("minus_half", [P, TILES])
        self.areas = [sb("area_a", [P, AREA_A]), sb("area_b", [P, AREA_B])]
        self.psum = ctx.enter_context(nc.psum_tensor("psum", [P, 8, BANK], F32))
        self.mask_at = columns(MASKS)

    def sem(self, name):
        if name not in self.tallies:
            self.tallies[name] = Tally(self.ctx.enter_context(self.nc.semaphore(name)))
        return self.tallies[name]

    def fresh(self, name):
        self.made += 1
        return f"{name}_{self.made}"

    def mask(self, name):
        at, n = self.mask_at[name]
        return self.masks[:, at:at + n]

    def weights(self, area, layout):
        where = columns(layout)
        return lambda name: self.areas[area][:, where[name][0]:where[name][0] + where[name][1]]


def need(engine, tally, n):
    engine.wait_ge(tally.handle, tally.done + n)



def normalise_block(core, source, out, eps, evacuate=None, rms=False, only_transpose=False):
    nc, psum = core.nc, core.psum
    HALF = TILES // 2
    chain, spread_ready, done_pow, normed, turned, taken = (core.sem(n) for n in (
        "vector_chain", "spread_ready", "rstd_ready", "tile_normalised", "bank_transposed", "bank_evacuated"))
    scalar_chain = core.sem("scalar_chain")
    with nc.Block() as block:
        if not only_transpose:
            @block.vector
            def _(dve):
                link = Steps(dve, chain)
                for h in range(2):
                    tiles = range(h * HALF, (h + 1) * HALF)
                    half = slice(h * HALF, (h + 1) * HALF)
                    for i in tiles:
                        last = nc.vector.bn_stats(core.stats[:, i, :], source[:, i, :])
                    link(last)
                    for i in tiles:
                        last = nc.vector.bn_aggr(core.moments[:, i, :], core.stats[:, i, :])
                    link(last)
                    if rms:
                        link(nc.vector.tensor_tensor(core.spread[:, half], core.moments[:, half, 0], core.moments[:, half, 0], ALU.mult))
                        link(nc.vector.tensor_tensor(core.spread[:, half], core.spread[:, half], core.moments[:, half, 1], ALU.add))
                        last = nc.vector.tensor_scalar(core.spread[:, half], core.spread[:, half], eps, None, ALU.add)
                    else:
                        last = nc.vector.tensor_scalar(core.spread[:, half], core.moments[:, half, 1], eps, None, ALU.add)
                    last.then_inc(spread_ready.handle, 1)
                link.close()
                for h in range(2):
                    need(dve, done_pow, h + 1)
                    for i in range(h * HALF, (h + 1) * HALF):
                        if rms:
                            nc.vector.tensor_scalar(out[:, i, :], source[:, i, :], core.rstd[:, i:i + 1], None,
                                                    ALU.mult).then_inc(normed.handle, 1)
                        else:
                            nc.vector.tensor_scalar(out[:, i, :], source[:, i, :], core.moments[:, i, 0:1],
                                                    core.rstd[:, i:i + 1], ALU.subtract, ALU.mult).then_inc(normed.handle, 1)

            @block.gpsimd
            def _(pool):
                for h in range(2):
                    half = slice(h * HALF, (h + 1) * HALF)
                    need(pool, spread_ready, h + 1)
                    nc.gpsimd.tensor_tensor(core.rstd[:, half], core.spread[:, half], core.minus_half[:, half],
                                            ALU.pow).then_inc(done_pow.handle, 1)

        if evacuate is None:
            @block.sync
            def _(sp):
                need(sp, normed, TILES)

        @block.tensor
        def _(pe):
            if evacuate is None:
                return
            for g in range(CHUNKS):
                if g >= 2:
                    need(pe, taken, g - 1)
                for j in range(PER_CHUNK):
                    if not only_transpose:
                        need(pe, normed, PER_CHUNK * g + j + 1)
                    last = nc.tensor.transpose(psum[:, g % 2, j * P:(j + 1) * P], out[:, PER_CHUNK * g + j, :], core.ident[:])
                last.then_inc(turned.handle, 1)

        @block.scalar
        def _(act):
            if evacuate is None:
                return
            for g in range(CHUNKS):
                need(act, turned, g + 1)
                for ins in evacuate(g, psum[:, g % 2, :]):
                    last = ins
                last.then_inc(taken.handle, 1)
    if not only_transpose:
        spread_ready.done += 2
        done_pow.done += 2
        normed.done += TILES
    if evacuate is not None:
        turned.done += CHUNKS
        taken.done += CHUNKS


def tokens_product(core, weights, take, offset=0):
    nc, psum, zt = core.nc, core.psum, core.zt
    made, taken, chain = core.sem("tokens_product"), core.sem("tokens_product_taken"), core.sem("vector_chain")
    width = weights.shape[1]
    per = BANK // width if BANK % width == 0 else 2
    banks = -(-PER_CHUNK // per)
    with nc.Block() as block:
        @block.tensor
        def _(pe):
            for g in range(CHUNKS):
                if g >= 2:
                    need(pe, taken, g - 1)
                for j in range(PER_CHUNK):
                    at = offset + (g * PER_CHUNK + j) * P
                    last = nc.tensor.matmul(psum[:, g % 2 * banks + j // per, j % per * width:(j % per + 1) * width],
                                            zt[:, at:at + P], weights, start=True, stop=True)
                last.then_inc(made.handle, 1)

        @block.vector
        def _(dve):
            link = Steps(dve, chain)
            for g in range(CHUNKS):
                need(dve, made, g + 1)
                got = psum[:, g % 2 * banks:(g % 2 + 1) * banks, 0:min(per, PER_CHUNK) * width].rearrange("p b (j n) -> p (b j) n", n=width) \
                    if per * width == BANK else psum[:, g % 2 * banks:(g % 2 + 1) * banks, 0:per * width].rearrange("p b (j n) -> p b j n", n=width)
                take(g, got, link).then_inc(taken.handle, 1)
            link.close()
    made.done += CHUNKS
    taken.done += CHUNKS


def add_to_x(core, bias=None, also=None):
    nc, x = core.nc, core.x

    def take(g, got, link):
        tiles = slice(g * PER_CHUNK, (g + 1) * PER_CHUNK)
        if bias is not None:
            link(nc.vector.tensor_tensor(x[:, tiles, :], x[:, tiles, :], bias.unsqueeze(1).to_broadcast([P, PER_CHUNK, P]), ALU.add))
        if also is not None:
            link(nc.vector.tensor_tensor(x[:, tiles, :], x[:, tiles, :], also[:, tiles, :], ALU.add))
        return nc.vector.tensor_tensor(x[:, tiles, :], got, x[:, tiles, :], ALU.add)
    return take


def rotated_product(core, pairs, cos, sin):
    nc, psum, zt = core.nc, core.psum, core.zt
    made, turned, chain = core.sem("rotary_product"), core.sem("rotary_taken"), core.sem("vector_chain")
    with ExitStack() as ctx:
        part_a = ctx.enter_context(nc.sbuf_tensor(core.fresh("rotary_a"), [P, 2, CHUNK], F32))
        part_b = ctx.enter_context(nc.sbuf_tensor(core.fresh("rotary_b"), [P, 2, CHUNK], F32))
        R = len(pairs)
        with nc.Block() as block:
            @block.tensor
            def _(pe):
                for n in range(CHUNKS * R):
                    _, wa, _, wb, _ = pairs[n % R]
                    if n >= 4:
                        need(pe, turned, n - 3)
                    at = n // R * CHUNK
                    for half, weights in enumerate((wa, wb)):
                        last = nc.tensor.matmul(psum[:, 2 * (n % 4) + half, :], weights, zt[:, at:at + CHUNK], start=True, stop=True)
                    last.then_inc(made.handle, 1)

            @block.vector
            def _(dve):
                link = Steps(dve, chain)
                for n in range(CHUNKS * R):
                    out, _, ba, _, bb = pairs[n % R]
                    need(dve, made, n + 1)
                    if n >= 2:
                        need(dve, turned, n - 1)
                    at = n // R * CHUNK % SEQ
                    for half, part, bias, table in ((0, part_a, ba, cos), (1, part_b, bb, sin)):
                        got = psum[:, 2 * (n % 4) + half, :]
                        if bias is None:
                            last = nc.vector.tensor_tensor(part[:, n % 2, :], got, table[:, at:at + CHUNK], ALU.mult)
                        else:
                            last = nc.vector.scalar_tensor_tensor(out=part[:, n % 2, :], in0=got, scalar=bias, in1=table[:, at:at + CHUNK],
                                                                  op0=ALU.add, op1=ALU.mult)
                    link(last)
                    at = n // R * CHUNK
                    nc.vector.tensor_tensor(out[:, at:at + CHUNK], part_a[:, n % 2, :], part_b[:, n % 2, :],
                                            ALU.add).then_inc(turned.handle, 1)
                link.close()
        made.done += R * CHUNKS
        turned.done += R * CHUNKS


def plain(core):
    def evacuate(g, bank):
        yield core.nc.scalar.copy(core.zt[:, g * CHUNK:(g + 1) * CHUNK], bank)
    return evacuate


def affine(core, scale, bias):
    def evacuate(g, bank):
        yield core.nc.scalar.activation(core.zt[:, g * CHUNK:(g + 1) * CHUNK], bank, ACT.Identity, bias=bias, scale=scale)
    return evacuate


def ternary_ffn(core, area):
    nc, psum, x, zt = core.nc, core.psum, core.x, core.zt
    w = core.weights(area, TERNARY)
    normalise_block(core, x, core.y, 1e-5, plain(core))
    up, silu, gated, hid, acted, low, added = (core.sem(n) for n in (
        "tf_up_product", "tf_silu", "tf_gated", "tf_hidden_product", "tf_gelu", "tf_out_product", "tf_added"))
    chain = core.sem("vector_chain")
    M = TF_PARTS
    with ExitStack() as ctx:
        sb = lambda name, shape: ctx.enter_context(nc.sbuf_tensor(core.fresh(name), shape, F32))
        ha, hb = sb("hidden_a", [P, 2, M, CHUNK]), sb("hidden_b", [P, 2, M, CHUNK])
        gate, scaled = sb("gate", [P, 2, CHUNK]), sb("scaled", [P, PER_CHUNK, P])
        with nc.Block() as block:
            @block.tensor
            def _(pe):
                with pe.Fori(0, CHUNKS // 2) as i:
                    for c in range(2):
                        for m in range(M):
                            n = c * M + m
                            if n >= 2:
                                pe.wait_ge(gated.handle, gated.done + i * 2 * M + n - 1)
                            tokens = zt[:, bass.ds(i * 2 * CHUNK + c * CHUNK, CHUNK)]
                            nc.tensor.matmul(psum[:, n % 2, :], w("w1")[:, m * P:(m + 1) * P], tokens, start=True, stop=True)
                            nc.tensor.matmul(psum[:, 2 + n % 2, :], w("w2")[:, m * P:(m + 1) * P], tokens,
                                             start=True, stop=True).then_inc(up.handle, 1)
                    for step, (name, src) in enumerate((("h1", ha), ("h2", hb))):
                        for c in range(2):
                            if step == 0:
                                pe.wait_ge(gated.handle, gated.done + i * 2 * M + (c + 1) * M)
                            else:
                                pe.wait_ge(acted.handle, acted.done + i * 4 * M + (c + 1) * M)
                            for m in range(M):
                                n = step * 2 * M + c * M + m
                                if n >= 2:
                                    pe.wait_ge(acted.handle, acted.done + i * 4 * M + n - 1)
                                for k in range(M):
                                    last = nc.tensor.matmul(psum[:, 4 + n % 2, :], w(name)[:, k * TF_HID + m * P:k * TF_HID + (m + 1) * P],
                                                            src[:, c, k, :], start=(k == 0), stop=(k == M - 1))
                                last.then_inc(hid.handle, 1)
                    for c in range(2):
                        pe.wait_ge(acted.handle, acted.done + i * 4 * M + (2 + c + 1) * M)
                        for j in range(PER_CHUNK):
                            for k in range(M):
                                last = nc.tensor.matmul(psum[:, 6 + c, j * P:(j + 1) * P], ha[:, c, k, j * P:(j + 1) * P],
                                                        w("w3")[:, k * P:(k + 1) * P], start=(k == 0), stop=(k == M - 1))
                        last.then_inc(low.handle, 1)
                    pe.wait_ge(added.handle, added.done + (i + 1) * 2)

            @block.scalar
            def _(act):
                with act.Fori(0, CHUNKS // 2) as i:
                    for n in range(2 * M):
                        act.wait_ge(up.handle, up.done + i * 2 * M + n + 1)
                        if n >= 2:
                            act.wait_ge(gated.handle, gated.done + i * 2 * M + n - 1)
                        nc.scalar.activation(gate[:, n % 2, :], psum[:, n % 2, :], ACT.Silu,
                                             scale=w("s1")[:, n % M:n % M + 1]).then_inc(silu.handle, 1)
                    for step, (dst, scale) in enumerate(((hb, "t1"), (ha, "t2"))):
                        for c in range(2):
                            for m in range(M):
                                n = step * 2 * M + c * M + m
                                act.wait_ge(hid.handle, hid.done + i * 4 * M + n + 1)
                                nc.scalar.activation(dst[:, c, m, :], psum[:, 4 + n % 2, :], ACT.Gelu,
                                                     scale=w(scale)[:, m:m + 1]).then_inc(acted.handle, 1)

            @block.vector
            def _(dve):
                with dve.Fori(0, CHUNKS // 2) as i:
                    link = Steps(dve, chain, 2, i)
                    for n in range(2 * M):
                        dve.wait_ge(silu.handle, silu.done + i * 2 * M + n + 1)
                        nc.vector.scalar_tensor_tensor(out=ha[:, n // M, n % M, :], in0=psum[:, 2 + n % 2, :],
                                                       scalar=w("s2")[:, n % M:n % M + 1], in1=gate[:, n % 2, :],
                                                       op0=ALU.mult, op1=ALU.mult).then_inc(gated.handle, 1)
                    for c in range(2):
                        dve.wait_ge(low.handle, low.done + i * 2 + c + 1)
                        link(nc.vector.tensor_tensor(scaled[:], psum[:, 6 + c, :].rearrange("p (j n) -> p j n", j=PER_CHUNK),
                                                     w("s3").unsqueeze(1).to_broadcast([P, PER_CHUNK, P]), ALU.mult))
                        tiles = x[:, bass.ds(i * 2 * PER_CHUNK + c * PER_CHUNK, PER_CHUNK), :]
                        nc.vector.scalar_tensor_tensor(out=tiles, in0=scaled[:], scalar=0.5, in1=tiles,
                                                       op0=ALU.mult, op1=ALU.add).then_inc(added.handle, 1)
                        dve.wait_ge(added.handle, added.done + i * 2 + c + 1)
                link.close(CHUNKS // 2)
        turns = CHUNKS // 2
        for tally, n in ((up, 2 * M), (silu, 2 * M), (gated, 2 * M), (hid, 4 * M), (acted, 4 * M), (low, 2), (added, 2)):
            tally.done += n * turns



def shifted(core):
    half, zt = P // 2, core.zt

    def evacuate(g, bank):
        at = 64 + g * CHUNK
        n = CHUNK - 1 if (g + 1) * CHUNK % SEQ == 0 else CHUNK
        yield core.nc.scalar.copy(zt[0:half, at:at + CHUNK], bank[0:half, :])
        yield core.nc.scalar.copy(zt[half:P, at + 1:at + 1 + n], bank[half:P, 0:n])
    return evacuate


def first_tokens(core):
    cleared = core.sem("first_token_cleared")
    with core.nc.Block() as block:
        @block.gpsimd
        def _(pool):
            for b in range(BATCH):
                core.nc.gpsimd.memset(core.zt[P // 2:P, 64 + b * SEQ:65 + b * SEQ], 0.0).then_inc(cleared.handle, 1)
    cleared.done += BATCH


def local_attention(core, w, layer):
    nc, psum, y, zt = core.nc, core.psum, core.y, core.zt
    H, D, W = LA_HEADS, LA_DIM, LA_WIN
    names = ("la_tokens_staged", "la_qk_product", "la_v_product", "la_squared", "la_square_sums", "la_norms", "la_rotated",
             "la_qk_turned", "la_q_evacuated", "la_scores", "la_shifted_scores", "la_probs", "la_probs_turned",
             "la_probs_evacuated", "la_v_evacuated", "la_values", "la_values_normed", "la_values_turned",
             "la_values_evacuated", "la_out_product", "la_added", "la_tables")
    (staged, qk_ready, v_ready, squared, sums, norms, rotated, qk_turned, q_taken, scores, shifted_s, probs, p_turned,
     p_taken, v_taken, values, o_normed, o_turned, o_taken, out_ready, added, tables) = (core.sem(n) for n in names)
    chain, chain_act = core.sem("vector_chain"), core.sem("scalar_chain")
    wq = w(f"wqkv{layer}")
    wo = w(f"wo{layer}").rearrange("p (k n) -> p k n", k=LA_INNER // P)
    with ExitStack() as ctx:
        sb = lambda name, shape, dt=F32: ctx.enter_context(nc.sbuf_tensor(core.fresh(name), shape, dt))
        direct = sb("direct", [P, 2, TILES, D])
        cross = sb("cross", [P, 2, TILES, D])
        window = sb("window", [P, W + P])
        squares = sb("squares", [P, 2 * H, D])
        square_sum = sb("square_sum", [P, 2 * H])
        norm = sb("norm", [P, 2 * H])
        turn_a, turn_b = sb("turn_a", [P, 2 * H, D]), sb("turn_b", [P, 2 * H, D])
        qk = sb("qk", [P, 2 * H, D])
        q_t = sb("q_t", [P, H // 2, P])
        k_t = sb("k_t", [P, H // 2, W + P])
        v = sb("v", [P, 2, H, D + 1])
        top = sb("top", [P, H])
        shifted_scores, prob = sb("shifted_scores", [P, H, P]), sb("prob", [P, H, P])
        prob_t = sb("prob_t", [P, H, P])
        rec = sb("rec", [P, H])
        o = sb("o", [P, H, D])
        o_t = sb("o_t", [P, LA_INNER // P, P])
        score_banks, qk_banks, v_banks, turn_banks = psum[:, 0:2, :], psum[:, 2:4, :], psum[:, 4:6, :], psum[:, 6:8, :]

        def heads_of(banks):
            return banks.rearrange("p b (h n) -> p (b h) n", h=H // 2)

        with nc.Block() as block:
            @block.vector
            def _(dve):
                for s, (name, scale) in enumerate((("q", f"qs{layer}"), ("k", f"ks{layer}"))):
                    learned = w(scale).rearrange("p (a d) -> p a d", a=2)
                    for b in range(BATCH):
                        tiles = slice(b * SEQ_TILES, (b + 1) * SEQ_TILES)
                        nc.vector.tensor_tensor(direct[:, s, tiles, :], w("c" + name).rearrange("p (t d) -> p t d", d=D),
                                                w(scale).unsqueeze(1).to_broadcast([P, SEQ_TILES, D]),
                                                ALU.mult).then_inc(tables.handle, 1)
                        for a in range(2):
                            half = slice(a * D // 2, (a + 1) * D // 2)
                            nc.vector.tensor_tensor(cross[:, s, tiles, half],
                                                    w("s" + name).rearrange("p (t d) -> p t d", d=D)[:, :, half],
                                                    learned[:, 1 - a, :].unsqueeze(1).to_broadcast([P, SEQ_TILES, D // 2]),
                                                    ALU.mult).then_inc(tables.handle, 1)

            @block.gpsimd
            def _(pool):
                nc.gpsimd.memset(v[:], 1.0).then_inc(tables.handle, 1)
                nc.gpsimd.memset(k_t[:], 0.0).then_inc(tables.handle, 1)
        tables.done += 14

        def pool_first(pool, n, opening):
            if not opening:
                pool.wait_ge(v_ready.handle, v_ready.done + n)
            nc.gpsimd.tensor_copy(window[:], zt[:, bass.ds(n * P, W + P)]).then_inc(staged.handle, 1)
            pool.wait_ge(sums.handle, sums.done + n + 1)
            nc.gpsimd.tensor_tensor(norm[:], square_sum[:], core.minus_half[:], ALU.pow).then_inc(norms.handle, 1)

        def pe_project(pe, n, opening, then_scores=False):
            pe.wait_ge(staged.handle, staged.done + n + 1)
            if not opening:
                pe.wait_ge(rotated.handle, rotated.done + n)
                pe.wait_ge(v_taken.handle, v_taken.done + n)
            nc.tensor.matmul(qk_banks[:, 0, :], window[:, W:W + P], wq[:, 0:LA_INNER], start=True, stop=True)
            nc.tensor.matmul(qk_banks[:, 1, :], window[:, W:W + P], wq[:, LA_INNER:2 * LA_INNER],
                             start=True, stop=True).then_inc(qk_ready.handle, 1)
            for a in range(2):
                if a and then_scores:
                    pe.wait_ge(q_taken.handle, q_taken.done + n)
                last = nc.tensor.matmul(v_banks[:, a, :], window[:, a * W:a * W + P], wq[:, 2 * LA_INNER:], start=True, stop=True)
            last.then_inc(v_ready.handle, 1)

        def pe_turn_qk(pe, n, opening):
            pe.wait_ge(rotated.handle, rotated.done + n + 1)
            if not opening:
                pe.wait_ge(added.handle, added.done + n)
            for s in range(2):
                for k in range(H // 2):
                    last = nc.tensor.transpose(turn_banks[:, s, k * P:(k + 1) * P],
                                               qk[:, s * H + 2 * k:s * H + 2 * k + 2, :], core.ident[:])
            last.then_inc(qk_turned.handle, 1)

        def pe_scores(pe, n):
            for s in range(2):
                rows = slice(D * s, D * s + D)
                for h in range(H // 2):
                    for a in range(2):
                        nc.tensor.matmul(score_banks[a * W:(a + 1) * W, s, h * P:(h + 1) * P],
                                         q_t[rows, h, a * W:(a + 1) * W], k_t[rows, h, a * W:a * W + P],
                                         start=(h == 0), stop=False, skip_group_check=True)
            for s in range(2):
                last = nc.tensor.matmul(score_banks[:, s, :], core.mask("ident"),
                                        core.mask("local").rearrange("p (t k) -> p t k", k=P)[:, bass.ds(n, 1), :].to_broadcast([P, H // 2, P]),
                                        start=False, stop=True, skip_group_check=True)
            last.then_inc(scores.handle, 1)

        def pe_values(pe, n):
            pe.wait_ge(probs.handle, probs.done + n + 1)
            for h in range(H):
                last = nc.tensor.transpose(heads_of(turn_banks)[:, h, :], prob[:, h, :], core.ident[:])
            last.then_inc(p_turned.handle, 1)
            pe.wait_ge(p_taken.handle, p_taken.done + n + 1)
            for h in range(H):
                for a in range(2):
                    last = nc.tensor.matmul(score_banks[a * W:(a + 1) * W, h // 4, (h % 4) * (D + 1):(h % 4 + 1) * (D + 1)],
                                            prob_t[:, h, a * W:(a + 1) * W], v[:, a, 2 * (h % 4) + h // 4, :], start=True, stop=True,
                                            skip_group_check=True)
            last.then_inc(values.handle, 1)
            pe.wait_ge(o_normed.handle, o_normed.done + n + 1)
            for k in range(LA_INNER // P):
                last = nc.tensor.transpose(turn_banks[:, 0, k * P:(k + 1) * P], o[:, 2 * k:2 * k + 2, :], core.ident[:])
            last.then_inc(o_turned.handle, 1)
            pe.wait_ge(o_taken.handle, o_taken.done + n + 1)
            for k in range(LA_INNER // P):
                last = nc.tensor.matmul(turn_banks[:, 1, 0:P], o_t[:, k, :], wo[:, k, :], start=(k == 0), stop=(k == LA_INNER // P - 1))
            last.then_inc(out_ready.handle, 1)

        def act_square(act, n):
            act.wait_ge(qk_ready.handle, qk_ready.done + n + 1)
            nc.scalar.activation(squares[:], heads8(qk_banks), ACT.Square).then_inc(squared.handle, 1)

        def heads8(banks):
            return banks.rearrange("p b (h d) -> p (b h) d", d=D)

        def act_take_v(act, n):
            act.wait_ge(v_ready.handle, v_ready.done + n + 1)
            nc.scalar.copy(v[:, :, :, 0:D], v_banks.rearrange("p a (h d) -> p a h d", d=D)).then_inc(v_taken.handle, 1)

        def act_take_qk(act, n, turn):
            act.wait_ge(qk_turned.handle, qk_turned.done + n + 1)
            link = Steps(act, chain_act, 1, turn)
            link(nc.scalar.copy(k_t[:, :, 0:W], k_t[:, :, P:P + W]))
            nc.scalar.copy(q_t[:], turn_banks[:, 0, :].rearrange("p (k n) -> p k n", k=H // 2))
            nc.scalar.copy(k_t[:, :, W:W + P], turn_banks[:, 1, :].rearrange("p (k n) -> p k n", k=H // 2)).then_inc(q_taken.handle, 1)
            return link

        def act_second(act, n, take_next_v):
            act.wait_ge(shifted_s.handle, shifted_s.done + n + 1)
            nc.scalar.activation(prob[:], shifted_scores[:], ACT.Exp, scale=8.0).then_inc(probs.handle, 1)
            act.wait_ge(p_turned.handle, p_turned.done + n + 1)
            nc.scalar.copy(prob_t[:], heads_of(turn_banks)).then_inc(p_taken.handle, 1)
            act.wait_ge(values.handle, values.done + n + 1)
            if take_next_v:
                act_take_v(act, n + 1)
            act.wait_ge(o_turned.handle, o_turned.done + n + 1)
            nc.scalar.copy(o_t[:], turn_banks[:, 0, :].rearrange("p (k n) -> p k n", k=LA_INNER // P)).then_inc(o_taken.handle, 1)

        FIRST, SECOND = 3, 2

        def dve_first(dve, n, link):
            dve.wait_ge(squared.handle, squared.done + n + 1)
            link(nc.vector.tensor_reduce(square_sum[:], squares[:], AX.X, ALU.add))
            nc.vector.tensor_scalar(square_sum[:], square_sum[:], 1e-24, None, ALU.max).then_inc(sums.handle, 1)
            nc.vector.tensor_tensor(turn_a[:].rearrange("p (s h) d -> p s h d", s=2), qk_banks.rearrange("p s (h d) -> p s h d", d=D),
                                    direct[:, :, bass.ds(n, 1), :].to_broadcast([P, 2, H, D]), ALU.mult)
            for s in range(2):
                partner = qk_banks[:, s, :].rearrange("p (h a d) -> p h a d", h=H, a=2)[:, :, ::-1, :]
                last = nc.vector.tensor_tensor(turn_b[:, s * H:(s + 1) * H, :].rearrange("p h (a d) -> p h a d", a=2), partner,
                                               cross[:, s, bass.ds(n, 1), :].to_broadcast([P, H, D]).rearrange("p h (a d) -> p h a d", a=2),
                                               ALU.mult)
            link(last)
            link(nc.vector.tensor_tensor(turn_a[:], turn_a[:], turn_b[:], ALU.add))

        def dve_norm_qk(dve, n):
            dve.wait_ge(norms.handle, norms.done + n + 1)
            nc.vector.tensor_tensor(qk[:], turn_a[:], norm[:].unsqueeze(2).to_broadcast([P, 2 * H, D]), ALU.mult).then_inc(rotated.handle, 1)

        def dve_softmax(dve, n, link):
            dve.wait_ge(scores.handle, scores.done + n + 1)
            link(nc.vector.tensor_reduce(top[:], heads_of(score_banks), AX.X, ALU.max))
            nc.vector.tensor_tensor(shifted_scores[:], heads_of(score_banks), top[:].unsqueeze(2).to_broadcast([P, H, P]),
                                    ALU.subtract).then_inc(shifted_s.handle, 1)

        def dve_values(dve, n, link):
            dve.wait_ge(values.handle, values.done + n + 1)
            got = score_banks[:, :, 0:4 * (D + 1)].rearrange("p b (h e) -> p b h e", e=D + 1)
            link(nc.vector.reciprocal(rec[:].rearrange("p (b h) -> p b h", b=2), got[:, :, :, D]))
            nc.vector.tensor_tensor(o[:].rearrange("p (h b) d -> p b h d", b=2), got[:, :, :, 0:D],
                                    rec[:].rearrange("p (b h) -> p b h", b=2).unsqueeze(3).to_broadcast([P, 2, 4, D]),
                                    ALU.mult).then_inc(o_normed.handle, 1)

        def dve_add(dve, n):
            dve.wait_ge(out_ready.handle, out_ready.done + n + 1)
            tile = y[:, bass.ds(n, 1), :]
            nc.vector.tensor_tensor(tile, turn_banks[:, 1, 0:P].unsqueeze(1), tile, ALU.add).then_inc(added.handle, 1)

        with nc.Block() as block:
            @block.gpsimd
            def _(pool):
                pool_first(pool, 0, True)
                with pool.Fori(1, TILES) as n:
                    pool_first(pool, n, False)

            @block.tensor
            def _(pe):
                pe_project(pe, 0, True)
                pe_turn_qk(pe, 0, True)
                with pe.Fori(0, TILES - 1) as n:
                    pe_project(pe, n + 1, False, then_scores=True)
                    pe_scores(pe, n)
                    pe_values(pe, n)
                    pe_turn_qk(pe, n + 1, False)
                need(pe, q_taken, TILES)
                pe_scores(pe, TILES - 1)
                pe_values(pe, TILES - 1)

            @block.scalar
            def _(act):
                act_square(act, 0)
                act_take_v(act, 0)
                act_take_qk(act, 0, 0)
                with act.Fori(0, TILES - 1) as n:
                    act_square(act, n + 1)
                    act_second(act, n, True)
                    link = act_take_qk(act, n + 1, n + 1)
                act_second(act, TILES - 1, False)
                link.close(TILES)

            @block.vector
            def _(dve):
                link = Steps(dve, chain)
                dve_first(dve, 0, link)
                dve_norm_qk(dve, 0)
                link.close()
                with dve.Fori(0, TILES - 1) as n:
                    link = Steps(dve, chain, FIRST + SECOND, n)
                    dve_softmax(dve, n, link)
                    dve_first(dve, n + 1, link)
                    dve_values(dve, n, link)
                    dve_norm_qk(dve, n + 1)
                    dve_add(dve, n)
                link.close(TILES - 1)
                link = Steps(dve, chain)
                dve_softmax(dve, TILES - 1, link)
                dve_values(dve, TILES - 1, link)
                dve_add(dve, TILES - 1)
                link.close()
        for tally in (staged, qk_ready, v_ready, squared, sums, norms, rotated, qk_turned, q_taken, scores, shifted_s, probs,
                      p_turned, p_taken, v_taken, values, o_normed, o_turned, o_taken, out_ready, added):
            tally.done += TILES


def glu(core, w, layer):
    nc, psum, y, zt = core.nc, core.psum, core.y, core.zt
    up, act_done, gated, low, added = (core.sem(n) for n in ("glu_up_product", "glu_gelu", "glu_gated", "glu_out_product", "glu_added"))
    chain = core.sem("vector_chain")
    M = len(GLU_PARTS)
    w1, w2 = w(f"w1{layer}"), w(f"w2{layer}")
    with ExitStack() as ctx:
        sb = lambda name, shape: ctx.enter_context(nc.sbuf_tensor(core.fresh(name), shape, F32))
        hidden, gate, summed = sb("hidden", [P, 2, M, CHUNK]), sb("glu_gate", [P, 2, CHUNK]), sb("summed", [P, PER_CHUNK, P])
        with nc.Block() as block:
            @block.tensor
            def _(pe):
                with pe.Fori(0, CHUNKS // 2) as i:
                    for c in range(2):
                        for m, (at, rows) in enumerate(GLU_PARTS):
                            n = c * M + m
                            if n >= 2:
                                pe.wait_ge(gated.handle, gated.done + i * 2 * M + n - 1)
                            tokens = zt[:, bass.ds(i * 2 * CHUNK + c * CHUNK, CHUNK)]
                            nc.tensor.matmul(psum[0:rows, n % 2, :], w1[:, at:at + rows], tokens, start=True, stop=True)
                            nc.tensor.matmul(psum[0:rows, 2 + n % 2, :], w1[:, GLU_HID + at:GLU_HID + at + rows], tokens,
                                             start=True, stop=True).then_inc(up.handle, 1)
                    for c in range(2):
                        pe.wait_ge(gated.handle, gated.done + i * 2 * M + (c + 1) * M)
                        for j in range(PER_CHUNK):
                            for m, (at, rows) in enumerate(GLU_PARTS):
                                last = nc.tensor.matmul(psum[:, 4 + c, j * P:(j + 1) * P], hidden[0:rows, c, m, j * P:(j + 1) * P],
                                                        w2[0:rows, m * P:(m + 1) * P], start=(m == 0), stop=(m == M - 1))
                        last.then_inc(low.handle, 1)
                    pe.wait_ge(added.handle, added.done + (i + 1) * 2)

            @block.scalar
            def _(act):
                with act.Fori(0, CHUNKS // 2) as i:
                    for n in range(2 * M):
                        rows = GLU_PARTS[n % M][1]
                        act.wait_ge(up.handle, up.done + i * 2 * M + n + 1)
                        if n >= 2:
                            act.wait_ge(gated.handle, gated.done + i * 2 * M + n - 1)
                        nc.scalar.activation(gate[0:rows, n % 2, :], psum[0:rows, 2 + n % 2, :], ACT.Gelu,
                                             bias=w(f"b1g{layer}")[0:rows, n % M:n % M + 1]).then_inc(act_done.handle, 1)

            @block.vector
            def _(dve):
                with dve.Fori(0, CHUNKS // 2) as i:
                    link = Steps(dve, chain, 2, i)
                    for n in range(2 * M):
                        rows = GLU_PARTS[n % M][1]
                        dve.wait_ge(act_done.handle, act_done.done + i * 2 * M + n + 1)
                        nc.vector.scalar_tensor_tensor(out=hidden[0:rows, n // M, n % M, :], in0=psum[0:rows, n % 2, :],
                                                       scalar=w(f"b1a{layer}")[0:rows, n % M:n % M + 1], in1=gate[0:rows, n % 2, :],
                                                       op0=ALU.add, op1=ALU.mult).then_inc(gated.handle, 1)
                    for c in range(2):
                        dve.wait_ge(low.handle, low.done + i * 2 + c + 1)
                        link(nc.vector.tensor_tensor(summed[:], psum[:, 4 + c, :].rearrange("p (j n) -> p j n", j=PER_CHUNK),
                                                     w(f"b2{layer}").unsqueeze(1).to_broadcast([P, PER_CHUNK, P]), ALU.add))
                        tiles = y[:, bass.ds(i * 2 * PER_CHUNK + c * PER_CHUNK, PER_CHUNK), :]
                        nc.vector.tensor_tensor(tiles, summed[:], tiles, ALU.add).then_inc(added.handle, 1)
                        dve.wait_ge(added.handle, added.done + i * 2 + c + 1)
                link.close(CHUNKS // 2)
        turns = CHUNKS // 2
        for tally, n in ((up, 2 * M), (act_done, 2 * M), (gated, 2 * M), (low, 2), (added, 2)):
            tally.done += n * turns


def unshift(core, out):
    nc, psum = core.nc, core.psum
    turned, taken = core.sem("bank_transposed"), core.sem("bank_evacuated")
    with nc.Block() as block:
        @block.tensor
        def _(pe):
            for g in range(CHUNKS):
                if g >= 2:
                    need(pe, taken, g - 1)
                for j in range(PER_CHUNK):
                    at = 64 + g * CHUNK + j * P
                    last = nc.tensor.transpose(psum[:, g % 2, j * P:(j + 1) * P], core.zt[:, at:at + P], core.ident[:])
                last.then_inc(turned.handle, 1)

        @block.scalar
        def _(act):
            for g in range(CHUNKS):
                need(act, turned, g + 1)
                nc.scalar.copy(out[:, g * PER_CHUNK:(g + 1) * PER_CHUNK, :],
                               psum[:, g % 2, :].rearrange("p (j n) -> p j n", j=PER_CHUNK)).then_inc(taken.handle, 1)
    turned.done += CHUNKS
    taken.done += CHUNKS


def l0_ffn(core, area):
    nc, x, y = core.nc, core.x, core.y
    w = core.weights(area, L0_FFN)
    summed = core.sem("residual_added")
    for layer in range(2):
        first_tokens(core)
        normalise_block(core, x, y, 1e-5, shifted(core), only_transpose=(layer == 1))
        local_attention(core, w, layer)
        first_tokens(core)
        normalise_block(core, x, y, 1e-5, shifted(core), only_transpose=True)
        with ExitStack() as ctx:
            tokens = ctx.enter_context(nc.sbuf_tensor(core.fresh("shifted_tokens"), [P, TILES, P], F32))
            normed = ctx.enter_context(nc.sbuf_tensor(core.fresh("normed_tokens"), [P, TILES, P], F32))
            unshift(core, tokens)
            normalise_block(core, tokens, normed, 1e-5, affine(core, w(f"lg{layer}"), w(f"lb{layer}")))
        glu(core, w, layer)
    with nc.Block() as block:
        @block.vector
        def _(dve):
            for g in range(CHUNKS):
                tiles = slice(g * PER_CHUNK, (g + 1) * PER_CHUNK)
                nc.vector.scalar_tensor_tensor(out=x[:, tiles, :], in0=y[:, tiles, :], scalar=0.5, in1=x[:, tiles, :],
                                               op0=ALU.mult, op1=ALU.add).then_inc(summed.handle, 1)
    summed.done += CHUNKS



def l0_attn(core, area):
    nc, psum, x, y, zt = core.nc, core.psum, core.x, core.y, core.zt
    H, D, G = GA_HEADS, GA_DIM, 2
    R = H // G
    w = core.weights(area, L0_ATTN)
    chain, gates_done = core.sem("vector_chain"), core.sem("ga_gate_exps")
    names = ("ga_staged", "ga_products", "ga_decays", "ga_weighted", "ga_values", "ga_state")
    staged, products, decays, weighted, values, state_done = (core.sem(n) for n in names)
    with ExitStack() as ctx:
        sb = lambda name, shape, dt=F32: ctx.enter_context(nc.sbuf_tensor(core.fresh(name), shape, dt))
        normed = sb("rms_tokens", [P, TILES, P])
        normalise_block(core, x, y, 1e-5)
        normalise_block(core, y, normed, 1e-6, affine(core, w("nw"), 0.0), rms=True)
        q_t, k_t = sb("ga_q_t", [P, G, TOKENS]), sb("ga_k_t", [P, G, TOKENS])
        pairs = [(out[:, g, :], w(a)[:, g * P:(g + 1) * P], None, w(b)[:, g * P:(g + 1) * P], None)
                 for out, a, b in ((q_t, "wq", "wqs"), (k_t, "wk", "wks")) for g in range(G)]
        rotated_product(core, pairs, w("cos"), w("sin"))
        values_in = sb("ga_v", [P, TILES, H, D])
        gate = sb("ga_gate", [P, TILES, 3 * H])
        log_f = sb("ga_log_f", [P, TILES, 2, R, G])
        magnitude, soft = sb("ga_magnitude", [P, TILES, H]), sb("ga_soft", [P, TILES, H])
        out_gate = sb("ga_out_gate", [P, TILES, H])

        def take(g, got, link):
            n = slice(g * PER_CHUNK, (g + 1) * PER_CHUNK)
            split = lambda t, m: t[:, n, :].rearrange("p (b j) m -> p b j m", b=2)
            v = values_in[:, n, :, :].rearrange("p (b j) h d -> p b j (h d)", b=2)
            nc.vector.tensor_copy(v, got[:, :, 0:2, 0:P])
            return nc.vector.tensor_tensor(split(gate, 3 * H), got[:, :, 0:2, P:P + 3 * H],
                                           w("bg").unsqueeze(1).unsqueeze(1).to_broadcast([P, 2, 2, 3 * H]), ALU.add)
        tokens_product(core, w("wvg"), take)
        with nc.Block() as block:
            @block.scalar
            def _(act):
                act_chain = core.sem("scalar_chain")
                link = Steps(act, act_chain)
                link(nc.scalar.activation(magnitude[:], gate[:, :, 0:H], ACT.Abs))
                link(nc.scalar.activation(magnitude[:], magnitude[:], ACT.Exp, scale=-1.0))
                nc.scalar.activation(out_gate[:], gate[:, :, 2 * H:], ACT.Exp, scale=-1.0).then_inc(gates_done.handle, 1)
                nc.scalar.activation(gate[:, :, H:2 * H], gate[:, :, H:2 * H], ACT.Exp, scale=-1.0).then_inc(gates_done.handle, 1)
                nc.scalar.activation(soft[:], magnitude[:], ACT.Ln, bias=1.0).then_inc(gates_done.handle, 1)
                link.close()

            @block.vector
            def _(dve):
                need(dve, gates_done, 3)
                link = Steps(dve, chain)
                for t in (out_gate[:], gate[:, :, H:2 * H]):
                    link(nc.vector.tensor_scalar(t, t, 1.0, None, ALU.add))
                    link(nc.vector.reciprocal(t, t))
                link(nc.vector.tensor_scalar(gate[:, :, H:2 * H], gate[:, :, H:2 * H], 1.0 / 4.0, None, ALU.mult))
                for n in range(2):
                    tiles = slice(n * SEQ_TILES, (n + 1) * SEQ_TILES)
                    nc.vector.tensor_tensor(values_in[:, tiles, :, :], values_in[:, tiles, :, :],
                                            gate[:, tiles, H:2 * H].unsqueeze(3).to_broadcast([P, SEQ_TILES, H, D]),
                                            ALU.mult).then_inc(gates_done.handle, 1)
                for r in range(R):
                    ins = nc.vector.scalar_tensor_tensor(
                        out=log_f[:, :, 0, r, :], in0=gate[:, :, 0:H].rearrange("p t (g r) -> p t g r", g=G)[:, :, :, r], scalar=0.0,
                        in1=soft[:].rearrange("p t (g r) -> p t g r", g=G)[:, :, :, r], op0=ALU.min, op1=ALU.subtract)
                link(ins)
                nc.vector.tensor_scalar(log_f[:, :, 1, :, :].rearrange("p t r g -> p t (r g)"),
                                        log_f[:, :, 0, :, :].rearrange("p t r g -> p t (r g)"), -1.0, None,
                                        ALU.mult).then_inc(gates_done.handle, 1)
                need(dve, gates_done, 6)
                link.close()
        gates_done.done += 6

        q_s, k_s = sb("ga_q", [P, 2, G, P]), sb("ga_k", [P, 2, G, P])
        f_s = sb("ga_f", [P, 2, 2, R, G])
        f_rows = sb("ga_f_rows", [P, 2, G, R * 32])
        v_s = sb("ga_vs", [P, 2, H, D])
        decay = sb("ga_decay", [P, 2, R, G, P])
        exps = sb("ga_exps", [P, 2, 2 * H + G])
        weights = sb("ga_weights", [P, 2, R, G, P])
        k_tok = sb("ga_k_tok", [P, 2, G, R, 32])
        inter, intra, block_u = sb("ga_inter", [P, H, D]), sb("ga_intra", [P, H, D]), sb("ga_block", [P, G, 64])
        state = sb("ga_state_m", [P, G, 64])
        o = normed
        YB, SB = psum[:, 6, :], psum[:, 7, :]
        ones_col = w("upper")[:, P - 1:P]
        TURNS = TILES // 2
        with nc.Block() as block:
            def each(engine, body):
                with engine.Fori(0, BATCH) as b:
                    body(b, None, -1)
                    with engine.Fori(0, SEQ_TILES // 2) as i:
                        for p in range(2):
                            body(b, b * SEQ_TILES + i * 2 + p, p)

            @block.gpsimd
            def _(pool):
                def body(b, n, p):
                    if n is None:
                        return
                    pool.wait_ge(state_done.handle, state_done.done + n + b + 1)
                    nc.gpsimd.tensor_copy(q_s[:, p], q_t[:, :, bass.ds(n * P, P)])
                    nc.gpsimd.tensor_copy(k_s[:, p], k_t[:, :, bass.ds(n * P, P)])
                    nc.gpsimd.tensor_copy(f_s[:, p].rearrange("p s r g -> p (s r g)").unsqueeze(1),
                                          log_f[:].rearrange("p t s r g -> p t (s r g)")[:, bass.ds(n, 1), :])
                    nc.gpsimd.tensor_copy(f_rows[:, p].rearrange("p g (r d) -> p g r d", r=R),
                                          log_f[:, :, 0, :, :].rearrange("p t r g -> p t g r")[:, bass.ds(n, 1), :, :]
                                          .rearrange("p t g r -> p (t g) r").unsqueeze(3).to_broadcast([P, G, R, 32]))
                    nc.gpsimd.tensor_copy(v_s[:, p].rearrange("p h d -> p (h d)").unsqueeze(1),
                                          values_in[:].rearrange("p t h d -> p t (h d)")[:, bass.ds(n, 1), :]).then_inc(staged.handle, 1)
                each(pool, body)

            @block.tensor
            def _(pe):
                def body(b, n, p):
                    if n is None:
                        return
                    pe.wait_ge(staged.handle, staged.done + n + 1)
                    for g in range(G):
                        nc.tensor.transpose(SB[:, P + g * P:P + (g + 1) * P], k_s[:, p, g, :], core.ident[:])
                    lf, nlf = f_s[:, p, 0].rearrange("p r g -> p (r g)"), f_s[:, p, 1].rearrange("p r g -> p (r g)")
                    nc.tensor.matmul(YB[:, 256:264], w("upper"), lf, start=True, stop=True)
                    nc.tensor.matmul(YB[:, 264:272], ones_col.to_broadcast([P, P]), lf, start=True, stop=False)
                    nc.tensor.matmul(YB[:, 264:272], w("upper"), nlf, start=False, stop=True)
                    for g in range(G):
                        nc.tensor.matmul(YB[:, 272 + g:273 + g], f_rows[:, p, g, :], ones_col,
                                         start=True, stop=True)
                    for k in range(2):
                        for a in range(4):
                            nc.tensor.matmul(psum[:, 4 + k, a * P:(a + 1) * P], lf[:, 4 * k + a:4 * k + a + 1].to_broadcast([P, P]), w("upper"),
                                             start=(a == 0), stop=False, skip_group_check=True)
                        nc.tensor.matmul(psum[:, 4 + k, :], w("upper"), nlf[:, 4 * k:4 * k + 4].unsqueeze(2).to_broadcast([P, 4, P]),
                                         start=False, stop=False, skip_group_check=True)
                        last = nc.tensor.matmul(psum[:, 4 + k, :], core.mask("ident"), core.mask("causal").unsqueeze(1).to_broadcast([P, 4, P]),
                                                start=False, stop=True, skip_group_check=True)
                    last.then_inc(products.handle, 1)
                    for g in range(G):
                        for r in range(R):
                            rows = slice(32 * r, 32 * r + D)
                            last = nc.tensor.matmul(psum[:, r, g * P:(g + 1) * P], k_s[rows, p, g, :], q_s[rows, p, g, :],
                                                    start=True, stop=True, skip_group_check=True)
                    last.then_inc(products.handle, 1)
                    pe.wait_ge(weighted.handle, weighted.done + n * 2 + 2)
                    for h in range(H):
                        nc.tensor.matmul(YB[:, h * D:(h + 1) * D], weights[:, p, h % R, h // R, :], v_s[:, p, h, :], start=True, stop=True)
                    for g in range(G):
                        nc.tensor.matmul(YB[:, P + g * 64:P + (g + 1) * 64], q_s[:, p, g, :], state[:, g, :], start=True, stop=True)
                    for g in range(G):
                        last = nc.tensor.matmul(SB[:, g * 64:(g + 1) * 64], k_tok[:, p, g].rearrange("p r d -> p (r d)"),
                                                v_s[:, p, g * R:(g + 1) * R, :], start=True, stop=True)
                    last.then_inc(values.handle, 1)
                each(pe, body)

            @block.scalar
            def _(act):
                def body(b, n, p):
                    if n is None:
                        return
                    act.wait_ge(products.handle, products.done + n * 2 + 1)
                    nc.scalar.activation(exps[:, p, :], YB[:, 256:274], ACT.Exp)
                    nc.scalar.activation(decay[:, p].rearrange("p r g n -> p (r g n)").rearrange("p (b n) -> p b n", b=2), psum[:, 4:6, :],
                                         ACT.Exp).then_inc(decays.handle, 1)
                each(act, body)

            @block.vector
            def _(dve):
                def body(b, n, p):
                    if n is None:
                        nc.vector.memset(state[:], 0.0).then_inc(state_done.handle, 1)
                        return
                    dve.wait_ge(decays.handle, decays.done + n + 1)
                    nc.vector.tensor_tensor(k_tok[:, p], SB[:, P:3 * P].rearrange("p (g r d) -> p g r d", g=G, r=R),
                                            exps[:, p, H:2 * H].rearrange("p (r g) -> p g r", r=R).unsqueeze(3).to_broadcast([P, G, R, 32]),
                                            ALU.mult).then_inc(weighted.handle, 1)
                    dve.wait_ge(products.handle, products.done + n * 2 + 2)
                    nc.vector.tensor_tensor(weights[:, p].rearrange("p r g n -> p r (g n)"), psum[:, 0:4, 0:G * P],
                                            decay[:, p].rearrange("p r g n -> p r (g n)"), ALU.mult).then_inc(weighted.handle, 1)
                    dve.wait_ge(values.handle, values.done + n + 1)
                    link = Steps(dve, chain, 2, n)
                    nc.vector.tensor_tensor(inter[:].rearrange("p (g r) d -> p g r d", g=G), YB[:, P:2 * P].rearrange("p (g r d) -> p g r d", g=G, r=R),
                                            exps[:, p, 0:H].rearrange("p (r g) -> p g r", r=R).unsqueeze(3).to_broadcast([P, G, R, D]),
                                            ALU.mult)
                    link(nc.vector.tensor_tensor(block_u[:].rearrange("p g m -> p (g m)"), SB[:, 0:P], w("diag"), ALU.mult))
                    nc.vector.tensor_tensor(intra[:].rearrange("p h d -> p (h d)"), YB[:, 0:P], inter[:].rearrange("p h d -> p (h d)"), ALU.add)
                    for g in range(G):
                        last = nc.vector.scalar_tensor_tensor(out=state[:, g, :], in0=state[:, g, :], scalar=exps[:, p, 2 * H + g:2 * H + g + 1],
                                                              in1=block_u[:, g, :], op0=ALU.mult, op1=ALU.add)
                    link(last)
                    nc.vector.tensor_tensor(o[:].rearrange("p t (h d) -> p t h d", h=H)[:, bass.ds(n, 1), :, :], intra[:].unsqueeze(1),
                                                 out_gate[:, bass.ds(n, 1), :].unsqueeze(3).to_broadcast([P, 1, H, D]), ALU.mult).then_inc(state_done.handle, 1)
                each(dve, body)
        chain.done += 2 * TILES
        for tally, n in ((staged, 1), (products, 2), (decays, 1), (weighted, 2), (values, 1), (state_done, 1)):
            tally.done += n * TILES
        state_done.done += BATCH
        normalise_block(core, x, o, 1e-5, plain(core), only_transpose=True)
        tokens_product(core, w("wout"), add_to_x(core, bias=w("bout")))


STACK = 74
MAX_ROWS = 72


class Stacks:

    PARTS = [(a, b) for a in range(3) for b in range(3)]

    def __init__(self, core, ctx, before, behind):
        nc = core.nc
        sb = lambda name, shape, dt: ctx.enter_context(nc.sbuf_tensor(core.fresh(name), shape, dt))
        self.before, self.behind = before, behind
        self.q = sb("stack_q", [P, FA_HEADS, SEQ + behind], BF16)
        self.k = sb("stack_k", [P, FA_HEADS, before + SEQ], BF16)
        self.parts = [[sb(f"part_{n}{i}", [P, SEQ], BF16) for i in range(3)] for n in "qk"]
        self.scratch = nc.dram_tensor(core.fresh("parts_dram"), (BATCH, 2, 3, P, SEQ), BF16).ap()

    def place(self, core, engine, which, b, ready=None):
        placed = core.sem(("q_parts_placed", "k_parts_placed")[which])
        to, at = (self.q, 0) if which == 0 else (self.k, self.before)
        for n, pair in enumerate(self.PARTS):
            if ready is not None and n == len(self.PARTS) - 1:
                need(engine, *ready)
            engine.dma_start(to[8 * n:8 * n + 8, :, at:at + SEQ],
                             self.scratch[b, which, pair[which]].rearrange("(h d) t -> d h t", d=FA_DIM)).then_inc(placed.handle, 16)
        need(engine, placed, 16 * len(self.PARTS))

    def fill_first(self, core, q, k):
        nc = core.nc
        chain, split, cleared = (core.sem(n) for n in ("vector_chain", "parts_split", "stack_cleared"))
        stored = [core.sem("q_parts_stored"), core.sem("k_parts_stored")]
        with nc.Block() as block:
            @block.vector
            def _(dve):
                link = Steps(dve, chain)
                for b in range(BATCH):
                    for which, all_tokens in enumerate((q, k)):
                        src, parts = all_tokens[:, b * SEQ:(b + 1) * SEQ], self.parts[which]
                        if b:
                            need(dve, stored[which], 48 * b)
                        link(nc.vector.tensor_copy(parts[0][:], src))
                        link(nc.vector.tensor_tensor(src, src, parts[0][:], ALU.subtract))
                        link(nc.vector.tensor_copy(parts[1][:], src))
                        nc.vector.tensor_tensor(parts[2][:], src, parts[1][:], ALU.subtract).then_inc(split.handle, 1)
                link.close()

            @block.gpsimd
            def _(pool):
                nc.gpsimd.memset(self.k[64:STACK, :, :], 1.0).then_inc(cleared.handle, 1)
                if self.before:
                    need(pool, cleared, 1)
                    nc.gpsimd.memset(self.k[0:96, :, 0:self.before], 0.0).then_inc(cleared.handle, 1)
                if self.behind:
                    nc.gpsimd.memset(self.q[0:96, :, SEQ:], 0.0).then_inc(cleared.handle, 1)

            def store_and_place(engine, which):
                for b in range(BATCH):
                    need(engine, split, 2 * b + which + 1)
                    for i in range(3):
                        engine.dma_start(self.scratch[b, which, i], self.parts[which][i][:]).then_inc(stored[which].handle, 16)
                    need(engine, stored[which], 48 * (b + 1))
                    if b == 0:
                        self.place(core, engine, which, 0, (cleared, edges) if which else None)

            edges = 1 + bool(self.before) + bool(self.behind)

            @block.sync
            def _(sp):
                store_and_place(sp, 0)

            @block.scalar
            def _(act):
                store_and_place(act, 1)
        split.done += 2 * BATCH
        for tally in stored:
            tally.done += 48 * BATCH
        cleared.done += edges
        self.placed(core)

    def fill_next(self, core, b):
        with core.nc.Block() as block:
            @block.sync
            def _(sp):
                self.place(core, sp, 0, b)

            @block.scalar
            def _(act):
                self.place(core, act, 1, b)
        self.placed(core)

    def placed(self, core):
        for name in ("q_parts_placed", "k_parts_placed"):
            core.sem(name).done += 16 * len(self.PARTS)


def value_tokens(core, out, weights, bias):
    nc = core.nc
    ones = core.sem("value_ones")
    with nc.Block() as block:
        @block.gpsimd
        def _(pool):
            nc.gpsimd.memset(out, 1.0).then_inc(ones.handle, 1)
    ones.done += 1

    def take(g, got, link):
        to = out[:, g * PER_CHUNK:(g + 1) * PER_CHUNK, :, 0:FA_DIM]
        got = got.rearrange("p j (h d) -> p j h d", h=FA_HEADS)
        if bias is None:
            return nc.vector.tensor_copy(to, got)
        for j in range(PER_CHUNK):
            last = nc.vector.tensor_tensor(to[:, j], got[:, j], bias.rearrange("p (h d) -> p h d", h=FA_HEADS), ALU.add)
        return last
    tokens_product(core, weights, take)


def l1_attn(core, area):
    nc, psum, x, y, zt = core.nc, core.psum, core.x, core.y, core.zt
    w = core.weights(area, L1_ATTN)
    H, D, T = FA_HEADS, FA_DIM, SEQ_TILES
    QUADS, GROUP = FA_HEADS // 4, 32
    UNITS = 2 * T
    base = sum(n for _, n in L1_ATTN)
    q_t, k_t = (core.areas[area][:, base + i * TOKENS:base + (i + 1) * TOKENS] for i in range(2))
    chain = core.sem("vector_chain")
    (max_scores, max_read, rows_ready, rows_stored, rows_placed, scores, probs, v_staged, used, taken, turned, normed,
     cleared) = (core.sem(n) for n in (
        "fa_max_scores", "fa_max_read", "fa_rows_split", "fa_rows_stored", "fa_rows_placed", "fa_scores", "fa_probs",
        "fa_values_staged", "fa_probs_used", "fa_sums_taken", "fa_sums_turned", "fa_normed", "fa_cleared"))
    with ExitStack() as ctx:
        sb = lambda name, shape, dt=F32: ctx.enter_context(nc.sbuf_tensor(core.fresh(name), shape, dt))
        normalise_block(core, x, y, 1e-5, plain(core))
        rotated_product(core, [(q_t, w("wq"), w("bq"), w("wqs"), w("bqs")), (k_t, w("wk"), w("bk"), w("wks"), w("bks"))],
                        w("cos"), w("sin"))
        v = sb("fa_v", [P, TILES, H, D + 1])
        value_tokens(core, v[:], w("wv"), w("bv"))
        stacks = Stacks(core, ctx, 0, 0)
        prob = sb("fa_prob", [P, 4, SEQ])
        pair_v = sb("fa_pair_v", [P, 2, T, 2, GROUP])
        sums = sb("fa_sums", [P, 2, CHUNK])
        half_top = sb("fa_half_top", [P, 2, 2, T, 2])
        top = sb("fa_top", [P, 2, 2, T])
        top_turned = sb("fa_top_turned", [P, GROUP])
        rows = sb("fa_rows", [P, 2, GROUP], BF16)
        rec = sb("fa_rec", [P, 4, 4])
        max_dram = nc.dram_tensor("fa_max_dram", (P // GROUP, GROUP, 2, GROUP), BF16).ap()
        q_s = stacks.q[0:STACK].rearrange("p h t -> p (h t)")
        k_s = stacks.k[0:STACK].rearrange("p h t -> p (h t)")
        q_parts, k_parts = q_s[0:MAX_ROWS], k_s[0:MAX_ROWS]

        with nc.Block() as block:
            @block.gpsimd
            def _(pool):
                nc.gpsimd.memset(pair_v[:], 0.0).then_inc(cleared.handle, 1)

            @block.vector
            def _(dve):
                nc.vector.memset(top[:], 0.0).then_inc(cleared.handle, 1)
        cleared.done += 2

        for b in range(BATCH):
            if b:
                stacks.fill_next(core, b)
            else:
                stacks.fill_first(core, q_t, k_t)


            def pe_max(pe, q, r, opening=False):
                head, t = q * 2 + r % 2, r // 2
                for half in range(2):
                    if not (opening and r == 0):
                        pe.wait_ge(max_read.handle, max_read.done + q * 2 * UNITS + 2 * r + half - 1)
                    nc.tensor.matmul(psum[:, half, :], q_parts[:, bass.ds(head * SEQ + t * P, P)],
                                     k_parts[:, bass.ds(head * SEQ + half * CHUNK, CHUNK)],
                                     start=True, stop=True).then_inc(max_scores.handle, 1)

            def pe_scores(pe, q, r, first):
                head, t = q * 2 + r % 2, r // 2
                if not (first and r < 2):
                    pe.wait_ge(probs.handle, probs.done + q * UNITS + r - 1)
                for half in range(2):
                    last = nc.tensor.matmul(psum[:, 2 + 2 * (r % 2) + half, :], k_s[:, bass.ds(head * SEQ + t * P, P)],
                                            q_s[:, bass.ds(head * SEQ + half * CHUNK, CHUNK)], start=True, stop=True)
                last.then_inc(scores.handle, 1)

            def pe_values(pe, q, parity, t, first):
                if t == 0:
                    pe.wait_ge(v_staged.handle, v_staged.done + q + 1)
                    if not first:
                        pe.wait_ge(normed.handle, normed.done + q - 1)
                pe.wait_ge(probs.handle, probs.done + q * UNITS + 2 * t + 2)
                for j in range(2):
                    for half in range(2):
                        at = GROUP * (2 * j + half)
                        last = nc.tensor.matmul(psum[at:at + GROUP, 6 + parity, :], pair_v[:, parity, t, j, :],
                                                prob[:, (2 * t + j) % 4, half * CHUNK:(half + 1) * CHUNK],
                                                start=(t == 0), stop=(t == T - 1), tile_position=(0, at), skip_group_check=True)
                last.then_inc(used.handle, 1)

            def pe_turn_sums(pe, q, parity):
                pe.wait_ge(taken.handle, taken.done + q + 1)
                for s in range(4):
                    last = nc.tensor.transpose(psum[:, 6 + parity, s * P:(s + 1) * P], sums[:, parity, s * P:(s + 1) * P], core.ident[:])
                last.then_inc(turned.handle, 1)

            def pe_pair(pe, q, parity, ahead, first):
                pe.wait_ge(rows_placed.handle, rows_placed.done + q * 32 + 32)
                for t in range(T):
                    for j in range(2):
                        pe_scores(pe, q, 2 * t + j, first and parity == 0)
                        if ahead:
                            pe_max(pe, q + 2, 2 * t + j)
                    if t:
                        pe_values(pe, q, parity, t - 1, first)
                    elif not (first and parity == 0):
                        pe_values(pe, q - 1, 1 - parity, T - 1, False)
                    if t == 2 and not (first and parity == 0):
                        pe_turn_sums(pe, q - 1, 1 - parity)

            def act_pair(act, q, parity, first):
                for r in range(UNITS):
                    act.wait_ge(scores.handle, scores.done + q * UNITS + r + 1)
                    if not (first and parity == 0 and r < 4) and r % 2 == 0:
                        act.wait_ge(used.handle, used.done + q * T + r // 2 - 1)
                    nc.scalar.activation(prob[:, r % 4, :], psum[:, 2 + 2 * (r % 2):4 + 2 * (r % 2), :].rearrange("p a n -> p (a n)"),
                                         ACT.Exp, scale=float(D) ** -0.5).then_inc(probs.handle, 1)
                    if r == 2 and not (first and parity == 0):
                        act_take(act, q - 1, 1 - parity)

            def act_take(act, q, parity):
                act.wait_ge(used.handle, used.done + q * T + T)
                nc.scalar.copy(sums[:, parity, :], psum[:, 6 + parity, :]).then_inc(taken.handle, 1)

            def dve_max(dve, q, parity, link, between=None):
                for r in range(UNITS):
                    for half in range(2):
                        dve.wait_ge(max_scores.handle, max_scores.done + q * 2 * UNITS + 2 * r + half + 1)
                        nc.vector.tensor_reduce(half_top[:, parity, r % 2, r // 2, half:half + 1], psum[:, half, :], AX.X,
                                                ALU.max).then_inc(max_read.handle, 1)
                    if r == 8 and between:
                        between()
                dve.wait_ge(max_read.handle, max_read.done + q * 2 * UNITS + 2 * UNITS)
                link(nc.vector.tensor_reduce(top[:, parity], half_top[:, parity], AX.X, ALU.max, negate=True))
                link(nc.vector.transpose(top_turned[:], top[:].rearrange("p a j t -> p (a j t)")))
                if not isinstance(q, int) or q:
                    dve.wait_ge(rows_stored.handle, rows_stored.done + q * 16)
                link(nc.vector.tensor_copy(rows[:, 0, :], top_turned[:]))
                nc.vector.tensor_tensor(rows[:, 1, :], top_turned[:], rows[:, 0, :], ALU.subtract).then_inc(rows_ready.handle, 1)

            def dve_normalise(dve, q, parity, link):
                dve.wait_ge(turned.handle, turned.done + q + 1)
                if not isinstance(q, int) or q:
                    dve.wait_ge(normed.handle, normed.done + q)
                got = psum[:, 6 + parity, :].rearrange("p (s g e) -> p s g e", s=4, g=4)
                link(nc.vector.reciprocal(rec[:], got[:, :, :, D]))
                out = y[:, b * T:(b + 1) * T, bass.ds(q * 2 * D, 2 * D)].rearrange("p (a s) (j d) -> p a s j d", a=2, j=2)
                for g in range(4):
                    last = nc.vector.tensor_tensor(out[:, g % 2, :, g // 2, :], got[:, :, g, 0:D],
                                                   rec[:, :, g:g + 1].to_broadcast([P, 4, D]), ALU.mult)
                last.then_inc(normed.handle, 1)

            def pool_values(pool, q, parity):
                nc.gpsimd.tensor_copy(pair_v[:, parity, :, :, 0:D + 1],
                                      v[:, b * T:(b + 1) * T, bass.ds(q * 2, 2), :]).then_inc(v_staged.handle, 1)

            def sp_rows(sp, q):
                need(sp, rows_ready, q + 1)
                if q:
                    need(sp, rows_placed, q * 32)
                sp.dma_start(max_dram.rearrange("b c i r -> (b c) i r"), rows[:]).then_inc(rows_stored.handle, 16)
                need(sp, rows_stored, (q + 1) * 16)
                mine = slice(UNITS * (q % 2), UNITS * (q % 2) + UNITS)
                for i in range(2):
                    sp.dma_start(stacks.q[MAX_ROWS + i:MAX_ROWS + i + 1, 2 * q:2 * q + 2, :].rearrange("o j (t b r) -> o (j t) b r", t=T, r=GROUP),
                                 max_dram[:, mine, i:i + 1, :].rearrange("b c i r -> i c b r")).then_inc(rows_placed.handle, 16)

            with nc.Block() as block:
                @block.tensor
                def _(pe):
                    for q in range(2):
                        for r in range(UNITS):
                            pe_max(pe, q, r, opening=(q == 0))
                    for q in range(2):
                        pe_pair(pe, q, q, True, True)
                    with pe.Fori(1, QUADS - 1) as i:
                        for parity in range(2):
                            pe_pair(pe, i * 2 + parity, parity, True, False)
                    for q in (H // 2 - 2, H // 2 - 1):
                        pe_pair(pe, q, q % 2, False, False)
                    pe_values(pe, H // 2 - 1, 1, T - 1, False)
                    pe_turn_sums(pe, H // 2 - 1, 1)

                @block.scalar
                def _(act):
                    for q in range(2):
                        act_pair(act, q, q, True)
                    with act.Fori(1, QUADS) as i:
                        for parity in range(2):
                            act_pair(act, i * 2 + parity, parity, False)
                    act_take(act, H // 2 - 1, 1)

                @block.vector
                def _(dve):
                    link = Steps(dve, chain)
                    for q in range(2):
                        dve_max(dve, q, q, link)
                    dve_max(dve, 2, 0, link)
                    dve_max(dve, 3, 1, link, lambda: dve_normalise(dve, 0, 0, link))
                    link.close()
                    with dve.Fori(2, QUADS) as i:
                        link = Steps(dve, chain, 2 * (3 + 1), i - 2)
                        for parity in range(2):
                            dve_max(dve, i * 2 + parity, parity, link,
                                    lambda: dve_normalise(dve, i * 2 + parity - 3, 1 - parity, link))
                    link.close(QUADS - 2)
                    link = Steps(dve, chain)
                    for q in range(H // 2 - 3, H // 2):
                        dve_normalise(dve, q, q % 2, link)
                    link.close()

                @block.gpsimd
                def _(pool):
                    for q in range(2):
                        pool_values(pool, q, q)
                    with pool.Fori(1, QUADS) as i:
                        for parity in range(2):
                            pool.wait_ge(used.handle, used.done + (i * 2 + parity - 1) * T)
                            pool_values(pool, i * 2 + parity, parity)

                @block.sync
                def _(sp):
                    for q in range(H // 2):
                        sp_rows(sp, q)
            for tally, n in ((max_scores, 2 * UNITS), (max_read, 2 * UNITS), (rows_ready, 1), (rows_placed, 32), (rows_stored, 16),
                             (scores, UNITS), (probs, UNITS), (v_staged, 1), (used, T), (taken, 1), (turned, 1), (normed, 1)):
                tally.done += n * H // 2
        normalise_block(core, x, y, 1e-5, plain(core), only_transpose=True)
        tokens_product(core, w("wo"), add_to_x(core, bias=w("bo")))


I32 = mybir.dt.int32
QUANT_STEPS = 14


def quantise(nc, link, source, out, tmp, ready=None):
    n = source.shape[1]
    blocks = lambda t: t[:, 0:n].rearrange("p (b e) -> p b e", e=Q4_BLOCK)
    nb = n // Q4_BLOCK
    biggest, scale, inverse = (t[:, 0:nb] for t in tmp["small"])
    scaled, size, high, low = (t[:, 0:n] for t in tmp["wide"])
    spread = lambda t: t.unsqueeze(2).to_broadcast([P, nb, Q4_BLOCK])
    link(nc.vector.tensor_reduce(biggest, blocks(source), AX.X, ALU.max, apply_absolute_value=True))
    link(nc.vector.tensor_scalar(scale, biggest, 1.0 / 6.0, 1e-12, ALU.mult, ALU.max))
    link(nc.vector.reciprocal(inverse, scale))
    link(nc.vector.tensor_tensor(blocks(scaled), blocks(source), spread(inverse), ALU.mult))
    link(nc.vector.tensor_scalar(size.bitcast(I32), scaled.bitcast(I32), 0x7FFFFFFF, None, ALU.bitwise_and))
    link(nc.vector.tensor_scalar(high, size, 5.0, 2.0, ALU.is_gt, ALU.mult))
    for mid in (3.5, 2.5):
        link(nc.vector.scalar_tensor_tensor(out=high, in0=size, scalar=mid, in1=high, op0=ALU.is_gt, op1=ALU.add))
    link(nc.vector.tensor_scalar(low, size, 1.75, None, ALU.is_gt))
    for mid in (1.25, 0.75, 0.25):
        link(nc.vector.scalar_tensor_tensor(out=low, in0=size, scalar=mid, in1=low, op0=ALU.is_gt, op1=ALU.add))
    link(nc.vector.scalar_tensor_tensor(out=high, in0=low, scalar=0.5, in1=high, op0=ALU.mult, op1=ALU.add))
    link(nc.vector.scalar_tensor_tensor(out=low.bitcast(I32), in0=scaled.bitcast(I32), scalar=-2147483648, in1=high.bitcast(I32),
                                        op0=ALU.bitwise_and, op1=ALU.bitwise_or))
    last = nc.vector.tensor_tensor(blocks(out), blocks(low), spread(scale), ALU.mult)
    link(last) if ready is None else last.then_inc(ready.handle, 1)


def l2_ffn(core, area):
    nc, psum, x, y, zt = core.nc, core.psum, core.x, core.y, core.zt
    w = core.weights(area, L2_FFN)
    chain = core.sem("vector_chain")
    base = sum(n for _, n in L2_FFN)
    gate_up = core.areas[area][:, base:base + 2 * Q4_HID]
    down = core.areas[area][:, base + 2 * Q4_HID:base + 2 * Q4_HID + 3 * P]
    turned, taken = core.sem("bank_transposed"), core.sem("bank_evacuated")
    products, silu, gated, ready, h_turned, h_taken, out_made, added = (core.sem(n) for n in (
        "q4_up_product", "q4_silu", "q4_gated", "q4_hidden_quantised", "q4_hidden_turned", "q4_hidden_taken",
        "q4_out_product", "q4_added"))
    WIDE = PER_CHUNK * Q4_HID
    with ExitStack() as ctx:
        sb = lambda name, shape, dt=F32: ctx.enter_context(nc.sbuf_tensor(core.fresh(name), shape, dt))
        tmp = {"small": [sb(f"q4_small{i}", [P, WIDE // Q4_BLOCK]) for i in range(3)],
               "wide": [sb(f"q4_wide{i}", [P, WIDE]) for i in range(4)]}
        if not core.weights_quantised:
            core.weights_quantised = True
            dequant = sb("q4_weights", [P, 6 * P + Q4_HID])
            with nc.Block() as block:
                @block.vector
                def _(dve):
                    link = Steps(dve, chain)
                    packed = core.areas[area][:, 0:base]
                    quantise(nc, link, packed, dequant, tmp)
                    link.close()
            with nc.Block() as block:
                @block.tensor
                def _(pe):
                    for s in range(2):
                        for m, (at, rows) in enumerate(Q4_PARTS):
                            last = nc.tensor.transpose(psum[:, s, at:at + rows], dequant[0:rows, (3 * s + m) * P:(3 * s + m + 1) * P],
                                                       core.ident[0:rows, 0:rows])
                    for m, (at, rows) in enumerate(Q4_PARTS):
                        last = nc.tensor.transpose(psum[0:rows, 2, m * P:(m + 1) * P], dequant[:, 6 * P + at:6 * P + at + rows], core.ident[:])
                    last.then_inc(turned.handle, 1)

                @block.scalar
                def _(act):
                    need(act, turned, 1)
                    nc.scalar.copy(gate_up.rearrange("p (s n) -> p s n", s=2), psum[:, 0:2, 0:Q4_HID]).then_inc(taken.handle, 1)
                    for m, (at, rows) in enumerate(Q4_PARTS):
                        nc.scalar.copy(down[0:rows, m * P:(m + 1) * P], psum[0:rows, 2, m * P:(m + 1) * P]).then_inc(taken.handle, 1)
            turned.done += 1
            taken.done += 4
        normalise_block(core, x, y, 1e-5)
        with nc.Block() as block:
            @block.vector
            def _(dve):
                link = Steps(dve, chain)
                half = TOKENS // 2
                flat = y[:].rearrange("p t d -> p (t d)")
                for b in range(2):
                    quantise(nc, link, flat[:, b * half:(b + 1) * half], flat[:, b * half:(b + 1) * half], tmp)
                link.close()
        normalise_block(core, x, y, 1e-5, plain(core), only_transpose=True)
        act_gate = sb("q4_gate", [P, 2, Q4_HID])
        hidden = sb("q4_hidden", [P, PER_CHUNK, Q4_HID])
        hidden_q = sb("q4_hidden_q", [P, PER_CHUNK, Q4_HID])
        hidden_t = sb("q4_hidden_t", [P, 3, CHUNK])
        with nc.Block() as block:
            @block.tensor
            def _(pe):
                def up(c):
                    for j in range(PER_CHUNK):
                        n = c * PER_CHUNK + j
                        if n >= 2:
                            need(pe, gated, n - 1)
                        for s in range(2):
                            last = nc.tensor.matmul(psum[:, 2 * (n % 2) + s, 0:Q4_HID], zt[:, n * P:(n + 1) * P],
                                                    gate_up[:, s * Q4_HID:(s + 1) * Q4_HID], start=True, stop=True)
                        last.then_inc(products.handle, 1)
                for c in range(CHUNKS):
                    up(c)
                    need(pe, ready, c + 1)
                    for m, (at, rows) in enumerate(Q4_PARTS):
                        for j in range(PER_CHUNK):
                            last = nc.tensor.transpose(psum[0:rows, 4 + m, j * P:(j + 1) * P], hidden_q[:, j, at:at + rows], core.ident[:])
                    last.then_inc(h_turned.handle, 1)
                    need(pe, h_taken, 3 * (c + 1))
                    if c >= 1:
                        need(pe, added, c)
                    for j in range(PER_CHUNK):
                        for m, (at, rows) in enumerate(Q4_PARTS):
                            last = nc.tensor.matmul(psum[:, 7, j * P:(j + 1) * P], hidden_t[0:rows, m, j * P:(j + 1) * P],
                                                    down[0:rows, m * P:(m + 1) * P], start=(m == 0), stop=(m == 2))
                    last.then_inc(out_made.handle, 1)

            @block.scalar
            def _(act):
                for c in range(CHUNKS):
                    for j in range(PER_CHUNK):
                        n = c * PER_CHUNK + j
                        need(act, products, n + 1)
                        if n >= 2:
                            need(act, gated, n - 1)
                        nc.scalar.activation(act_gate[:, n % 2, :], psum[:, 2 * (n % 2), 0:Q4_HID], ACT.Silu).then_inc(silu.handle, 1)
                    need(act, h_turned, c + 1)
                    for m, (at, rows) in enumerate(Q4_PARTS):
                        nc.scalar.copy(hidden_t[0:rows, m, :], psum[0:rows, 4 + m, :]).then_inc(h_taken.handle, 1)

            @block.vector
            def _(dve):
                with dve.Fori(0, CHUNKS) as c:
                    for j in range(PER_CHUNK):
                        dve.wait_ge(silu.handle, silu.done + c * PER_CHUNK + j + 1)
                        nc.vector.tensor_tensor(hidden[:, j, :], psum[:, 2 * (j % 2) + 1, 0:Q4_HID], act_gate[:, j % 2, :],
                                                ALU.mult).then_inc(gated.handle, 1)
                    dve.wait_ge(gated.handle, gated.done + (c + 1) * PER_CHUNK)
                    link = Steps(dve, chain, QUANT_STEPS, c)
                    quantise(nc, link, hidden[:].rearrange("p j n -> p (j n)"), hidden_q[:].rearrange("p j n -> p (j n)"), tmp, ready)
                    dve.wait_ge(out_made.handle, out_made.done + c + 1)
                    tiles = x[:, bass.ds(c * PER_CHUNK, PER_CHUNK), :]
                    nc.vector.scalar_tensor_tensor(out=tiles, in0=psum[:, 7, :].rearrange("p (j n) -> p j n", j=PER_CHUNK), scalar=0.5,
                                                   in1=tiles, op0=ALU.mult, op1=ALU.add).then_inc(added.handle, 1)
                link.close(CHUNKS)
        for tally, n in ((products, TILES), (silu, TILES), (gated, TILES), (ready, CHUNKS), (h_turned, CHUNKS),
                         (h_taken, 3 * CHUNKS), (out_made, CHUNKS), (added, CHUNKS)):
            tally.done += n



def l2_attn(core, area):
    nc, psum, x, y, zt = core.nc, core.psum, core.x, core.y, core.zt
    w = core.weights(area, L2_ATTN)
    H, D, T, W = FA_HEADS, FA_DIM, SEQ_TILES, WA_WIN
    GROUP = 3
    GROUPS = [(g, min(GROUP, H - g)) for g in range(0, H, GROUP)]
    SETS = [GROUPS[:len(GROUPS) // 2], GROUPS[len(GROUPS) // 2:]]
    COLS = 32
    QUADS = H // 4
    chain = core.sem("vector_chain")
    (feature_made, feature_taken, max_scores, tops, tops_turned, rows_ready, rows_stored, rows_placed, scores, probs, v_staged,
     v_used, sums_made, sums_taken, sums_turned, normed, cleared) = (core.sem(n) for n in (
        "wa_feature_product", "wa_feature_taken", "wa_max_scores", "wa_tops", "wa_tops_turned", "wa_rows_split", "wa_rows_stored",
        "wa_rows_placed", "wa_scores", "wa_probs", "wa_values_staged", "wa_values_used", "wa_sums", "wa_sums_taken", "wa_sums_turned", "wa_normed",
        "wa_values_cleared"))
    with ExitStack() as ctx:
        sb = lambda name, shape, dt=F32: ctx.enter_context(nc.sbuf_tensor(core.fresh(name), shape, dt))
        o = sb("wa_tokens", [P, TILES, P])
        normalise_block(core, x, y, 1e-5)
        normalise_block(core, y, o, 1e-5, affine(core, w("gamma"), w("beta")))
        spare = L2_FFN_HELD
        q_t, k_t = (core.areas[0][:, spare + i * TOKENS:spare + (i + 1) * TOKENS] for i in range(2))
        with nc.Block() as block:
            @block.tensor
            def _(pe):
                for n in range(2 * CHUNKS):
                    if n >= 4:
                        need(pe, feature_taken, n - 3)
                    nc.tensor.matmul(psum[:, n % 4, :], w("wq" if n < CHUNKS else "wk"), zt[:, n % CHUNKS * CHUNK:(n % CHUNKS + 1) * CHUNK],
                                     start=True, stop=True).then_inc(feature_made.handle, 1)

            @block.scalar
            def _(act):
                for n in range(2 * CHUNKS):
                    need(act, feature_made, n + 1)
                    to = q_t if n < CHUNKS else k_t
                    nc.scalar.copy(to[:, n % CHUNKS * CHUNK:(n % CHUNKS + 1) * CHUNK], psum[:, n % 4, :]).then_inc(feature_taken.handle, 1)
        feature_made.done += 2 * CHUNKS
        feature_taken.done += 2 * CHUNKS
        v = core.areas[0][:, spare + 2 * TOKENS:spare + 2 * TOKENS + TILES * H * (D + 1)].rearrange("p (t h e) -> p t h e", t=TILES, h=H)
        value_tokens(core, v, w("wv"), None)
        stacks = Stacks(core, ctx, W, W)
        prob = sb("wa_prob", [P, 2, H, BAND])
        tile_v = sb("wa_tile_values", [P, 2, H, COLS])
        sums = sb("wa_sums_copy", [P, CHUNK])
        top = sb("wa_top", [P, H, T])
        rows = sb("wa_rows", [P, 2, P], BF16)
        rec = sb("wa_rec", [P, H])
        max_dram = nc.dram_tensor("wa_max_dram", (2, H, SEQ), BF16).ap()
        with nc.Block() as block:
            @block.gpsimd
            def _(pool):
                nc.gpsimd.memset(tile_v[:], 0.0).then_inc(cleared.handle, 1)
        cleared.done += 1
        q_s, k_s = stacks.q[0:STACK], stacks.k[0:STACK]

        def banded(left, right, at_left, at_right, mask, half, first_bank):
            for g, (head, n) in enumerate(SETS[half]):
                bank = psum[:, first_bank + g, :]
                for h in range(n):
                    nc.tensor.matmul(bank[:, h * BAND:(h + 1) * BAND], left[:, head + h, bass.ds(at_left, P)],
                                     right[:, head + h, bass.ds(at_right, BAND)], start=(h == 0), stop=False, skip_group_check=True)
                last = nc.tensor.matmul(bank[:, 0:n * BAND], core.mask("ident"), mask.unsqueeze(1).to_broadcast([P, n, BAND]),
                                        start=False, stop=True, skip_group_check=True)
            return last

        def whole_and_rest(half):
            head, groups = SETS[half][0][0], SETS[half]
            whole = sum(n == GROUP for _, n in groups)
            parts = [(slice(head, head + whole * GROUP), 0, whole, GROUP)]
            if whole < len(groups):
                parts.append((slice(groups[whole][0], groups[whole][0] + groups[whole][1]), whole, 1, groups[whole][1]))
            return parts

        for b in range(BATCH):
            if b:
                stacks.fill_next(core, b)
            else:
                stacks.fill_first(core, q_t, k_t)
            with nc.Block() as block:
                @block.tensor
                def _(pe):
                    def tile(t, first):
                        for half in range(2):
                            if not first:
                                pe.wait_ge(tops.handle, tops.done + t * 2 + half - 1)
                            banded(q_s[0:MAX_ROWS], k_s[0:MAX_ROWS], t * P, t * P, core.mask("band_q")[:, bass.ds(t * BAND, BAND)],
                                   half, 3 * half).then_inc(max_scores.handle, 1)
                    tile(0, True)
                    with pe.Fori(1, T) as t:
                        tile(t, False)
                    need(pe, tops, 2 * T)
                    nc.tensor.transpose(psum[:, 6, 0:P], top[:].rearrange("p h t -> p (h t)"), core.ident[:]).then_inc(tops_turned.handle, 1)

                @block.vector
                def _(dve):
                    with dve.Fori(0, T) as t:
                        for half in range(2):
                            dve.wait_ge(max_scores.handle, max_scores.done + t * 2 + half + 1)
                            for heads, bank, banks, n in whole_and_rest(half):
                                last = nc.vector.tensor_reduce(top[:, heads, bass.ds(t, 1)].rearrange("p (g h) o -> p g (h o)", g=banks),
                                                               psum[:, 3 * half + bank:3 * half + bank + banks, 0:n * BAND].rearrange("p g (h k) -> p g h k", k=BAND),
                                                               AX.X, ALU.max, negate=True)
                            last.then_inc(tops.handle, 1)
                    link = Steps(dve, chain)
                    need(dve, tops_turned, 1)
                    link(nc.vector.tensor_copy(rows[:, 0, :], psum[:, 6, 0:P]))
                    nc.vector.tensor_tensor(rows[:, 1, :], psum[:, 6, 0:P], rows[:, 0, :], ALU.subtract).then_inc(rows_ready.handle, 1)
                    link.close()

                @block.sync
                def _(sp):
                    need(sp, rows_ready, 1)
                    sp.dma_start(max_dram.rearrange("i h (t p) -> (h t) i p", p=P), rows[:]).then_inc(rows_stored.handle, 16)
                    need(sp, rows_stored, 16)
                    sp.dma_start(stacks.q[MAX_ROWS:MAX_ROWS + 2, :, 0:SEQ], max_dram).then_inc(rows_placed.handle, 16)
                    need(sp, rows_placed, 16)
            for tally, n in ((max_scores, 2 * T), (tops, 2 * T), (tops_turned, 1), (rows_ready, 1), (rows_stored, 16), (rows_placed, 16)):
                tally.done += n
            with nc.Block() as block:
                @block.tensor
                def _(pe):
                    def scores_of(t, first):
                        for half in range(2):
                            if not first:
                                pe.wait_ge(probs.handle, probs.done + t * 2 + half - 1)
                            banded(k_s, q_s, t * P + W, t * P, core.mask("band_k"), half, 3 * half).then_inc(scores.handle, 1)

                    def sums_of(t, p, first, last_tile):
                        pe.wait_ge(v_staged.handle, v_staged.done + t + 1)
                        pe.wait_ge(probs.handle, probs.done + t * 2 + 2)
                        for j in range(QUADS):
                            for c in range(4):
                                last = nc.tensor.matmul(psum[COLS * c:COLS * (c + 1), 6 + p, j * P:(j + 1) * P], tile_v[:, p, 4 * j + c, :],
                                                        prob[:, p, 4 * j + c, 0:P], start=(first and j == 0), stop=(j == QUADS - 1),
                                                        tile_position=(0, COLS * c), skip_group_check=True)
                        last.then_inc(sums_made.handle, 1)
                        if last_tile:
                            return
                        if not first:
                            pe.wait_ge(normed.handle, normed.done + t)
                        for j in range(QUADS):
                            for c in range(4):
                                last = nc.tensor.matmul(psum[COLS * c:COLS * (c + 1), 7 - p, j * P:j * P + W], tile_v[:, p, 4 * j + c, :],
                                                        prob[:, p, 4 * j + c, P:BAND], start=(j == 0), stop=False,
                                                        tile_position=(0, COLS * c), skip_group_check=True)
                        last.then_inc(v_used.handle, 1)

                    def turn(t, p):
                        pe.wait_ge(sums_taken.handle, sums_taken.done + t + 1)
                        for j in range(QUADS):
                            last = nc.tensor.transpose(psum[:, 6 + p, j * P:(j + 1) * P], sums[:, j * P:(j + 1) * P], core.ident[:])
                        last.then_inc(sums_turned.handle, 1)

                    scores_of(0, True)
                    sums_of(0, 0, True, False)
                    scores_of(1, False)
                    turn(0, 0)
                    sums_of(1, 1, False, False)
                    with pe.Fori(1, T // 2 - 1) as i:
                        for p in range(2):
                            scores_of(i * 2 + p, False)
                            turn(i * 2 + p - 1, 1 - p)
                            sums_of(i * 2 + p, p, False, False)
                    for t in (T - 2, T - 1):
                        scores_of(t, False)
                        turn(t - 1, (t - 1) % 2)
                        sums_of(t, t % 2, False, t == T - 1)
                    turn(T - 1, (T - 1) % 2)

                @block.scalar
                def _(act):
                    def exp(t, p, first):
                        for half in range(2):
                            act.wait_ge(scores.handle, scores.done + t * 2 + half + 1)
                            if not first and half == 0:
                                act.wait_ge(v_used.handle, v_used.done + t - 1)
                            for heads, bank, banks, n in whole_and_rest(half):
                                last = nc.scalar.activation(prob[:, p, heads, :].rearrange("p (g h) k -> p g (h k)", g=banks),
                                                            psum[:, 3 * half + bank:3 * half + bank + banks, 0:n * BAND], ACT.Exp,
                                                            scale=float(D) ** -0.5)
                            last.then_inc(probs.handle, 1)

                    def take(t, p, first):
                        act.wait_ge(sums_made.handle, sums_made.done + t + 1)
                        if not first:
                            act.wait_ge(sums_turned.handle, sums_turned.done + t)
                        nc.scalar.copy(sums[:], psum[:, 6 + p, :]).then_inc(sums_taken.handle, 1)

                    exp(0, 0, True)
                    take(0, 0, True)
                    exp(1, 1, True)
                    take(1, 1, False)
                    with act.Fori(1, T // 2) as i:
                        for p in range(2):
                            exp(i * 2 + p, p, False)
                            take(i * 2 + p, p, False)

                @block.vector
                def _(dve):
                    with dve.Fori(0, T // 2) as i:
                        link = Steps(dve, chain, 2, i)
                        for p in range(2):
                            dve.wait_ge(sums_turned.handle, sums_turned.done + i * 2 + p + 1)
                            got = psum[:, 6 + p, :].rearrange("p (h e) -> p h e", e=COLS)
                            link(nc.vector.reciprocal(rec[:], got[:, :, D]))
                            nc.vector.tensor_tensor(o[:].rearrange("p t (h d) -> p t h d", h=H)[:, bass.ds(b * T + i * 2 + p, 1)],
                                                    got[:, :, 0:D].unsqueeze(1),
                                                    rec[:].unsqueeze(1).unsqueeze(3).to_broadcast([P, 1, H, D]), ALU.mult).then_inc(normed.handle, 1)
                            dve.wait_ge(normed.handle, normed.done + i * 2 + p + 1)
                    link.close(T // 2)

                @block.gpsimd
                def _(pool):
                    def stage(t, p):
                        nc.gpsimd.tensor_copy(tile_v[:, p, :, 0:D + 1].unsqueeze(1), v[:, bass.ds(b * T + t, 1), :, :]).then_inc(v_staged.handle, 1)
                    stage(0, 0)
                    stage(1, 1)
                    with pool.Fori(1, T // 2) as i:
                        for p in range(2):
                            pool.wait_ge(v_used.handle, v_used.done + i * 2 + p - 1)
                            stage(i * 2 + p, p)
            for tally, n in ((scores, 2 * T), (probs, 2 * T), (sums_made, T), (v_used, T - 1), (v_staged, T), (sums_taken, T), (sums_turned, T), (normed, T)):
                tally.done += n
        normalise_block(core, x, o, 1e-5, plain(core), only_transpose=True)
        tokens_product(core, w("wout"), add_to_x(core, also=y))



def l3_attn(core, area):
    nc, psum, x, y, zt = core.nc, core.psum, core.x, core.y, core.zt
    w = core.weights(area, L3_ATTN)
    L, S = RA_STEP, RA_SEG
    K = 3
    chain, made, taken = core.sem("vector_chain"), core.sem("ra_product"), core.sem("ra_activated")
    with ExitStack() as ctx:
        sb = lambda name, shape, dt=F32: ctx.enter_context(nc.sbuf_tensor(core.fresh(name), shape, dt))
        normalise_block(core, x, y, 1e-5, plain(core))
        q, k, v, g, beta = (sb(n, [P, TOKENS]) for n in ("ra_q", "ra_k", "ra_v", "ra_g", "ra_beta"))
        decay = sb("ra_decay_gates", [P, 2, TOKENS])
        runs = [("wq", q[:], ACT.Silu, None), ("wk", k[:], ACT.Silu, None), ("wv", v[:], ACT.Silu, None),
                ("wg", g[:], ACT.Sigmoid, None), ("wb", beta[:], ACT.Sigmoid, None),
                ("wfd", decay[:, 0, :], ACT.Sigmoid, "bfd"), ("wsd", decay[:, 1, :], ACT.Sigmoid, "bsd")]
        N = len(runs)
        with nc.Block() as block:
            @block.tensor
            def _(pe):
                for r, (name, _, _, _) in enumerate(runs):
                    for c in range(CHUNKS):
                        n = r * CHUNKS + c
                        if n >= 4:
                            need(pe, taken, n - 3)
                        nc.tensor.matmul(psum[:, n % 4, :], w(name), zt[:, c * CHUNK:(c + 1) * CHUNK],
                                         start=True, stop=True).then_inc(made.handle, 1)

            @block.scalar
            def _(act):
                for r, (_, out, func, bias) in enumerate(runs):
                    for c in range(CHUNKS):
                        n = r * CHUNKS + c
                        need(act, made, n + 1)
                        nc.scalar.activation(out[:, c * CHUNK:(c + 1) * CHUNK], psum[:, n % 4, :], func,
                                             bias=0.0 if bias is None else w(bias)).then_inc(taken.handle, 1)

            @block.vector
            def _(dve):
                link = Steps(dve, chain)
                need(dve, taken, 3 * CHUNKS)
                link(nc.vector.scalar_tensor_tensor(out=k[:], in0=k[:], scalar=1.0 + RA_MIX, in1=v[:], op0=ALU.mult, op1=ALU.mult))
                need(dve, taken, 4 * CHUNKS)
                nc.vector.scalar_tensor_tensor(out=q[:], in0=q[:], scalar=0.5, in1=g[:], op0=ALU.mult, op1=ALU.mult)
                need(dve, taken, 5 * CHUNKS)
                link(nc.vector.tensor_tensor(k[:], k[:], beta[:], ALU.mult))
                link.close()
        made.done += N * CHUNKS
        taken.done += N * CHUNKS

        states, faded = sb("ra_states", [P, 2, K, S]), sb("ra_faded", [P, 2, K, S])
        read = sb("ra_read", [P, K, S, L])
        starts = sb("ra_starts", [P, 2, S])
        piece = sb("ra_piece", [P, 2, 2, BATCH])
        seg = S // BATCH
        state2 = lambda t: t[:].rearrange("p a k s -> p a (k s)")
        u = k[:].rearrange("p (s l) -> p s l", l=L)
        fades = decay[:].rearrange("p a (s l) -> p a s l", l=L)
        with nc.Block() as block:
            @block.vector
            def _(dve):
                link = Steps(dve, chain)
                link(nc.vector.memset(states[:], 0.0))
                nc.vector.memset(states[:, 0, 1, :], 1.0)
                nc.vector.memset(starts[:], 0.0)
                link(nc.vector.memset(states[:, 1, 2, :], 1.0))
                link.close()
                with dve.Fori(0, L) as t:
                    link = Steps(dve, chain, 3, t)
                    link(nc.vector.tensor_tensor(faded[:], states[:],
                                                 fades[:, :, :, bass.ds(t, 1)].rearrange("p a s l -> p a (s l)").unsqueeze(2)
                                                 .to_broadcast([P, 2, K, S]), ALU.mult))
                    nc.vector.tensor_tensor(read[:, :, :, bass.ds(t, 1)].rearrange("p k s l -> p k (s l)"), faded[:, 0], faded[:, 1], ALU.add)
                    link(nc.vector.scalar_tensor_tensor(out=state2(states), in0=state2(faded)[:, ::-1, :], scalar=RA_MIX,
                                                        in1=state2(faded), op0=ALU.mult, op1=ALU.add))
                    link(nc.vector.tensor_tensor(states[:, :, 0, :], states[:, :, 0, :],
                                                 u[:, :, bass.ds(t, 1)].rearrange("p s l -> p (s l)").unsqueeze(1).to_broadcast([P, 2, S]),
                                                 ALU.add))
                link.close(L)
                ends = states[:].rearrange("p a k (b c) -> p a k b c", b=BATCH)
                at = starts[:, :, 0:S].rearrange("p k (b c) -> p k b c", b=BATCH)
                with dve.Fori(0, seg - 1) as c:
                    link = Steps(dve, chain, 4, c)
                    for a in range(2):
                        last = nc.vector.tensor_tensor(piece[:, a], ends[:, a, 1:3, :, bass.ds(c, 1)].rearrange("p k b c -> p k (b c)"),
                                                       at[:, :, :, bass.ds(c, 1)].rearrange("p k b c -> p k (b c)"), ALU.mult)
                        link(last)
                    link(nc.vector.tensor_tensor(piece[:, :, 0, :], piece[:, :, 0, :], piece[:, :, 1, :], ALU.add))
                    link(nc.vector.tensor_tensor(at[:, :, :, bass.ds(c + 1, 1)].rearrange("p k b c -> p k (b c)"), piece[:, :, 0, :],
                                                 ends[:, :, 0, :, bass.ds(c, 1)].rearrange("p a b c -> p a (b c)"), ALU.add))
                link.close(seg - 1)
                link = Steps(dve, chain)
                flat = lambda t: t.rearrange("p s l -> p (s l)")
                for a in range(2):
                    link(nc.vector.tensor_tensor(read[:, 1 + a], read[:, 1 + a], starts[:, a, 0:S].unsqueeze(2).to_broadcast([P, S, L]), ALU.mult))
                link(nc.vector.tensor_tensor(read[:, 0], read[:, 0], read[:, 1], ALU.add))
                link(nc.vector.tensor_tensor(read[:, 0], read[:, 0], read[:, 2], ALU.add))
                link(nc.vector.tensor_tensor(zt[:, 0:TOKENS], flat(read[:, 0]), q[:], ALU.mult))
                link.close()
        tokens_product(core, w("wo"), add_to_x(core))


def fetch(core, area, source):
    ready = core.sem(f"weights_{'ab'[area]}_arrived")
    with core.nc.Block() as block:
        @block.sync
        def _(sp):
            sp.dma_start(core.areas[area][:, 0:source.shape[1]], source).then_inc(ready.handle, 16)
    ready.done += 16


def arrived(core, area):
    ready = core.sem(f"weights_{'ab'[area]}_arrived")
    with core.nc.Block() as block:
        @block.sync
        def _(sp):
            sp.wait_ge(ready.handle, ready.done)


STAGES = [("L0_ffn", l0_ffn, 0), ("L0_attn", l0_attn, 1), ("L0_ffn", l0_ffn, 0),
          ("L1_ffn", ternary_ffn, 1), ("L1_attn", l1_attn, 0), ("L1_ffn", ternary_ffn, 1),
          ("L2_ffn", l2_ffn, 0), ("L2_attn", l2_attn, 1), ("L2_ffn", l2_ffn, 0),
          ("L3_ffn", ternary_ffn, 1), ("L3_attn", l3_attn, 0), ("L3_ffn", ternary_ffn, 1)]


def macaron_d4(nc, x_in, blobs, out, stages=STAGES):
    with ExitStack() as ctx:
        core = Core(nc, ctx)
        loaded = core.sem("inputs_arrived")
        stored = core.sem("output_stored")
        half = core.sem("constants_set")
        with nc.Block() as block:
            @block.sync
            def _(sp):
                sp.dma_start(core.x[:], x_in.rearrange("b (i p) d -> p (b i) d", p=P)).then_inc(loaded.handle, 16)
                sp.dma_start(core.ident[:], blobs["constants"]).then_inc(loaded.handle, 16)
                sp.wait_ge(loaded.handle, 32)

            @block.gpsimd
            def _(pool):
                pool.dma_start(core.masks[:], blobs["masks"]).then_inc(core.sem("masks_arrived").handle, 16)
                nc.gpsimd.memset(core.minus_half[:], -0.5).then_inc(half.handle, 1)
                nc.gpsimd.memset(core.zt[:], 0.0).then_inc(half.handle, 1)
                pool.wait_ge(core.sem("masks_arrived").handle, 16)
        held = [None, None]

        def fetch_for(n):
            name, _, area = stages[n]
            if held[area] != name:
                fetch(core, area, blobs[name])
                held[area] = name
        fetch_for(0)
        for n, (_, stage, area) in enumerate(stages):
            if n + 1 < len(stages) and stages[n + 1][2] != area:
                fetch_for(n + 1)
            arrived(core, area)
            stage(core, area)
            if n + 1 < len(stages) and stages[n + 1][2] == area:
                fetch_for(n + 1)
        with nc.Block() as block:
            @block.sync
            def _(sp):
                sp.dma_start(out.rearrange("b (i p) d -> p (b i) d", p=P), core.x[:]).then_inc(stored.handle, 16)
                sp.wait_ge(stored.handle, 16)


def _pack(layout, arrays):
    import numpy as np
    cols = []
    for name, n in layout:
        a = arrays[name]
        a = a.reshape(a.shape[0], -1)
        assert a.shape[1] == n, (name, a.shape, n)
        if a.shape[0] < 128:
            a = np.concatenate([a, np.zeros((128 - a.shape[0], n), a.dtype)])
        cols.append(a)
    return np.ascontiguousarray(np.concatenate(cols, axis=1))


def _rows(w, part=128):
    import numpy as np
    n = -(-w.shape[0] // part)
    w = np.concatenate([w, np.zeros((n * part - w.shape[0], w.shape[1]), w.dtype)])
    return w.reshape(n, part, w.shape[1]).transpose(1, 0, 2).reshape(part, -1)


def _all_rows(v):
    import numpy as np
    return np.broadcast_to(v[None, :], (128, v.shape[0]))


def _tables():
    import numpy as np
    f = np.float32
    out = {}
    t = np.arange(1024, dtype=f)
    hi = np.arange(0, 64, 2, dtype=f)
    inv = (f(1.0) / f(10000.0) ** (hi / f(64))).astype(f)
    fr = (t[:, None] * inv[None, :]).astype(f)
    fr = np.concatenate([fr, fr], -1)
    base = ((hi + f(0.4 * 64)) / f(1.4 * 64)).astype(f)
    power = ((t - 512) / f(32)).astype(f)
    scale = (base[None, :] ** power[:, None]).astype(f)
    scale = np.concatenate([scale, scale], -1)
    cos, sin = np.cos(fr), np.sin(fr)
    sign = np.concatenate([-np.ones(32, f), np.ones(32, f)])
    tok = lambda a: a.astype(f).reshape(8, 128, 64).transpose(1, 0, 2).reshape(128, -1)
    out["xpos"] = {"cq": tok(cos * scale), "sq": tok(sin * scale * sign), "ck": tok(cos / scale), "sk": tok(sin / scale * sign)}
    inv = (f(1.0) / f(10000.0) ** (np.arange(8, dtype=f) / f(8))).astype(f)
    fr = (t[:, None] * inv[None, :]).astype(f)
    c = np.zeros((4, 32, 1024), f)
    s = np.zeros((4, 32, 1024), f)
    c[:, :8] = c[:, 8:16] = np.cos(fr).T
    s[:, :8], s[:, 8:16] = -np.sin(fr).T, np.sin(fr).T
    out["ga"] = (c.reshape(128, 1024), s.reshape(128, 1024))
    inv = (f(1.0) / f(10000.0) ** (np.arange(0, 8, 2, dtype=f) / f(8))).astype(f)
    fr = (t[:, None] * inv[None, :]).astype(f)
    c8 = np.repeat(np.cos(fr), 2, -1).T
    s8 = np.repeat(np.sin(fr), 2, -1).T * np.array([-1] * 4 + [1] * 4, f)[:, None]
    out["fa"] = (np.tile(c8, (16, 1)).astype(f), np.tile(s8, (16, 1)).astype(f))
    off = f(-1e30)
    q, k = np.arange(64)[:, None], np.arange(128)[None, :]
    local = np.where((k >= q) & (k <= q + 64), f(0), off).astype(f)
    first = np.where(k < 64, off, local).astype(f)
    masks = np.zeros((128, 16, 128), f)
    for i in range(16):
        masks[:64, i] = first if i % 8 == 0 else local
        masks[64:, i] = local
    j, i = np.arange(128)[:, None], np.arange(128)[None, :]
    causal = np.where(j <= i, f(0), off).astype(f)
    q, k = np.arange(128)[:, None], np.arange(160)[None, :] - 32
    band_q = np.where((k <= q) & (k >= q - 32), f(0), off).astype(f)
    band_q0 = np.where((k <= q) & (k >= q - 32) & (k >= 0), f(0), off).astype(f)
    k, q = np.arange(128)[:, None], np.arange(160)[None, :]
    band_qs = np.concatenate([band_q0] + [band_q] * 7, 1)
    band_k = np.where((k <= q) & (k >= q - 32), f(0), off).astype(f)
    out["masks"] = {"ident": np.eye(128, dtype=f), "local": masks.reshape(128, -1), "causal": causal,
                    "band_q": band_qs, "band_k": band_k}
    out["upper"] = (j <= i).astype(f)
    d = (np.arange(128)[:, None] // 32 == np.arange(64)[None, :] // 16).astype(f)
    out["diag"] = np.concatenate([d, d], 1)
    return out


def _blobs(a):
    import numpy as np
    tb = _tables()
    parts = {}
    r = {}
    for l in range(2):
        w1, w2, b1 = a["L0_ffn_w1"][l], a["L0_ffn_w2"][l], a["L0_ffn_b1"][l]
        col = lambda b: _rows(b[:, None])
        qs, ks = a["L0_ffn_q_scale"][l], a["L0_ffn_k_scale"][l]
        r.update({f"wqkv{l}": a["L0_ffn_wqkv"][l], f"wo{l}": _rows(a["L0_ffn_wo"][l]), f"w1{l}": w1, f"w2{l}": _rows(w2),
                  f"qs{l}": _all_rows(qs), f"ks{l}": _all_rows(ks), f"lg{l}": a["L0_ffn_ln_g"][l][:, None],
                  f"lb{l}": a["L0_ffn_ln_b"][l][:, None], f"b1a{l}": col(b1[:341]), f"b1g{l}": col(b1[341:]),
                  f"b2{l}": _all_rows(a["L0_ffn_b2"][l])})
    r.update(tb["xpos"])
    parts["L0_ffn"] = r

    def spaced(w, swap=False):
        w = w.reshape(8, 16, 128)
        if swap:
            w = np.concatenate([w[:, 8:], w[:, :8]], 1)
        w = np.concatenate([w, np.zeros_like(w)], 1).reshape(256, 128)
        return w.T
    A = "L0_attn_"
    parts["L0_attn"] = {"wq": spaced(a[A + "Wq"]), "wqs": spaced(a[A + "Wq"], True), "wk": spaced(a[A + "Wk"]),
                        "wks": spaced(a[A + "Wk"], True),
                        "wvg": np.concatenate([a[A + "Wv"], a[A + "Wbeta"], a[A + "Wig"], a[A + "Wog"]]).T,
                        "wout": a[A + "Wout"].T, "bg": _all_rows(np.concatenate([a[A + "bbeta"], a[A + "big"], a[A + "bog"]])),
                        "bout": _all_rows(a[A + "bout"]), "nw": a[A + "norm_w"][:, None],
                        "cos": tb["ga"][0], "sin": tb["ga"][1], "upper": tb["upper"], "diag": tb["diag"]}
    for L in ("L1_ffn", "L3_ffn"):
        g = lambda n: a[f"{L}_{n}"]
        col = lambda v: _rows(v[:, None])
        parts[L] = {"w1": g("w1_w").T, "w2": g("w2_w").T, "h1": _rows(g("h1_w").T), "h2": _rows(g("h2_w").T),
                    "w3": _rows(g("w3_w").T), "s1": col(g("w1_s")), "s2": col(g("w2_s")), "t1": col(g("h1_s")),
                    "t2": col(g("h2_s")), "s3": _all_rows(g("w3_s"))}
    swap8 = lambda w: w.reshape(16, 2, 4, -1)[:, ::-1].reshape(128, -1)
    A = "L1_attn_"
    parts["L1_attn"] = {"wq": a[A + "wq"].T, "wqs": swap8(a[A + "wq"]).T, "wk": a[A + "wk"].T, "wks": swap8(a[A + "wk"]).T,
                        "wv": a[A + "wv"].T, "wo": a[A + "wo"].T, "bq": a[A + "bq"][:, None], "bqs": swap8(a[A + "bq"]),
                        "bk": a[A + "bk"][:, None], "bks": swap8(a[A + "bk"]), "bv": _all_rows(a[A + "bv"]),
                        "bo": _all_rows(a[A + "bo"]), "cos": tb["fa"][0], "sin": tb["fa"][1]}
    parts["L2_ffn"] = {"wg": _rows(a["L2_ffn_w_gate"]), "wu": _rows(a["L2_ffn_w_up"]), "wd": a["L2_ffn_w_down"]}
    W = a["L2_attn_W_qkv"]
    parts["L2_attn"] = {"wq": W[:128].T, "wk": W[128:256].T, "wv": W[256:].T, "wout": a["L2_attn_W_out"].T,
                        "gamma": a["L2_attn_gamma"][:, None], "beta": a["L2_attn_beta"][:, None]}
    A = "L3_attn_"
    rep = lambda w: np.repeat(w, 8, axis=0)
    parts["L3_attn"] = {"wq": a[A + "Wq"].T, "wk": a[A + "Wk"].T, "wv": a[A + "Wv"].T, "wg": a[A + "Wg"].T,
                        "wb": rep(a[A + "Wb"]).T, "wfd": rep(a[A + "Wfd"]).T, "wsd": rep(a[A + "Wsd"]).T,
                        "wo": a[A + "Wo"].T, "bfd": rep(a[A + "bfd"])[:, None], "bsd": rep(a[A + "bsd"])[:, None]}
    blobs = {name: _pack(LAYOUTS[name], parts[name]) for name in LAYOUTS}
    blobs["constants"] = np.eye(128, dtype=np.float32)
    blobs["masks"] = _pack(MASKS, tb["masks"])
    return blobs


def kernel(**inputs):
    import numpy as _np
    import concourse.bacc as _bacc
    from concourse import mybir as _mybir
    from concourse.bass_utils import run_bass_kernel_spmd as _run

    nc = _bacc.Bacc("TRN2", target_bir_lowering=False, num_devices=1)
    given = {k: _np.asarray(v) for k, v in inputs.items()}
    arrays = {"in_x": _np.ascontiguousarray(given["L0_attn_x"])}
    arrays.update({f"in_{k}": v for k, v in _blobs(given).items()})
    args = {k: nc.dram_tensor(k, v.shape, _mybir.dt.from_np(v.dtype), kind="ExternalInput").ap() for k, v in arrays.items()}
    out = nc.dram_tensor("out_x", (BATCH, SEQ, P), F32, kind="ExternalOutput").ap()
    macaron_d4(nc, args["in_x"], {k[3:]: v for k, v in args.items()}, out)
    r = _run(nc, [arrays], core_ids=[0])
    return r.results[0]["out_x"]
```

```python
from contextlib import ExitStack

import concourse.bass as bass
from concourse import mybir

ALU = mybir.AluOpType
ACT = mybir.ActivationFunctionType
AX = mybir.AxisListType
F32 = mybir.dt.float32
BF16 = mybir.dt.bfloat16

P = 128
BATCH, SEQ = 2, 1024
TOKENS = BATCH * SEQ
TILES = TOKENS // P
SEQ_TILES = SEQ // P
CHUNK = 512
CHUNKS = TOKENS // CHUNK
PER_CHUNK = CHUNK // P
BANK = 512

LA_HEADS, LA_DIM, LA_WIN = 8, 64, 64
LA_INNER = LA_HEADS * LA_DIM
GLU_HID = 341
GLU_PARTS = [(m * P, min(P, GLU_HID - m * P)) for m in range(-(-GLU_HID // P))]
TF_HID = 512
TF_PARTS = TF_HID // P
GA_HEADS, GA_DIM = 8, 16
FA_HEADS, FA_DIM = 16, 8
WA_WIN = 32
BAND = P + WA_WIN
Q4_HID, Q4_BLOCK = 352, 16
Q4_PARTS = [(m * P, min(P, Q4_HID - m * P)) for m in range(-(-Q4_HID // P))]
RA_MIX = 0.05
RA_STEP = 32
RA_SEG = TOKENS // RA_STEP

L0_FFN = []
for _l in range(2):
    L0_FFN += [(f"wqkv{_l}", 3 * LA_INNER), (f"wo{_l}", LA_INNER), (f"w1{_l}", 2 * GLU_HID),
               (f"w2{_l}", len(GLU_PARTS) * P), (f"qs{_l}", LA_DIM), (f"ks{_l}", LA_DIM),
               (f"lg{_l}", 1), (f"lb{_l}", 1), (f"b1a{_l}", len(GLU_PARTS)), (f"b1g{_l}", len(GLU_PARTS)),
               (f"b2{_l}", P)]
L0_FFN += [("cq", SEQ_TILES * LA_DIM), ("ck", SEQ_TILES * LA_DIM),
           ("sq", SEQ_TILES * LA_DIM), ("sk", SEQ_TILES * LA_DIM)]
L0_ATTN = [("wq", 256), ("wqs", 256), ("wk", 256), ("wks", 256), ("wvg", P + 3 * GA_HEADS),
           ("wout", P), ("bg", 3 * GA_HEADS), ("bout", P), ("nw", 1), ("cos", SEQ), ("sin", SEQ), ("upper", P),
           ("diag", 2 * 64)]
TERNARY = [("w1", TF_HID), ("w2", TF_HID), ("h1", TF_PARTS * TF_HID), ("h2", TF_PARTS * TF_HID),
           ("w3", TF_PARTS * P), ("s1", TF_PARTS), ("s2", TF_PARTS), ("t1", TF_PARTS), ("t2", TF_PARTS), ("s3", P)]
L1_ATTN = [("wq", P), ("wqs", P), ("wk", P), ("wks", P), ("wv", P), ("wo", P), ("bq", 1), ("bqs", 1),
           ("bk", 1), ("bks", 1), ("bv", P), ("bo", P), ("cos", SEQ), ("sin", SEQ)]
L2_FFN = [("wg", 3 * P), ("wu", 3 * P), ("wd", Q4_HID)]
L2_ATTN = [("wq", P), ("wk", P), ("wv", P), ("wout", P), ("gamma", 1), ("beta", 1)]
L3_ATTN = [("wq", P), ("wk", P), ("wv", P), ("wg", P), ("wb", P), ("wfd", P), ("wsd", P), ("wo", P),
           ("bfd", 1), ("bsd", 1)]
MASKS = [("ident", P), ("local", TILES * P), ("causal", P), ("band_q", SEQ_TILES * BAND), ("band_k", BAND)]
L2_FFN_HELD = sum(n for _, n in L2_FFN) + 2 * Q4_HID + len(Q4_PARTS) * P
AREA_A = sum(n for _, n in L0_FFN)
AREA_B = sum(n for _, n in TERNARY)
LAYOUTS = {"L0_ffn": L0_FFN, "L0_attn": L0_ATTN, "L1_ffn": TERNARY, "L1_attn": L1_ATTN, "L2_ffn": L2_FFN,
           "L2_attn": L2_ATTN, "L3_ffn": TERNARY, "L3_attn": L3_ATTN}


def columns(layout):
    at, out = 0, {}
    for name, n in layout:
        out[name] = (at, n)
        at += n
    return out


class Tally:

    def __init__(self, handle):
        self.handle, self.done = handle, 0


class Steps:

    def __init__(self, engine, tally, per_turn=0, turn=None):
        self.engine, self.tally, self.per_turn, self.made = engine, tally, per_turn, 0
        self.start = tally.done if turn is None else tally.done + turn * per_turn

    def __call__(self, instruction):
        self.made += 1
        instruction.then_inc(self.tally.handle, 1)
        self.engine.wait_ge(self.tally.handle, self.start + self.made)

    def close(self, turns=1):
        assert not self.per_turn or self.made == self.per_turn, self.made
        self.tally.done += self.made * turns


class Core:

    def __init__(self, nc, ctx):
        self.nc, self.ctx, self.tallies, self.made = nc, ctx, {}, 0
        self.weights_quantised = False
        sb = lambda name, shape, dt=F32: ctx.enter_context(nc.sbuf_tensor(name, shape, dt))
        self.x = sb("x", [P, TILES, P])
        self.y = sb("y", [P, TILES, P])
        self.zt = sb("zt", [P, 64 + TOKENS + 64])
        self.ident = sb("ident", [P, P])
        self.masks = sb("masks", [P, sum(n for _, n in MASKS)], BF16)
        self.stats = sb("stats", [P, TILES, 6])
        self.moments = sb("moments", [P, TILES, 2])
        self.spread = sb("spread", [P, TILES])
        self.rstd = sb("rstd", [P, TILES])
        self.minus_half = sb("minus_half", [P, TILES])
        self.areas = [sb("area_a", [P, AREA_A]), sb("area_b", [P, AREA_B])]
        self.psum = ctx.enter_context(nc.psum_tensor("psum", [P, 8, BANK], F32))
        self.mask_at = columns(MASKS)

    def sem(self, name):
        if name not in self.tallies:
            self.tallies[name] = Tally(self.ctx.enter_context(self.nc.semaphore(name)))
        return self.tallies[name]

    def fresh(self, name):
        self.made += 1
        return f"{name}_{self.made}"

    def mask(self, name):
        at, n = self.mask_at[name]
        return self.masks[:, at:at + n]

    def weights(self, area, layout):
        where = columns(layout)
        return lambda name: self.areas[area][:, where[name][0]:where[name][0] + where[name][1]]


def need(engine, tally, n):
    engine.wait_ge(tally.handle, tally.done + n)


def wait(engine, tally, count):
    if not isinstance(count, int) or count > 0:
        engine.wait_ge(tally.handle, tally.done + count)


def turns(engine, order):
    low, high = 2, TILES - 2
    first, last = -max(at for _, at in order), TILES - min(at for _, at in order)

    def turn(j):
        for step, at in order:
            if 0 <= j + at < TILES:
                step(engine, j + at, (j + at) % 2)
    for j in range(first, low):
        turn(j)
    with engine.Fori(low // 2, high // 2) as i:
        for parity in range(2):
            for step, at in order:
                step(engine, i * 2 + (parity + at), (parity + at) % 2)
    for j in range(high, last):
        turn(j)


def normalise_block(core, source, out, eps, evacuate=None, rms=False, only_transpose=False):
    nc, psum = core.nc, core.psum
    HALF = TILES // 2
    chain, spread_ready, done_pow, normed, turned, taken = (core.sem(n) for n in (
        "vector_chain", "spread_ready", "rstd_ready", "tile_normalised", "bank_transposed", "bank_evacuated"))
    with nc.Block() as block:
        if not only_transpose:
            @block.vector
            def _(dve):
                link = Steps(dve, chain)
                for h in range(2):
                    tiles = range(h * HALF, (h + 1) * HALF)
                    half = slice(h * HALF, (h + 1) * HALF)
                    for i in tiles:
                        last = nc.vector.bn_stats(core.stats[:, i, :], source[:, i, :])
                    link(last)
                    for i in tiles:
                        last = nc.vector.bn_aggr(core.moments[:, i, :], core.stats[:, i, :])
                    link(last)
                    if rms:
                        link(nc.vector.tensor_tensor(core.spread[:, half], core.moments[:, half, 0], core.moments[:, half, 0], ALU.mult))
                        link(nc.vector.tensor_tensor(core.spread[:, half], core.spread[:, half], core.moments[:, half, 1], ALU.add))
                        last = nc.vector.tensor_scalar(core.spread[:, half], core.spread[:, half], eps, None, ALU.add)
                    else:
                        last = nc.vector.tensor_scalar(core.spread[:, half], core.moments[:, half, 1], eps, None, ALU.add)
                    last.then_inc(spread_ready.handle, 1)
                link.close()
                for h in range(2):
                    need(dve, done_pow, h + 1)
                    for i in range(h * HALF, (h + 1) * HALF):
                        if rms:
                            nc.vector.tensor_scalar(out[:, i, :], source[:, i, :], core.rstd[:, i:i + 1], None,
                                                    ALU.mult).then_inc(normed.handle, 1)
                        else:
                            nc.vector.tensor_scalar(out[:, i, :], source[:, i, :], core.moments[:, i, 0:1],
                                                    core.rstd[:, i:i + 1], ALU.subtract, ALU.mult).then_inc(normed.handle, 1)

            @block.gpsimd
            def _(pool):
                for h in range(2):
                    half = slice(h * HALF, (h + 1) * HALF)
                    need(pool, spread_ready, h + 1)
                    nc.gpsimd.tensor_tensor(core.rstd[:, half], core.spread[:, half], core.minus_half[:, half],
                                            ALU.pow).then_inc(done_pow.handle, 1)

        if evacuate is None:
            @block.sync
            def _(sp):
                need(sp, normed, TILES)

        @block.tensor
        def _(pe):
            if evacuate is None:
                return
            for g in range(CHUNKS):
                if g >= 2:
                    need(pe, taken, g - 1)
                for j in range(PER_CHUNK):
                    if not only_transpose:
                        need(pe, normed, PER_CHUNK * g + j + 1)
                    last = nc.tensor.transpose(psum[:, g % 2, j * P:(j + 1) * P], out[:, PER_CHUNK * g + j, :], core.ident[:])
                last.then_inc(turned.handle, 1)

        @block.scalar
        def _(act):
            if evacuate is None:
                return
            for g in range(CHUNKS):
                need(act, turned, g + 1)
                for ins in evacuate(g, psum[:, g % 2, :]):
                    last = ins
                last.then_inc(taken.handle, 1)
    if not only_transpose:
        spread_ready.done += 2
        done_pow.done += 2
        normed.done += TILES
    if evacuate is not None:
        turned.done += CHUNKS
        taken.done += CHUNKS


def tokens_product(core, weights, take, offset=0):
    nc, psum, zt = core.nc, core.psum, core.zt
    made, taken, chain = core.sem("tokens_product"), core.sem("tokens_product_taken"), core.sem("vector_chain")
    width = weights.shape[1]
    per = BANK // width if BANK % width == 0 else 2
    banks = -(-PER_CHUNK // per)
    with nc.Block() as block:
        @block.tensor
        def _(pe):
            for g in range(CHUNKS):
                if g >= 2:
                    need(pe, taken, g - 1)
                for j in range(PER_CHUNK):
                    at = offset + (g * PER_CHUNK + j) * P
                    last = nc.tensor.matmul(psum[:, g % 2 * banks + j // per, j % per * width:(j % per + 1) * width],
                                            zt[:, at:at + P], weights, start=True, stop=True)
                last.then_inc(made.handle, 1)

        @block.vector
        def _(dve):
            link = Steps(dve, chain)
            for g in range(CHUNKS):
                need(dve, made, g + 1)
                got = psum[:, g % 2 * banks:(g % 2 + 1) * banks, 0:min(per, PER_CHUNK) * width].rearrange("p b (j n) -> p (b j) n", n=width) \
                    if per * width == BANK else psum[:, g % 2 * banks:(g % 2 + 1) * banks, 0:per * width].rearrange("p b (j n) -> p b j n", n=width)
                take(g, got, link).then_inc(taken.handle, 1)
            link.close()
    made.done += CHUNKS
    taken.done += CHUNKS


def add_to_x(core, bias=None, also=None):
    nc, x = core.nc, core.x

    def take(g, got, link):
        tiles = slice(g * PER_CHUNK, (g + 1) * PER_CHUNK)
        if bias is not None:
            link(nc.vector.tensor_tensor(x[:, tiles, :], x[:, tiles, :], bias.unsqueeze(1).to_broadcast([P, PER_CHUNK, P]), ALU.add))
        if also is not None:
            link(nc.vector.tensor_tensor(x[:, tiles, :], x[:, tiles, :], also[:, tiles, :], ALU.add))
        return nc.vector.tensor_tensor(x[:, tiles, :], got, x[:, tiles, :], ALU.add)
    return take


def rotated_product(core, pairs, cos, sin):
    nc, psum, zt = core.nc, core.psum, core.zt
    made, turned, chain = core.sem("rotary_product"), core.sem("rotary_taken"), core.sem("vector_chain")
    with ExitStack() as ctx:
        part_a = ctx.enter_context(nc.sbuf_tensor(core.fresh("rotary_a"), [P, 2, CHUNK], F32))
        part_b = ctx.enter_context(nc.sbuf_tensor(core.fresh("rotary_b"), [P, 2, CHUNK], F32))
        R = len(pairs)
        with nc.Block() as block:
            @block.tensor
            def _(pe):
                for n in range(CHUNKS * R):
                    _, wa, _, wb, _ = pairs[n % R]
                    if n >= 4:
                        need(pe, turned, n - 3)
                    at = n // R * CHUNK
                    for half, weights in enumerate((wa, wb)):
                        last = nc.tensor.matmul(psum[:, 2 * (n % 4) + half, :], weights, zt[:, at:at + CHUNK], start=True, stop=True)
                    last.then_inc(made.handle, 1)

            @block.vector
            def _(dve):
                link = Steps(dve, chain)
                for n in range(CHUNKS * R):
                    out, _, ba, _, bb = pairs[n % R]
                    need(dve, made, n + 1)
                    if n >= 2:
                        need(dve, turned, n - 1)
                    at = n // R * CHUNK % SEQ
                    for half, part, bias, table in ((0, part_a, ba, cos), (1, part_b, bb, sin)):
                        got = psum[:, 2 * (n % 4) + half, :]
                        if bias is None:
                            last = nc.vector.tensor_tensor(part[:, n % 2, :], got, table[:, at:at + CHUNK], ALU.mult)
                        else:
                            last = nc.vector.scalar_tensor_tensor(out=part[:, n % 2, :], in0=got, scalar=bias, in1=table[:, at:at + CHUNK],
                                                                  op0=ALU.add, op1=ALU.mult)
                    link(last)
                    at = n // R * CHUNK
                    nc.vector.tensor_tensor(out[:, at:at + CHUNK], part_a[:, n % 2, :], part_b[:, n % 2, :],
                                            ALU.add).then_inc(turned.handle, 1)
                link.close()
        made.done += R * CHUNKS
        turned.done += R * CHUNKS


def plain(core):
    def evacuate(g, bank):
        yield core.nc.scalar.copy(core.zt[:, g * CHUNK:(g + 1) * CHUNK], bank)
    return evacuate


def affine(core, scale, bias):
    def evacuate(g, bank):
        yield core.nc.scalar.activation(core.zt[:, g * CHUNK:(g + 1) * CHUNK], bank, ACT.Identity, bias=bias, scale=scale)
    return evacuate


def ternary_ffn(core, area):
    nc, psum, x, zt = core.nc, core.psum, core.x, core.zt
    w = core.weights(area, TERNARY)
    normalise_block(core, x, core.y, 1e-5, plain(core))
    up, silu, gated, hid, acted, low, added = (core.sem(n) for n in (
        "tf_up_product", "tf_silu", "tf_gated", "tf_hidden_product", "tf_gelu", "tf_out_product", "tf_added"))
    chain = core.sem("vector_chain")
    M = TF_PARTS
    with ExitStack() as ctx:
        sb = lambda name, shape: ctx.enter_context(nc.sbuf_tensor(core.fresh(name), shape, F32))
        ha, hb = sb("hidden_a", [P, 2, M, CHUNK]), sb("hidden_b", [P, 2, M, CHUNK])
        gate, scaled = sb("gate", [P, 2, CHUNK]), sb("scaled", [P, PER_CHUNK, P])
        with nc.Block() as block:
            @block.tensor
            def _(pe):
                with pe.Fori(0, CHUNKS // 2) as i:
                    for c in range(2):
                        for m in range(M):
                            n = c * M + m
                            if n >= 2:
                                pe.wait_ge(gated.handle, gated.done + i * 2 * M + n - 1)
                            tokens = zt[:, bass.ds(i * 2 * CHUNK + c * CHUNK, CHUNK)]
                            nc.tensor.matmul(psum[:, n % 2, :], w("w1")[:, m * P:(m + 1) * P], tokens, start=True, stop=True)
                            nc.tensor.matmul(psum[:, 2 + n % 2, :], w("w2")[:, m * P:(m + 1) * P], tokens,
                                             start=True, stop=True).then_inc(up.handle, 1)
                    for step, (name, src) in enumerate((("h1", ha), ("h2", hb))):
                        for c in range(2):
                            if step == 0:
                                pe.wait_ge(gated.handle, gated.done + i * 2 * M + (c + 1) * M)
                            else:
                                pe.wait_ge(acted.handle, acted.done + i * 4 * M + (c + 1) * M)
                            for m in range(M):
                                n = step * 2 * M + c * M + m
                                if n >= 2:
                                    pe.wait_ge(acted.handle, acted.done + i * 4 * M + n - 1)
                                for k in range(M):
                                    last = nc.tensor.matmul(psum[:, 4 + n % 2, :], w(name)[:, k * TF_HID + m * P:k * TF_HID + (m + 1) * P],
                                                            src[:, c, k, :], start=(k == 0), stop=(k == M - 1))
                                last.then_inc(hid.handle, 1)
                    for c in range(2):
                        pe.wait_ge(acted.handle, acted.done + i * 4 * M + (2 + c + 1) * M)
                        for j in range(PER_CHUNK):
                            for k in range(M):
                                last = nc.tensor.matmul(psum[:, 6 + c, j * P:(j + 1) * P], ha[:, c, k, j * P:(j + 1) * P],
                                                        w("w3")[:, k * P:(k + 1) * P], start=(k == 0), stop=(k == M - 1))
                        last.then_inc(low.handle, 1)
                    pe.wait_ge(added.handle, added.done + (i + 1) * 2)

            @block.scalar
            def _(act):
                with act.Fori(0, CHUNKS // 2) as i:
                    for n in range(2 * M):
                        act.wait_ge(up.handle, up.done + i * 2 * M + n + 1)
                        if n >= 2:
                            act.wait_ge(gated.handle, gated.done + i * 2 * M + n - 1)
                        nc.scalar.activation(gate[:, n % 2, :], psum[:, n % 2, :], ACT.Silu,
                                             scale=w("s1")[:, n % M:n % M + 1]).then_inc(silu.handle, 1)
                    for step, (dst, scale) in enumerate(((hb, "t1"), (ha, "t2"))):
                        for c in range(2):
                            for m in range(M):
                                n = step * 2 * M + c * M + m
                                act.wait_ge(hid.handle, hid.done + i * 4 * M + n + 1)
                                nc.scalar.activation(dst[:, c, m, :], psum[:, 4 + n % 2, :], ACT.Gelu,
                                                     scale=w(scale)[:, m:m + 1]).then_inc(acted.handle, 1)

            @block.vector
            def _(dve):
                with dve.Fori(0, CHUNKS // 2) as i:
                    link = Steps(dve, chain, 2, i)
                    for n in range(2 * M):
                        dve.wait_ge(silu.handle, silu.done + i * 2 * M + n + 1)
                        nc.vector.scalar_tensor_tensor(out=ha[:, n // M, n % M, :], in0=psum[:, 2 + n % 2, :],
                                                       scalar=w("s2")[:, n % M:n % M + 1], in1=gate[:, n % 2, :],
                                                       op0=ALU.mult, op1=ALU.mult).then_inc(gated.handle, 1)
                    for c in range(2):
                        dve.wait_ge(low.handle, low.done + i * 2 + c + 1)
                        link(nc.vector.tensor_tensor(scaled[:], psum[:, 6 + c, :].rearrange("p (j n) -> p j n", j=PER_CHUNK),
                                                     w("s3").unsqueeze(1).to_broadcast([P, PER_CHUNK, P]), ALU.mult))
                        tiles = x[:, bass.ds(i * 2 * PER_CHUNK + c * PER_CHUNK, PER_CHUNK), :]
                        nc.vector.scalar_tensor_tensor(out=tiles, in0=scaled[:], scalar=0.5, in1=tiles,
                                                       op0=ALU.mult, op1=ALU.add).then_inc(added.handle, 1)
                        dve.wait_ge(added.handle, added.done + i * 2 + c + 1)
                link.close(CHUNKS // 2)
        turns = CHUNKS // 2
        for tally, n in ((up, 2 * M), (silu, 2 * M), (gated, 2 * M), (hid, 4 * M), (acted, 4 * M), (low, 2), (added, 2)):
            tally.done += n * turns



def shifted(core):
    half, zt = P // 2, core.zt

    def evacuate(g, bank):
        at = 64 + g * CHUNK
        n = CHUNK - 1 if (g + 1) * CHUNK % SEQ == 0 else CHUNK
        yield core.nc.scalar.copy(zt[0:half, at:at + CHUNK], bank[0:half, :])
        yield core.nc.scalar.copy(zt[half:P, at + 1:at + 1 + n], bank[half:P, 0:n])
    return evacuate


def first_tokens(core):
    cleared = core.sem("first_token_cleared")
    with core.nc.Block() as block:
        @block.gpsimd
        def _(pool):
            for b in range(BATCH):
                core.nc.gpsimd.memset(core.zt[P // 2:P, 64 + b * SEQ:65 + b * SEQ], 0.0).then_inc(cleared.handle, 1)
    cleared.done += BATCH


def local_attention(core, w, layer):
    nc, psum, y, zt = core.nc, core.psum, core.y, core.zt
    H, D, W = LA_HEADS, LA_DIM, LA_WIN
    K = LA_INNER // P
    (staged, qk_made, v_made, squared, summed_squares, sums, norms, products, rotary_sums, rotated, qk_turned, window_moved, qk_taken,
     scores, tops, shifted_s, probs, p_turned, p_taken, v_taken, values, recs, o_ready, o_turned, o_taken, out_made,
     added, tables) = (
        core.sem("la_" + n) for n in (
            "tokens_staged", "qk_product", "v_product", "squared", "square_sums", "safe_square_sums", "norms", "rotary_products",
            "rotary_sums", "rotated", "qk_turned", "last_keys_moved", "qk_evacuated", "scores", "tops", "shifted_scores", "probs",
            "probs_turned", "probs_evacuated", "v_evacuated", "values", "sums_inverted", "values_normed", "values_turned", "values_evacuated", "out_product", "added", "tables"))
    wq = w(f"wqkv{layer}")
    wo = w(f"wo{layer}").rearrange("p (k n) -> p k n", k=K)
    with ExitStack() as ctx:
        sb = lambda name, shape, dt=F32: ctx.enter_context(nc.sbuf_tensor(core.fresh(name), shape, dt))
        direct = sb("direct", [P, 2, TILES, D])
        cross = sb("cross", [P, 2, TILES, D])
        window = sb("window", [P, 2, P])
        squares = sb("squares", [P, 2 * H, D])
        square_sum = sb("square_sum", [P, 2 * H])
        norm = sb("norm", [P, 2 * H])
        turn_a, turn_b = sb("turn_a", [P, 2 * H, D]), sb("turn_b", [P, 2 * H, D])
        qk = sb("qk", [P, 2 * H, D])
        q_t = sb("q_t", [P, K, P])
        k_t = sb("k_t", [P, K, 3, W])
        v = sb("v", [P, 2, 2, H, D + 1])
        top = sb("top", [P, H])
        shifted_scores, prob = sb("shifted_scores", [P, H, P]), sb("prob", [P, H, P])
        prob_t = sb("prob_t", [P, H, P])
        rec = sb("rec", [P, H])
        o = sb("o", [P, H, D])
        o_t = sb("o_t", [P, K, P])
        qk_banks, v_bank, score_banks, turn_banks, out_bank = psum[:, 0:2, :], psum[:, 2, :], psum[:, 3:5, :], psum[:, 5:7, :], psum[:, 7, :]

        def heads_of(banks):
            return banks.rearrange("p b (h n) -> p (b h) n", h=H // 2)

        with nc.Block() as block:
            @block.vector
            def _(dve):
                for s, (name, scale) in enumerate((("q", f"qs{layer}"), ("k", f"ks{layer}"))):
                    learned = w(scale).rearrange("p (a d) -> p a d", a=2)
                    for b in range(BATCH):
                        tiles = slice(b * SEQ_TILES, (b + 1) * SEQ_TILES)
                        nc.vector.tensor_tensor(direct[:, s, tiles, :], w("c" + name).rearrange("p (t d) -> p t d", d=D),
                                                w(scale).unsqueeze(1).to_broadcast([P, SEQ_TILES, D]),
                                                ALU.mult).then_inc(tables.handle, 1)
                        for a in range(2):
                            half = slice(a * D // 2, (a + 1) * D // 2)
                            nc.vector.tensor_tensor(cross[:, s, tiles, half],
                                                    w("s" + name).rearrange("p (t d) -> p t d", d=D)[:, :, half],
                                                    learned[:, 1 - a, :].unsqueeze(1).to_broadcast([P, SEQ_TILES, D // 2]),
                                                    ALU.mult).then_inc(tables.handle, 1)

            @block.gpsimd
            def _(pool):
                nc.gpsimd.memset(v[:], 1.0).then_inc(tables.handle, 1)
                nc.gpsimd.memset(k_t[:, :, 1:3, :], 0.0).then_inc(tables.handle, 1)
        tables.done += 14

        def pool_stage(pool, n, p):
            wait(pool, v_made, n - 1)
            nc.gpsimd.tensor_copy(window[:, p, :], zt[:, bass.ds(64 + n * P, P)]).then_inc(staged.handle, 1)

        def pool_norm(pool, n, p):
            wait(pool, sums, n + 1)
            wait(pool, rotated, n)
            nc.gpsimd.tensor_tensor(norm[:], square_sum[:], core.minus_half[:], ALU.pow).then_inc(norms.handle, 1)

        def pool_rotary_sum(pool, n, p):
            wait(pool, products, n + 1)
            nc.gpsimd.tensor_tensor(turn_a[:], turn_a[:], turn_b[:], ALU.add).then_inc(rotary_sums.handle, 1)

        def pe_qk(pe, n, p):
            wait(pe, staged, n + 1)
            wait(pe, products, n)
            for s in range(2):
                last = nc.tensor.matmul(qk_banks[:, s, :], window[:, p, :], wq[:, s * LA_INNER:(s + 1) * LA_INNER], start=True, stop=True)
            last.then_inc(qk_made.handle, 1)

        def pe_v(pe, n, p):
            wait(pe, v_taken, n)
            nc.tensor.matmul(v_bank, window[:, p, :], wq[:, 2 * LA_INNER:], start=True, stop=True).then_inc(v_made.handle, 1)

        def pe_turn_qk(pe, n, p):
            wait(pe, rotated, n + 1)
            wait(pe, p_taken, n)
            for s in range(2):
                for k in range(K):
                    last = nc.tensor.transpose(turn_banks[:, s, k * P:(k + 1) * P],
                                               qk[:, s * H + 2 * k:s * H + 2 * k + 2, :], core.ident[:])
            last.then_inc(qk_turned.handle, 1)

        def pe_scores(pe, n, p):
            wait(pe, o_ready, n)
            wait(pe, qk_taken, n + 1)
            for s in range(2):
                nc.tensor.matmul(score_banks[:, s, :], core.mask("ident"),
                                 core.mask("local").rearrange("p (t k) -> p t k", k=P)[:, bass.ds(n, 1), :].to_broadcast([P, H // 2, P]),
                                 start=True, stop=False, skip_group_check=True)
            for h in range(K):
                for a in range(2):
                    for s in range(2):
                        rows = slice(D * s, D * s + D)
                        last = nc.tensor.matmul(score_banks[a * W:(a + 1) * W, s, h * P:(h + 1) * P], q_t[rows, h, a * W:(a + 1) * W],
                                                k_t[rows, h, 0:3 - (1 - a):1 + a, :], start=False, stop=True, skip_group_check=True)
            last.then_inc(scores.handle, 1)

        def pe_turn_p(pe, n, p):
            wait(pe, probs, n + 1)
            for h in range(H):
                last = nc.tensor.transpose(heads_of(turn_banks)[:, h, :], prob[:, h, :], core.ident[:])
            last.then_inc(p_turned.handle, 1)

        def pe_values(pe, n, p):
            wait(pe, v_taken, n + 1)
            wait(pe, p_taken, n + 1)
            for head in range(H):
                for a in range(2):
                    last = nc.tensor.matmul(value_sums(head)[a * W:(a + 1) * W, :], prob_t[:, slot(head), a * W:(a + 1) * W],
                                            v[:, p, a, head, :], start=True, stop=True, skip_group_check=True)
            last.then_inc(values.handle, 1)

        def value_sums(head):
            return score_banks[:, head // 4, head % 4 * (D + 1):(head % 4 + 1) * (D + 1)]

        def slot(head):
            return head % 2 * K + head // 2

        def pe_turn_o(pe, n, p):
            wait(pe, added, n)
            wait(pe, o_ready, n + 1)
            for k in range(K):
                last = nc.tensor.transpose(out_bank[:, k * P:(k + 1) * P], o[:, 2 * k:2 * k + 2, :], core.ident[:])
            last.then_inc(o_turned.handle, 1)

        def pe_out(pe, n, p):
            wait(pe, o_taken, n + 1)
            for k in range(K):
                last = nc.tensor.matmul(out_bank[:, 0:P], o_t[:, k, :], wo[:, k, :], start=(k == 0), stop=(k == K - 1))
            last.then_inc(out_made.handle, 1)

        def act_square(act, n, p):
            wait(act, sums, n)
            wait(act, qk_made, n + 1)
            nc.scalar.activation(squares[:], qk_banks.rearrange("p b (h d) -> p (b h) d", d=D), ACT.Square).then_inc(squared.handle, 1)

        def act_take_qk(act, n, p):
            wait(act, scores, n)
            nc.scalar.copy(k_t[:, :, 1, :], k_t[:, :, 2, :]).then_inc(window_moved.handle, 1)
            wait(act, qk_turned, n + 1)
            nc.scalar.copy(q_t[:], turn_banks[:, 0, :].rearrange("p (k n) -> p k n", k=K))
            wait(act, window_moved, n + 1)
            nc.scalar.copy(k_t[:, :, 0:3:2, :], turn_banks[:, 1, :].rearrange("p (k a n) -> p k a n", k=K, a=2)).then_inc(qk_taken.handle, 1)

        def act_exp(act, n, p):
            wait(act, p_turned, n)
            wait(act, shifted_s, n + 1)
            nc.scalar.activation(prob[:], shifted_scores[:], ACT.Exp, scale=8.0).then_inc(probs.handle, 1)

        def act_take_p(act, n, p):
            wait(act, values, n)
            wait(act, p_turned, n + 1)
            nc.scalar.copy(prob_t[:], heads_of(turn_banks)).then_inc(p_taken.handle, 1)

        def act_take_v(act, n, p):
            wait(act, values, n)
            wait(act, v_made, n + 1)
            made = v_bank.rearrange("p (h d) -> p h d", h=H)
            nc.scalar.copy(v[:, p, 1, :, 0:D], made)
            nc.scalar.copy(v[0:W, p, 0, :, 0:D], made[0:W])
            nc.scalar.copy(v[W:P, 1 - p, 0, :, 0:D], made[W:P]).then_inc(v_taken.handle, 1)

        def act_take_o(act, n, p):
            wait(act, out_made, n)
            wait(act, o_turned, n + 1)
            nc.scalar.copy(o_t[:], out_bank.rearrange("p (k n) -> p k n", k=K)).then_inc(o_taken.handle, 1)

        def dve_square_sum(dve, n, p):
            wait(dve, norms, n)
            wait(dve, squared, n + 1)
            nc.vector.tensor_reduce(square_sum[:], squares[:], AX.X, ALU.add).then_inc(summed_squares.handle, 1)
            wait(dve, summed_squares, n + 1)
            nc.vector.tensor_scalar(square_sum[:], square_sum[:], 1e-24, None, ALU.max).then_inc(sums.handle, 1)

        def dve_rotary(dve, n, p):
            wait(dve, rotated, n)
            nc.vector.tensor_tensor(turn_a[:].rearrange("p (s h) d -> p s h d", s=2), qk_banks.rearrange("p s (h d) -> p s h d", d=D),
                                    direct[:, :, bass.ds(n, 1), :].to_broadcast([P, 2, H, D]), ALU.mult)
            for s in range(2):
                partner = qk_banks[:, s, :].rearrange("p (h a d) -> p h a d", h=H, a=2)[:, :, ::-1, :]
                last = nc.vector.tensor_tensor(turn_b[:, s * H:(s + 1) * H, :].rearrange("p h (a d) -> p h a d", a=2), partner,
                                               cross[:, s, bass.ds(n, 1), :].to_broadcast([P, H, D]).rearrange("p h (a d) -> p h a d", a=2),
                                               ALU.mult)
            last.then_inc(products.handle, 1)

        def dve_norm_qk(dve, n, p):
            wait(dve, qk_turned, n)
            wait(dve, norms, n + 1)
            wait(dve, rotary_sums, n + 1)
            nc.vector.tensor_tensor(qk[:], turn_a[:], norm[:].unsqueeze(2).to_broadcast([P, 2 * H, D]), ALU.mult).then_inc(rotated.handle, 1)

        def dve_shift(dve, n, p):
            wait(dve, shifted_s, n)
            wait(dve, scores, n + 1)
            nc.vector.tensor_reduce(top[:], heads_of(score_banks), AX.X, ALU.max).then_inc(tops.handle, 1)
            wait(dve, probs, n)
            wait(dve, tops, n + 1)
            nc.vector.tensor_tensor(shifted_scores[:], heads_of(score_banks), top[:].unsqueeze(2).to_broadcast([P, H, P]),
                                    ALU.subtract).then_inc(shifted_s.handle, 1)

        def dve_norm_values(dve, n, p):
            wait(dve, o_ready, n)
            wait(dve, values, n + 1)
            got = score_banks[:, :, 0:H // 2 * (D + 1)].rearrange("p b (h e) -> p b h e", e=D + 1)
            inverse = rec[:].rearrange("p (b h) -> p b h", b=2)
            nc.vector.reciprocal(inverse, got[:, :, :, D]).then_inc(recs.handle, 1)
            wait(dve, o_turned, n)
            wait(dve, recs, n + 1)
            nc.vector.tensor_tensor(o[:].rearrange("p (b h) d -> p b h d", b=2), got[:, :, :, 0:D],
                                    inverse.unsqueeze(3).to_broadcast([P, 2, H // 2, D]), ALU.mult).then_inc(o_ready.handle, 1)

        def dve_add(dve, n, p):
            wait(dve, out_made, n + 1)
            tile = y[:, bass.ds(n, 1), :]
            nc.vector.tensor_tensor(tile, out_bank[:, 0:P].unsqueeze(1), tile, ALU.add).then_inc(added.handle, 1)

        with nc.Block() as block:
            @block.gpsimd
            def _(pool):
                turns(pool, [(pool_stage, 2), (pool_rotary_sum, 1), (pool_norm, 2)])

            @block.tensor
            def _(pe):
                turns(pe, [(pe_turn_qk, 0), (pe_turn_o, -1), (pe_scores, 0), (pe_v, 0), (pe_qk, 2), (pe_turn_p, 0), (pe_out, -1), (pe_values, 0)])

            @block.scalar
            def _(act):
                turns(act, [(act_take_p, 0), (act_square, 2), (act_take_qk, 1), (act_take_o, 0), (act_take_v, 1), (act_exp, 1)])

            @block.vector
            def _(dve):
                turns(dve, [(dve_norm_values, -1), (dve_square_sum, 1), (dve_rotary, 1), (dve_shift, 0), (dve_norm_qk, 1), (dve_add, -1)])
        for tally in (staged, qk_made, v_made, squared, summed_squares, sums, norms, products, rotary_sums, rotated, qk_turned,
                      window_moved, qk_taken, scores, tops, shifted_s, probs, p_turned, p_taken, v_taken, values, recs, o_ready,
                      o_turned, o_taken, out_made, added):
            tally.done += TILES



def glu(core, w, layer):
    nc, psum, y, zt = core.nc, core.psum, core.y, core.zt
    up, act_done, gated, low, added = (core.sem(n) for n in ("glu_up_product", "glu_gelu", "glu_gated", "glu_out_product", "glu_added"))
    chain = core.sem("vector_chain")
    M = len(GLU_PARTS)
    w1, w2 = w(f"w1{layer}"), w(f"w2{layer}")
    with ExitStack() as ctx:
        sb = lambda name, shape: ctx.enter_context(nc.sbuf_tensor(core.fresh(name), shape, F32))
        hidden, gate, summed = sb("hidden", [P, 2, M, CHUNK]), sb("glu_gate", [P, 2, CHUNK]), sb("summed", [P, PER_CHUNK, P])
        with nc.Block() as block:
            @block.tensor
            def _(pe):
                with pe.Fori(0, CHUNKS // 2) as i:
                    for c in range(2):
                        for m, (at, rows) in enumerate(GLU_PARTS):
                            n = c * M + m
                            if n >= 2:
                                pe.wait_ge(gated.handle, gated.done + i * 2 * M + n - 1)
                            tokens = zt[:, bass.ds(i * 2 * CHUNK + c * CHUNK, CHUNK)]
                            nc.tensor.matmul(psum[0:rows, n % 2, :], w1[:, at:at + rows], tokens, start=True, stop=True)
                            nc.tensor.matmul(psum[0:rows, 2 + n % 2, :], w1[:, GLU_HID + at:GLU_HID + at + rows], tokens,
                                             start=True, stop=True).then_inc(up.handle, 1)
                    for c in range(2):
                        pe.wait_ge(gated.handle, gated.done + i * 2 * M + (c + 1) * M)
                        for j in range(PER_CHUNK):
                            for m, (at, rows) in enumerate(GLU_PARTS):
                                last = nc.tensor.matmul(psum[:, 4 + c, j * P:(j + 1) * P], hidden[0:rows, c, m, j * P:(j + 1) * P],
                                                        w2[0:rows, m * P:(m + 1) * P], start=(m == 0), stop=(m == M - 1))
                        last.then_inc(low.handle, 1)
                    pe.wait_ge(added.handle, added.done + (i + 1) * 2)

            @block.scalar
            def _(act):
                with act.Fori(0, CHUNKS // 2) as i:
                    for n in range(2 * M):
                        rows = GLU_PARTS[n % M][1]
                        act.wait_ge(up.handle, up.done + i * 2 * M + n + 1)
                        if n >= 2:
                            act.wait_ge(gated.handle, gated.done + i * 2 * M + n - 1)
                        nc.scalar.activation(gate[0:rows, n % 2, :], psum[0:rows, 2 + n % 2, :], ACT.Gelu,
                                             bias=w(f"b1g{layer}")[0:rows, n % M:n % M + 1]).then_inc(act_done.handle, 1)

            @block.vector
            def _(dve):
                with dve.Fori(0, CHUNKS // 2) as i:
                    link = Steps(dve, chain, 2, i)
                    for n in range(2 * M):
                        rows = GLU_PARTS[n % M][1]
                        dve.wait_ge(act_done.handle, act_done.done + i * 2 * M + n + 1)
                        nc.vector.scalar_tensor_tensor(out=hidden[0:rows, n // M, n % M, :], in0=psum[0:rows, n % 2, :],
                                                       scalar=w(f"b1a{layer}")[0:rows, n % M:n % M + 1], in1=gate[0:rows, n % 2, :],
                                                       op0=ALU.add, op1=ALU.mult).then_inc(gated.handle, 1)
                    for c in range(2):
                        dve.wait_ge(low.handle, low.done + i * 2 + c + 1)
                        link(nc.vector.tensor_tensor(summed[:], psum[:, 4 + c, :].rearrange("p (j n) -> p j n", j=PER_CHUNK),
                                                     w(f"b2{layer}").unsqueeze(1).to_broadcast([P, PER_CHUNK, P]), ALU.add))
                        tiles = y[:, bass.ds(i * 2 * PER_CHUNK + c * PER_CHUNK, PER_CHUNK), :]
                        nc.vector.tensor_tensor(tiles, summed[:], tiles, ALU.add).then_inc(added.handle, 1)
                        dve.wait_ge(added.handle, added.done + i * 2 + c + 1)
                link.close(CHUNKS // 2)
        turns = CHUNKS // 2
        for tally, n in ((up, 2 * M), (act_done, 2 * M), (gated, 2 * M), (low, 2), (added, 2)):
            tally.done += n * turns


def unshift(core, out):
    nc, psum = core.nc, core.psum
    turned, taken = core.sem("bank_transposed"), core.sem("bank_evacuated")
    with nc.Block() as block:
        @block.tensor
        def _(pe):
            for g in range(CHUNKS):
                if g >= 2:
                    need(pe, taken, g - 1)
                for j in range(PER_CHUNK):
                    at = 64 + g * CHUNK + j * P
                    last = nc.tensor.transpose(psum[:, g % 2, j * P:(j + 1) * P], core.zt[:, at:at + P], core.ident[:])
                last.then_inc(turned.handle, 1)

        @block.scalar
        def _(act):
            for g in range(CHUNKS):
                need(act, turned, g + 1)
                nc.scalar.copy(out[:, g * PER_CHUNK:(g + 1) * PER_CHUNK, :],
                               psum[:, g % 2, :].rearrange("p (j n) -> p j n", j=PER_CHUNK)).then_inc(taken.handle, 1)
    turned.done += CHUNKS
    taken.done += CHUNKS


def l0_ffn(core, area):
    nc, x, y = core.nc, core.x, core.y
    w = core.weights(area, L0_FFN)
    summed = core.sem("residual_added")
    for layer in range(2):
        first_tokens(core)
        normalise_block(core, x, y, 1e-5, shifted(core), only_transpose=(layer == 1))
        local_attention(core, w, layer)
        first_tokens(core)
        normalise_block(core, x, y, 1e-5, shifted(core), only_transpose=True)
        with ExitStack() as ctx:
            tokens = ctx.enter_context(nc.sbuf_tensor(core.fresh("shifted_tokens"), [P, TILES, P], F32))
            normed = ctx.enter_context(nc.sbuf_tensor(core.fresh("normed_tokens"), [P, TILES, P], F32))
            unshift(core, tokens)
            normalise_block(core, tokens, normed, 1e-5, affine(core, w(f"lg{layer}"), w(f"lb{layer}")))
        glu(core, w, layer)
    with nc.Block() as block:
        @block.vector
        def _(dve):
            for g in range(CHUNKS):
                tiles = slice(g * PER_CHUNK, (g + 1) * PER_CHUNK)
                nc.vector.scalar_tensor_tensor(out=x[:, tiles, :], in0=y[:, tiles, :], scalar=0.5, in1=x[:, tiles, :],
                                               op0=ALU.mult, op1=ALU.add).then_inc(summed.handle, 1)
    summed.done += CHUNKS



def l0_attn(core, area):
    nc, psum, x, y, zt = core.nc, core.psum, core.x, core.y, core.zt
    H, D, G = GA_HEADS, GA_DIM, 2
    R = H // G
    w = core.weights(area, L0_ATTN)
    chain, gates_done = core.sem("vector_chain"), core.sem("ga_gate_exps")
    (staged, exponents, products, decays, keys_weighted, weighted, values, parts, summed, outputs, negated,
     cleared) = (
        core.sem("ga_" + n) for n in ("operands_staged", "exponents", "scores", "decays", "keys_weighted", "scores_weighted", "values",
                                      "output_parts", "output_sum", "outputs", "negated_sums", "cleared"))
    with ExitStack() as ctx:
        sb = lambda name, shape, dt=F32: ctx.enter_context(nc.sbuf_tensor(core.fresh(name), shape, dt))
        normed = sb("rms_tokens", [P, TILES, P])
        normalise_block(core, x, y, 1e-5)
        normalise_block(core, y, normed, 1e-6, affine(core, w("nw"), 0.0), rms=True)
        q_t, k_t = sb("ga_q_t", [P, G, TOKENS]), sb("ga_k_t", [P, G, TOKENS])
        pairs = [(out[:, g, :], w(a)[:, g * P:(g + 1) * P], None, w(b)[:, g * P:(g + 1) * P], None)
                 for out, a, b in ((q_t, "wq", "wqs"), (k_t, "wk", "wks")) for g in range(G)]
        rotated_product(core, pairs, w("cos"), w("sin"))
        values_in = sb("ga_v", [P, TILES, H, D])
        gate = sb("ga_gate", [P, TILES, 3 * H])
        log_f = sb("ga_log_f", [P, TILES, 2, R, G])
        magnitude, soft = sb("ga_magnitude", [P, TILES, H]), sb("ga_soft", [P, TILES, H])
        out_gate = sb("ga_out_gate", [P, TILES, H])

        def take(g, got, link):
            n = slice(g * PER_CHUNK, (g + 1) * PER_CHUNK)
            split = lambda t, m: t[:, n, :].rearrange("p (b j) m -> p b j m", b=2)
            v = values_in[:, n, :, :].rearrange("p (b j) h d -> p b j (h d)", b=2)
            nc.vector.tensor_copy(v, got[:, :, 0:2, 0:P])
            return nc.vector.tensor_tensor(split(gate, 3 * H), got[:, :, 0:2, P:P + 3 * H],
                                           w("bg").unsqueeze(1).unsqueeze(1).to_broadcast([P, 2, 2, 3 * H]), ALU.add)
        tokens_product(core, w("wvg"), take)
        with nc.Block() as block:
            @block.scalar
            def _(act):
                act_chain = core.sem("scalar_chain")
                link = Steps(act, act_chain)
                link(nc.scalar.activation(magnitude[:], gate[:, :, 0:H], ACT.Abs))
                link(nc.scalar.activation(magnitude[:], magnitude[:], ACT.Exp, scale=-1.0))
                nc.scalar.activation(out_gate[:], gate[:, :, 2 * H:], ACT.Exp, scale=-1.0).then_inc(gates_done.handle, 1)
                nc.scalar.activation(gate[:, :, H:2 * H], gate[:, :, H:2 * H], ACT.Exp, scale=-1.0).then_inc(gates_done.handle, 1)
                nc.scalar.activation(soft[:], magnitude[:], ACT.Ln, bias=1.0).then_inc(gates_done.handle, 1)
                link.close()

            @block.vector
            def _(dve):
                need(dve, gates_done, 3)
                link = Steps(dve, chain)
                for t in (out_gate[:], gate[:, :, H:2 * H]):
                    link(nc.vector.tensor_scalar(t, t, 1.0, None, ALU.add))
                    link(nc.vector.reciprocal(t, t))
                link(nc.vector.tensor_scalar(gate[:, :, H:2 * H], gate[:, :, H:2 * H], 1.0 / 4.0, None, ALU.mult))
                for n in range(2):
                    tiles = slice(n * SEQ_TILES, (n + 1) * SEQ_TILES)
                    nc.vector.tensor_tensor(values_in[:, tiles, :, :], values_in[:, tiles, :, :],
                                            gate[:, tiles, H:2 * H].unsqueeze(3).to_broadcast([P, SEQ_TILES, H, D]),
                                            ALU.mult).then_inc(gates_done.handle, 1)
                for r in range(R):
                    ins = nc.vector.scalar_tensor_tensor(
                        out=log_f[:, :, 0, r, :], in0=gate[:, :, 0:H].rearrange("p t (g r) -> p t g r", g=G)[:, :, :, r], scalar=0.0,
                        in1=soft[:].rearrange("p t (g r) -> p t g r", g=G)[:, :, :, r], op0=ALU.min, op1=ALU.subtract)
                link(ins)
                nc.vector.tensor_scalar(log_f[:, :, 1, :, :].rearrange("p t r g -> p t (r g)"),
                                        log_f[:, :, 0, :, :].rearrange("p t r g -> p t (r g)"), -1.0, None,
                                        ALU.mult).then_inc(gates_done.handle, 1)
                need(dve, gates_done, 6)
                link.close()
        gates_done.done += 6

        q_s, k_s = sb("ga_q", [P, 2, G, P]), sb("ga_k", [P, 2, G, P])
        f_s = sb("ga_f", [P, 2, 2, R, G])
        f_rows = sb("ga_f_rows", [P, 2, G, R * 32])
        v_s = sb("ga_vs", [P, 2, H, D])
        decay = sb("ga_decay", [P, 2, R, G, P])
        minus_f = sb("ga_minus_f", [P, 2, H])
        exps = sb("ga_exps", [P, 2, 2 * H + G])
        weights = sb("ga_weights", [P, 2, R, G, P])
        k_tok = sb("ga_k_tok", [P, 2, G, R, 32])
        inter, intra, block_u = sb("ga_inter", [P, H, D]), sb("ga_intra", [P, H, D]), sb("ga_block", [P, G, 64])
        state = sb("ga_state_m", [P, G, 64])
        keep = sb("ga_keep", [P, TILES])
        o = normed
        score_part = psum[:, 0:4, 0:G * P]
        turned_keys, sums_at = psum[:, 7, 0:G * P], psum[:, 7, G * P:G * P + 2 * H + G]
        values_at, update_at = psum[:, 6, 0:2 * P], psum[:, 6, 2 * P:3 * P]
        ones_col = w("upper")[:, P - 1:P]
        with nc.Block() as block:
            @block.gpsimd
            def _(pool):
                nc.gpsimd.memset(state[:], 0.0).then_inc(cleared.handle, 1)
                nc.gpsimd.memset(keep[:], 1.0).then_inc(cleared.handle, 1)
                need(pool, cleared, 2)
                nc.gpsimd.memset(keep[:, SEQ_TILES - 1::SEQ_TILES], 0.0).then_inc(cleared.handle, 1)
        cleared.done += 3

        def pool_stage(pool, n, p):
            wait(pool, values, n - 1)
            nc.gpsimd.tensor_copy(q_s[:, p], q_t[:, :, bass.ds(n * P, P)])
            nc.gpsimd.tensor_copy(k_s[:, p], k_t[:, :, bass.ds(n * P, P)])
            nc.gpsimd.tensor_copy(f_s[:, p].rearrange("p s r g -> p (s r g)").unsqueeze(1),
                                  log_f[:].rearrange("p t s r g -> p t (s r g)")[:, bass.ds(n, 1), :])
            nc.gpsimd.tensor_copy(f_rows[:, p].rearrange("p g (r d) -> p g r d", r=R),
                                  log_f[:, :, 0, :, :].rearrange("p t r g -> p t g r")[:, bass.ds(n, 1), :, :]
                                  .rearrange("p t g r -> p (t g) r").unsqueeze(3).to_broadcast([P, G, R, 32]))
            nc.gpsimd.tensor_copy(v_s[:, p].rearrange("p h d -> p (h d)").unsqueeze(1),
                                  values_in[:].rearrange("p t h d -> p t (h d)")[:, bass.ds(n, 1), :]).then_inc(staged.handle, 1)

        def pe_decays(pe, n, p):
            wait(pe, keys_weighted, n)
            wait(pe, decays, n)
            wait(pe, staged, n + 1)
            for g in range(G):
                nc.tensor.transpose(turned_keys[:, g * P:(g + 1) * P], k_s[:, p, g, :], core.ident[:])
            lf, nlf = f_s[:, p, 0].rearrange("p r g -> p (r g)"), f_s[:, p, 1].rearrange("p r g -> p (r g)")
            nc.tensor.matmul(sums_at[:, 0:H], w("upper"), lf, start=True, stop=True)
            nc.tensor.matmul(sums_at[:, H:2 * H], ones_col.to_broadcast([P, P]), lf, start=True, stop=False)
            nc.tensor.matmul(sums_at[:, H:2 * H], w("upper"), nlf, start=False, stop=True)
            for g in range(G):
                nc.tensor.matmul(sums_at[:, 2 * H + g:2 * H + g + 1], f_rows[:, p, g, :], ones_col, start=True, stop=True)
            for k in range(2):
                for a in range(4):
                    nc.tensor.matmul(psum[:, 4 + k, a * P:(a + 1) * P], lf[:, 4 * k + a:4 * k + a + 1].to_broadcast([P, P]), w("upper"),
                                     start=(a == 0), stop=False, skip_group_check=True)
                last = nc.tensor.matmul(psum[:, 4 + k, :], core.mask("ident"), core.mask("causal").unsqueeze(1).to_broadcast([P, 4, P]),
                                        start=False, stop=True, skip_group_check=True)
            last.then_inc(exponents.handle, 1)

        def pe_scores(pe, n, p):
            wait(pe, weighted, n)
            for g in range(G):
                for r in range(R):
                    rows = slice(32 * r, 32 * r + D)
                    last = nc.tensor.matmul(score_part[:, r, g * P:(g + 1) * P], k_s[rows, p, g, :], q_s[rows, p, g, :],
                                            start=True, stop=True, skip_group_check=True)
            last.then_inc(products.handle, 1)

        def pe_values(pe, n, p):
            wait(pe, outputs, n)
            wait(pe, weighted, n + 1)
            for h in range(H):
                nc.tensor.matmul(values_at[:, h * D:(h + 1) * D], weights[:, p, h % R, h // R, :], v_s[:, p, h, :], start=True, stop=True)
            for g in range(G):
                nc.tensor.matmul(values_at[:, P + g * 64:P + (g + 1) * 64], q_s[:, p, g, :], state[:, g, :], start=True, stop=True)
            for g in range(G):
                last = nc.tensor.matmul(update_at[:, g * 64:(g + 1) * 64], k_tok[:, p, g].rearrange("p r d -> p (r d)"),
                                        v_s[:, p, g * R:(g + 1) * R, :], start=True, stop=True)
            last.then_inc(values.handle, 1)

        def act_exps(act, n, p):
            wait(act, outputs, n - 1)
            wait(act, exponents, n + 1)
            nc.scalar.activation(minus_f[:, p, :], sums_at[:, 0:H], ACT.Copy, scale=-1.0).then_inc(negated.handle, 1)
            nc.scalar.activation(exps[:, p, :], sums_at, ACT.Exp)
            wait(act, negated, n + 1)
            for m in range(H):
                last = nc.scalar.activation(decay[:, p, m // G, m % G, :], psum[:, 4 + m // 4, m % 4 * P:(m % 4 + 1) * P],
                                            ACT.Exp, bias=minus_f[:, p, m:m + 1])
            last.then_inc(decays.handle, 1)

        def dve_weights(dve, n, p):
            wait(dve, values, n - 1)
            wait(dve, decays, n + 1)
            nc.vector.tensor_tensor(exps[:, p, 2 * H:], exps[:, p, 2 * H:], keep[:, bass.ds(n, 1)].to_broadcast([P, G]), ALU.mult)
            nc.vector.tensor_tensor(k_tok[:, p], turned_keys.rearrange("p (g r d) -> p g r d", g=G, r=R),
                                    exps[:, p, H:2 * H].rearrange("p (r g) -> p g r", r=R).unsqueeze(3).to_broadcast([P, G, R, 32]),
                                    ALU.mult).then_inc(keys_weighted.handle, 1)
            wait(dve, products, n + 1)
            nc.vector.tensor_tensor(weights[:, p].rearrange("p r g n -> p r (g n)"), score_part,
                                    decay[:, p].rearrange("p r g n -> p r (g n)"), ALU.mult).then_inc(weighted.handle, 1)

        def dve_outputs(dve, n, p):
            wait(dve, outputs, n)
            wait(dve, values, n + 1)
            nc.vector.tensor_tensor(inter[:].rearrange("p (g r) d -> p g r d", g=G), values_at[:, P:2 * P].rearrange("p (g r d) -> p g r d", g=G, r=R),
                                    exps[:, p, 0:H].rearrange("p (r g) -> p g r", r=R).unsqueeze(3).to_broadcast([P, G, R, D]),
                                    ALU.mult)
            nc.vector.scalar_tensor_tensor(out=block_u[:].rearrange("p g m -> p (g m)"), in0=update_at, scalar=keep[:, bass.ds(n, 1)],
                                           in1=w("diag"), op0=ALU.mult, op1=ALU.mult).then_inc(parts.handle, 1)
            wait(dve, parts, n + 1)
            for g in range(G):
                nc.vector.scalar_tensor_tensor(out=state[:, g, :], in0=state[:, g, :], scalar=exps[:, p, 2 * H + g:2 * H + g + 1],
                                               in1=block_u[:, g, :], op0=ALU.mult, op1=ALU.add)
            nc.vector.tensor_tensor(intra[:].rearrange("p h d -> p (h d)"), values_at[:, 0:P], inter[:].rearrange("p h d -> p (h d)"),
                                    ALU.add).then_inc(summed.handle, 1)
            wait(dve, summed, n + 1)
            nc.vector.tensor_tensor(o[:].rearrange("p t (h d) -> p t h d", h=H)[:, bass.ds(n, 1), :, :], intra[:].unsqueeze(1),
                                    out_gate[:, bass.ds(n, 1), :].unsqueeze(3).to_broadcast([P, 1, H, D]), ALU.mult).then_inc(outputs.handle, 1)

        with nc.Block() as block:
            @block.gpsimd
            def _(pool):
                turns(pool, [(pool_stage, 1)])

            @block.tensor
            def _(pe):
                turns(pe, [(pe_scores, 0), (pe_decays, 1), (pe_values, 0)])

            @block.scalar
            def _(act):
                turns(act, [(act_exps, 1)])

            @block.vector
            def _(dve):
                turns(dve, [(dve_weights, 1), (dve_outputs, 0)])
        for tally in (staged, exponents, products, decays, keys_weighted, weighted, values, parts, summed, outputs, negated):
            tally.done += TILES
        normalise_block(core, x, o, 1e-5, plain(core), only_transpose=True)
        tokens_product(core, w("wout"), add_to_x(core, bias=w("bout")))


STACK = 74
MAX_ROWS = 72


class Stacks:

    PARTS = [(a, b) for a in range(3) for b in range(3)]

    def __init__(self, core, ctx, before, behind, room=None):
        nc = core.nc
        sb = lambda name, shape, dt: ctx.enter_context(nc.sbuf_tensor(core.fresh(name), shape, dt))
        self.before, self.behind = before, behind
        self.q = sb("stack_q", [P, FA_HEADS, SEQ + behind], BF16)
        self.k = sb("stack_k", [P, FA_HEADS, before + SEQ], BF16)
        room = sb("parts", [P, 6 * SEQ], BF16)[:] if room is None else room.bitcast(BF16)
        self.parts = [[room[:, (3 * n + i) * SEQ:(3 * n + i + 1) * SEQ] for i in range(3)] for n in range(2)]
        self.scratch = nc.dram_tensor(core.fresh("parts_dram"), (BATCH, 2, 3, P, SEQ), BF16).ap()

    def place(self, core, engine, which, b, ready=None):
        placed = core.sem(("q_parts_placed", "k_parts_placed")[which])
        to, at = (self.q, 0) if which == 0 else (self.k, self.before)
        for n, pair in enumerate(self.PARTS):
            if ready is not None and n == len(self.PARTS) - 1:
                need(engine, *ready)
            engine.dma_start(to[8 * n:8 * n + 8, :, at:at + SEQ],
                             self.scratch[b, which, pair[which]].rearrange("(h d) t -> d h t", d=FA_DIM)).then_inc(placed.handle, 16)
        need(engine, placed, 16 * len(self.PARTS))

    def fill_first(self, core, q, k):
        nc = core.nc
        chain, split, cleared = (core.sem(n) for n in ("vector_chain", "parts_split", "stack_cleared"))
        stored = [core.sem("q_parts_stored"), core.sem("k_parts_stored")]
        with nc.Block() as block:
            @block.vector
            def _(dve):
                link = Steps(dve, chain)
                for b in range(BATCH):
                    for which, all_tokens in enumerate((q, k)):
                        src, parts = all_tokens[:, b * SEQ:(b + 1) * SEQ], self.parts[which]
                        if b:
                            need(dve, stored[which], 48 * b)
                        link(nc.vector.tensor_copy(parts[0], src))
                        link(nc.vector.tensor_tensor(src, src, parts[0], ALU.subtract))
                        link(nc.vector.tensor_copy(parts[1], src))
                        nc.vector.tensor_tensor(parts[2], src, parts[1], ALU.subtract).then_inc(split.handle, 1)
                link.close()

            @block.gpsimd
            def _(pool):
                nc.gpsimd.memset(self.k[64:STACK, :, :], 1.0).then_inc(cleared.handle, 1)
                if self.before:
                    need(pool, cleared, 1)
                    nc.gpsimd.memset(self.k[0:96, :, 0:self.before], 0.0).then_inc(cleared.handle, 1)
                if self.behind:
                    nc.gpsimd.memset(self.q[0:96, :, SEQ:], 0.0).then_inc(cleared.handle, 1)

            def store_and_place(engine, which):
                for b in range(BATCH):
                    need(engine, split, 2 * b + which + 1)
                    for i in range(3):
                        engine.dma_start(self.scratch[b, which, i], self.parts[which][i]).then_inc(stored[which].handle, 16)
                    need(engine, stored[which], 48 * (b + 1))
                    if b == 0:
                        self.place(core, engine, which, 0, (cleared, edges) if which else None)

            edges = 1 + bool(self.before) + bool(self.behind)

            @block.sync
            def _(sp):
                store_and_place(sp, 0)

            @block.scalar
            def _(act):
                store_and_place(act, 1)
        split.done += 2 * BATCH
        for tally in stored:
            tally.done += 48 * BATCH
        cleared.done += edges
        self.placed(core)

    def fill_next(self, core, b):
        with core.nc.Block() as block:
            @block.sync
            def _(sp):
                self.place(core, sp, 0, b)

            @block.scalar
            def _(act):
                self.place(core, act, 1, b)
        self.placed(core)

    def placed(self, core):
        for name in ("q_parts_placed", "k_parts_placed"):
            core.sem(name).done += 16 * len(self.PARTS)


def value_tokens(core, out, weights, bias):
    nc = core.nc
    ones = core.sem("value_ones")
    with nc.Block() as block:
        @block.gpsimd
        def _(pool):
            nc.gpsimd.memset(out, 1.0).then_inc(ones.handle, 1)
    ones.done += 1

    def take(g, got, link):
        to = out[:, g * PER_CHUNK:(g + 1) * PER_CHUNK, :, 0:FA_DIM]
        got = got.rearrange("p j (h d) -> p j h d", h=FA_HEADS)
        if bias is None:
            return nc.vector.tensor_copy(to, got)
        for j in range(PER_CHUNK):
            last = nc.vector.tensor_tensor(to[:, j], got[:, j], bias.rearrange("p (h d) -> p h d", h=FA_HEADS), ALU.add)
        return last
    tokens_product(core, weights, take)


def l1_attn(core, area):
    nc, psum, x, y, zt = core.nc, core.psum, core.x, core.y, core.zt
    w = core.weights(area, L1_ATTN)
    H, D, T = FA_HEADS, FA_DIM, SEQ_TILES
    QUADS, GROUP = FA_HEADS // 4, 32
    UNITS = 2 * T
    RING, LAG = 4, 2
    base = sum(n for _, n in L1_ATTN)
    q_t, k_t = (core.areas[area][:, base + i * TOKENS:base + (i + 1) * TOKENS] for i in range(2))
    chain = core.sem("vector_chain")
    (max_scores, max_read, rows_ready, rows_stored, rows_placed, scores, probs, v_staged, used, taken, turned, normed,
     cleared) = (core.sem(n) for n in (
        "fa_max_scores", "fa_max_read", "fa_rows_split", "fa_rows_stored", "fa_rows_placed", "fa_scores", "fa_probs",
        "fa_values_staged", "fa_probs_used", "fa_sums_taken", "fa_sums_turned", "fa_normed", "fa_cleared"))
    with ExitStack() as ctx:
        sb = lambda name, shape, dt=F32: ctx.enter_context(nc.sbuf_tensor(core.fresh(name), shape, dt))
        normalise_block(core, x, y, 1e-5, plain(core))
        rotated_product(core, [(q_t, w("wq"), w("bq"), w("wqs"), w("bqs")), (k_t, w("wk"), w("bk"), w("wks"), w("bks"))],
                        w("cos"), w("sin"))
        v = sb("fa_v", [P, TILES, H, D + 1])
        value_tokens(core, v[:], w("wv"), w("bv"))
        prob = sb("fa_prob", [P, 2 * RING, SEQ])
        stacks = Stacks(core, ctx, 0, 0, prob[:, 0:3, :].rearrange("p r n -> p (r n)"))
        pair_v = sb("fa_pair_v", [P, 2, T, 2, GROUP])
        sums = sb("fa_sums", [P, 2, CHUNK])
        half_top = sb("fa_half_top", [P, 2, 2, T, 2])
        top = sb("fa_top", [P, 2, 2, T])
        top_turned = sb("fa_top_turned", [P, GROUP])
        rows = sb("fa_rows", [P, 2, GROUP], BF16)
        rec = sb("fa_rec", [P, 4, 4])
        max_dram = nc.dram_tensor("fa_max_dram", (P // GROUP, GROUP, 2, GROUP), BF16).ap()
        q_s = stacks.q[0:STACK].rearrange("p h t -> p (h t)")
        k_s = stacks.k[0:STACK].rearrange("p h t -> p (h t)")
        q_parts, k_parts = q_s[0:MAX_ROWS], k_s[0:MAX_ROWS]

        with nc.Block() as block:
            @block.gpsimd
            def _(pool):
                nc.gpsimd.memset(pair_v[:], 0.0).then_inc(cleared.handle, 1)

            @block.vector
            def _(dve):
                nc.vector.memset(top[:], 0.0).then_inc(cleared.handle, 1)
        cleared.done += 2

        for b in range(BATCH):
            if b:
                stacks.fill_next(core, b)
            else:
                stacks.fill_first(core, q_t, k_t)


            def pe_max(pe, q, r, half, opening=False):
                head, t = q * 2 + r % 2, r // 2
                if not (opening and r == 0):
                    pe.wait_ge(max_read.handle, max_read.done + q * 2 * UNITS + 2 * r + half - 1)
                nc.tensor.matmul(psum[:, half, :], q_parts[:, bass.ds(head * SEQ + t * P, P)],
                                 k_parts[:, bass.ds(head * SEQ + half * CHUNK, CHUNK)],
                                 start=True, stop=True).then_inc(max_scores.handle, 1)

            def pe_scores(pe, q, r, half, first):
                head, t = q * 2 + r % 2, r // 2
                if half == 0 and not (first and r < 2):
                    pe.wait_ge(probs.handle, probs.done + q * UNITS + r - 1)
                made = nc.tensor.matmul(psum[:, 2 + 2 * (r % 2) + half, :], k_s[:, bass.ds(head * SEQ + t * P, P)],
                                        q_s[:, bass.ds(head * SEQ + half * CHUNK, CHUNK)], start=True, stop=True)
                if half:
                    made.then_inc(scores.handle, 1)

            def pe_values(pe, q, parity, t, first):
                if t == 0:
                    pe.wait_ge(v_staged.handle, v_staged.done + q + 1)
                    if not first:
                        pe.wait_ge(normed.handle, normed.done + q - 1)
                pe.wait_ge(probs.handle, probs.done + q * UNITS + 2 * t + 2)
                for j in range(2):
                    for half in range(2):
                        at = GROUP * (2 * j + half)
                        last = nc.tensor.matmul(psum[at:at + GROUP, 6 + parity, :], pair_v[:, parity, t, j, :],
                                                prob[:, (2 * t + j) % (2 * RING), half * CHUNK:(half + 1) * CHUNK],
                                                start=(t == 0), stop=(t == T - 1), tile_position=(0, at), skip_group_check=True)
                last.then_inc(used.handle, 1)

            def pe_turn_sums(pe, q, parity):
                pe.wait_ge(taken.handle, taken.done + q + 1)
                for s in range(4):
                    last = nc.tensor.transpose(psum[:, 6 + parity, s * P:(s + 1) * P], sums[:, parity, s * P:(s + 1) * P], core.ident[:])
                last.then_inc(turned.handle, 1)

            def pe_pair(pe, q, parity, ahead, first):
                pe.wait_ge(rows_placed.handle, rows_placed.done + q * 32 + 32)
                for t in range(T):
                    on_values = None
                    if t >= LAG:
                        on_values = lambda t=t: pe_values(pe, q, parity, t - LAG, first)
                    elif not (first and parity == 0):
                        on_values = lambda t=t: pe_values(pe, q - 1, 1 - parity, T - LAG + t, first)
                    for half in range(2):
                        pe_scores(pe, q, 2 * t, half, first and parity == 0)
                    for half in range(2):
                        if ahead:
                            pe_max(pe, q + 2, 2 * t, half)
                    if on_values:
                        on_values()
                    if ahead:
                        pe_max(pe, q + 2, 2 * t + 1, 0)
                    for half in range(2):
                        pe_scores(pe, q, 2 * t + 1, half, first and parity == 0)
                    if ahead:
                        pe_max(pe, q + 2, 2 * t + 1, 1)
                    if t == LAG + 1 and not (first and parity == 0):
                        pe_turn_sums(pe, q - 1, 1 - parity)

            def act_pair(act, q, parity, first):
                for r in range(UNITS):
                    act.wait_ge(scores.handle, scores.done + q * UNITS + r + 1)
                    if not (first and parity == 0 and r < 2 * RING) and r % 2 == 0:
                        act.wait_ge(used.handle, used.done + q * T + r // 2 - RING + 1)
                    nc.scalar.activation(prob[:, r % (2 * RING), :], psum[:, 2 + 2 * (r % 2):4 + 2 * (r % 2), :].rearrange("p a n -> p (a n)"),
                                         ACT.Exp, scale=float(D) ** -0.5).then_inc(probs.handle, 1)
                    if r == 2 * LAG and not (first and parity == 0):
                        act_take(act, q - 1, 1 - parity)

            def act_take(act, q, parity):
                act.wait_ge(used.handle, used.done + q * T + T)
                nc.scalar.copy(sums[:, parity, :], psum[:, 6 + parity, :]).then_inc(taken.handle, 1)

            def dve_max(dve, q, parity, link, between=None):
                for r in range(UNITS):
                    for half in range(2):
                        dve.wait_ge(max_scores.handle, max_scores.done + q * 2 * UNITS + 2 * r + half + 1)
                        nc.vector.tensor_reduce(half_top[:, parity, r % 2, r // 2, half:half + 1], psum[:, half, :], AX.X,
                                                ALU.max).then_inc(max_read.handle, 1)
                    if r == 8 and between:
                        between()
                dve.wait_ge(max_read.handle, max_read.done + q * 2 * UNITS + 2 * UNITS)
                link(nc.vector.tensor_reduce(top[:, parity], half_top[:, parity], AX.X, ALU.max, negate=True))
                link(nc.vector.transpose(top_turned[:], top[:].rearrange("p a j t -> p (a j t)")))
                if not isinstance(q, int) or q:
                    dve.wait_ge(rows_stored.handle, rows_stored.done + q * 16)
                link(nc.vector.tensor_copy(rows[:, 0, :], top_turned[:]))
                nc.vector.tensor_tensor(rows[:, 1, :], top_turned[:], rows[:, 0, :], ALU.subtract).then_inc(rows_ready.handle, 1)

            def dve_normalise(dve, q, parity, link):
                dve.wait_ge(turned.handle, turned.done + q + 1)
                if not isinstance(q, int) or q:
                    dve.wait_ge(normed.handle, normed.done + q)
                got = psum[:, 6 + parity, :].rearrange("p (s g e) -> p s g e", s=4, g=4)
                link(nc.vector.reciprocal(rec[:], got[:, :, :, D]))
                out = y[:, b * T:(b + 1) * T, bass.ds(q * 2 * D, 2 * D)].rearrange("p (a s) (j d) -> p a s j d", a=2, j=2)
                for g in range(4):
                    last = nc.vector.tensor_tensor(out[:, g % 2, :, g // 2, :], got[:, :, g, 0:D],
                                                   rec[:, :, g:g + 1].to_broadcast([P, 4, D]), ALU.mult)
                last.then_inc(normed.handle, 1)

            def pool_values(pool, q, parity):
                nc.gpsimd.tensor_copy(pair_v[:, parity, :, :, 0:D + 1],
                                      v[:, b * T:(b + 1) * T, bass.ds(q * 2, 2), :]).then_inc(v_staged.handle, 1)

            def sp_rows(sp, q):
                need(sp, rows_ready, q + 1)
                if q:
                    need(sp, rows_placed, q * 32)
                sp.dma_start(max_dram.rearrange("b c i r -> (b c) i r"), rows[:]).then_inc(rows_stored.handle, 16)
                need(sp, rows_stored, (q + 1) * 16)
                mine = slice(UNITS * (q % 2), UNITS * (q % 2) + UNITS)
                for i in range(2):
                    sp.dma_start(stacks.q[MAX_ROWS + i:MAX_ROWS + i + 1, 2 * q:2 * q + 2, :].rearrange("o j (t b r) -> o (j t) b r", t=T, r=GROUP),
                                 max_dram[:, mine, i:i + 1, :].rearrange("b c i r -> i c b r")).then_inc(rows_placed.handle, 16)

            with nc.Block() as block:
                @block.tensor
                def _(pe):
                    for q in range(2):
                        for r in range(UNITS):
                            for half in range(2):
                                pe_max(pe, q, r, half, opening=(q == 0))
                    for q in range(2):
                        pe_pair(pe, q, q, True, True)
                    with pe.Fori(1, QUADS - 1) as i:
                        for parity in range(2):
                            pe_pair(pe, i * 2 + parity, parity, True, False)
                    for q in (H // 2 - 2, H // 2 - 1):
                        pe_pair(pe, q, q % 2, False, False)
                    for t in range(T - LAG, T):
                        pe_values(pe, H // 2 - 1, 1, t, False)
                    pe_turn_sums(pe, H // 2 - 1, 1)

                @block.scalar
                def _(act):
                    for q in range(2):
                        act_pair(act, q, q, True)
                    with act.Fori(1, QUADS) as i:
                        for parity in range(2):
                            act_pair(act, i * 2 + parity, parity, False)
                    act_take(act, H // 2 - 1, 1)

                @block.vector
                def _(dve):
                    link = Steps(dve, chain)
                    for q in range(2):
                        dve_max(dve, q, q, link)
                    dve_max(dve, 2, 0, link)
                    dve_max(dve, 3, 1, link, lambda: dve_normalise(dve, 0, 0, link))
                    link.close()
                    with dve.Fori(2, QUADS) as i:
                        link = Steps(dve, chain, 2 * (3 + 1), i - 2)
                        for parity in range(2):
                            dve_max(dve, i * 2 + parity, parity, link,
                                    lambda: dve_normalise(dve, i * 2 + parity - 3, 1 - parity, link))
                    link.close(QUADS - 2)
                    link = Steps(dve, chain)
                    for q in range(H // 2 - 3, H // 2):
                        dve_normalise(dve, q, q % 2, link)
                    link.close()

                @block.gpsimd
                def _(pool):
                    for q in range(2):
                        pool_values(pool, q, q)
                    with pool.Fori(1, QUADS) as i:
                        for parity in range(2):
                            pool.wait_ge(used.handle, used.done + (i * 2 + parity - 1) * T)
                            pool_values(pool, i * 2 + parity, parity)

                @block.sync
                def _(sp):
                    for q in range(H // 2):
                        sp_rows(sp, q)
            for tally, n in ((max_scores, 2 * UNITS), (max_read, 2 * UNITS), (rows_ready, 1), (rows_placed, 32), (rows_stored, 16),
                             (scores, UNITS), (probs, UNITS), (v_staged, 1), (used, T), (taken, 1), (turned, 1), (normed, 1)):
                tally.done += n * H // 2
        normalise_block(core, x, y, 1e-5, plain(core), only_transpose=True)
        tokens_product(core, w("wo"), add_to_x(core, bias=w("bo")))


I32 = mybir.dt.int32


def quantise(nc, link, source, out, tmp, ready=None):
    n = source.shape[1]
    blocks = lambda t: t[:, 0:n].rearrange("p (b e) -> p b e", e=Q4_BLOCK)
    nb = n // Q4_BLOCK
    biggest, scale, inverse = (t[:, 0:nb] for t in tmp["small"])
    scaled, size, high, low = (t[:, 0:n] for t in tmp["wide"])
    spread = lambda t: t.unsqueeze(2).to_broadcast([P, nb, Q4_BLOCK])
    link(nc.vector.tensor_reduce(biggest, blocks(source), AX.X, ALU.max, apply_absolute_value=True))
    link(nc.vector.tensor_scalar(scale, biggest, 1.0 / 6.0, 1e-12, ALU.mult, ALU.max))
    link(nc.vector.reciprocal(inverse, scale))
    link(nc.vector.tensor_tensor(blocks(scaled), blocks(source), spread(inverse), ALU.mult))
    link(nc.vector.tensor_scalar(size.bitcast(I32), scaled.bitcast(I32), 0x7FFFFFFF, None, ALU.bitwise_and))
    link(nc.vector.tensor_scalar(high, size, 5.0, 2.0, ALU.is_gt, ALU.mult))
    for mid in (3.5, 2.5):
        link(nc.vector.scalar_tensor_tensor(out=high, in0=size, scalar=mid, in1=high, op0=ALU.is_gt, op1=ALU.add))
    link(nc.vector.tensor_scalar(low, size, 1.75, None, ALU.is_gt))
    for mid in (1.25, 0.75, 0.25):
        link(nc.vector.scalar_tensor_tensor(out=low, in0=size, scalar=mid, in1=low, op0=ALU.is_gt, op1=ALU.add))
    link(nc.vector.scalar_tensor_tensor(out=high, in0=low, scalar=0.5, in1=high, op0=ALU.mult, op1=ALU.add))
    link(nc.vector.scalar_tensor_tensor(out=low.bitcast(I32), in0=scaled.bitcast(I32), scalar=-2147483648, in1=high.bitcast(I32),
                                        op0=ALU.bitwise_and, op1=ALU.bitwise_or))
    last = nc.vector.tensor_tensor(blocks(out), blocks(low), spread(scale), ALU.mult)
    link(last) if ready is None else last.then_inc(ready.handle, 1)


def l2_ffn(core, area):
    nc, psum, x, y, zt = core.nc, core.psum, core.x, core.y, core.zt
    w = core.weights(area, L2_FFN)
    chain = core.sem("vector_chain")
    base = sum(n for _, n in L2_FFN)
    gate_up = core.areas[area][:, base:base + 2 * Q4_HID]
    down = core.areas[area][:, base + 2 * Q4_HID:base + 2 * Q4_HID + 3 * P]
    turned, taken = core.sem("bank_transposed"), core.sem("bank_evacuated")
    products, silu, gated, ready, h_turned, h_taken, out_made, added = (core.sem(n) for n in (
        "q4_up_product", "q4_silu", "q4_gated", "q4_hidden_quantised", "q4_hidden_turned", "q4_hidden_taken",
        "q4_out_product", "q4_added"))
    WIDE = PER_CHUNK * Q4_HID
    with ExitStack() as ctx:
        sb = lambda name, shape, dt=F32: ctx.enter_context(nc.sbuf_tensor(core.fresh(name), shape, dt))
        tmp = {"small": [sb(f"q4_small{i}", [P, WIDE // Q4_BLOCK]) for i in range(3)],
               "wide": [sb(f"q4_wide{i}", [P, WIDE]) for i in range(4)]}
        if not core.weights_quantised:
            core.weights_quantised = True
            dequant = sb("q4_weights", [P, 6 * P + Q4_HID])
            with nc.Block() as block:
                @block.vector
                def _(dve):
                    link = Steps(dve, chain)
                    packed = core.areas[area][:, 0:base]
                    quantise(nc, link, packed, dequant, tmp)
                    link.close()
            with nc.Block() as block:
                @block.tensor
                def _(pe):
                    for s in range(2):
                        for m, (at, rows) in enumerate(Q4_PARTS):
                            last = nc.tensor.transpose(psum[:, s, at:at + rows], dequant[0:rows, (3 * s + m) * P:(3 * s + m + 1) * P],
                                                       core.ident[0:rows, 0:rows])
                    for m, (at, rows) in enumerate(Q4_PARTS):
                        last = nc.tensor.transpose(psum[0:rows, 2, m * P:(m + 1) * P], dequant[:, 6 * P + at:6 * P + at + rows], core.ident[:])
                    last.then_inc(turned.handle, 1)

                @block.scalar
                def _(act):
                    need(act, turned, 1)
                    nc.scalar.copy(gate_up.rearrange("p (s n) -> p s n", s=2), psum[:, 0:2, 0:Q4_HID]).then_inc(taken.handle, 1)
                    for m, (at, rows) in enumerate(Q4_PARTS):
                        nc.scalar.copy(down[0:rows, m * P:(m + 1) * P], psum[0:rows, 2, m * P:(m + 1) * P]).then_inc(taken.handle, 1)
            turned.done += 1
            taken.done += 4
        normalise_block(core, x, y, 1e-5)
        with nc.Block() as block:
            @block.vector
            def _(dve):
                link = Steps(dve, chain)
                half = TOKENS // 2
                flat = y[:].rearrange("p t d -> p (t d)")
                for b in range(2):
                    quantise(nc, link, flat[:, b * half:(b + 1) * half], flat[:, b * half:(b + 1) * half], tmp)
                link.close()
        normalise_block(core, x, y, 1e-5, plain(core), only_transpose=True)
        act_gate = sb("q4_gate", [P, 2, Q4_HID])
        hidden = sb("q4_hidden", [P, PER_CHUNK, Q4_HID])
        hidden_q = sb("q4_hidden_q", [P, PER_CHUNK, Q4_HID])
        hidden_t = sb("q4_hidden_t", [P, 3, CHUNK])
        with nc.Block() as block:
            @block.tensor
            def _(pe):
                def up(c):
                    for j in range(PER_CHUNK):
                        n = c * PER_CHUNK + j
                        if n >= 2:
                            need(pe, gated, n - 1)
                        for s in range(2):
                            last = nc.tensor.matmul(psum[:, 2 * (n % 2) + s, 0:Q4_HID], zt[:, n * P:(n + 1) * P],
                                                    gate_up[:, s * Q4_HID:(s + 1) * Q4_HID], start=True, stop=True)
                        last.then_inc(products.handle, 1)
                def down_product(c):
                    need(pe, ready, c + 1)
                    for m, (at, rows) in enumerate(Q4_PARTS):
                        for j in range(PER_CHUNK):
                            last = nc.tensor.transpose(psum[0:rows, 4 + m, j * P:(j + 1) * P], hidden_q[:, j, at:at + rows], core.ident[:])
                    last.then_inc(h_turned.handle, 1)
                    need(pe, h_taken, 3 * (c + 1))
                    if c >= 1:
                        need(pe, added, c)
                    for j in range(PER_CHUNK):
                        for m, (at, rows) in enumerate(Q4_PARTS):
                            last = nc.tensor.matmul(psum[:, 7, j * P:(j + 1) * P], hidden_t[0:rows, m, j * P:(j + 1) * P],
                                                    down[0:rows, m * P:(m + 1) * P], start=(m == 0), stop=(m == 2))
                    last.then_inc(out_made.handle, 1)

                up(0)
                for c in range(1, CHUNKS):
                    up(c)
                    down_product(c - 1)
                down_product(CHUNKS - 1)

            @block.scalar
            def _(act):
                def gate(c):
                    for j in range(PER_CHUNK):
                        n = c * PER_CHUNK + j
                        need(act, products, n + 1)
                        if n >= 2:
                            need(act, gated, n - 1)
                        nc.scalar.activation(act_gate[:, n % 2, :], psum[:, 2 * (n % 2), 0:Q4_HID], ACT.Silu).then_inc(silu.handle, 1)

                def take(c):
                    need(act, h_turned, c + 1)
                    if c:
                        need(act, out_made, c)
                    for m, (at, rows) in enumerate(Q4_PARTS):
                        nc.scalar.copy(hidden_t[0:rows, m, :], psum[0:rows, 4 + m, :]).then_inc(h_taken.handle, 1)

                gate(0)
                for c in range(1, CHUNKS):
                    gate(c)
                    take(c - 1)
                take(CHUNKS - 1)

            @block.vector
            def _(dve):
                link = Steps(dve, chain)

                def add(c):
                    need(dve, out_made, c + 1)
                    tiles = x[:, c * PER_CHUNK:(c + 1) * PER_CHUNK, :]
                    nc.vector.scalar_tensor_tensor(out=tiles, in0=psum[:, 7, :].rearrange("p (j n) -> p j n", j=PER_CHUNK), scalar=0.5,
                                                   in1=tiles, op0=ALU.mult, op1=ALU.add).then_inc(added.handle, 1)

                for c in range(CHUNKS):
                    for j in range(PER_CHUNK):
                        need(dve, silu, c * PER_CHUNK + j + 1)
                        nc.vector.tensor_tensor(hidden[:, j, :], psum[:, 2 * (j % 2) + 1, 0:Q4_HID], act_gate[:, j % 2, :],
                                                ALU.mult).then_inc(gated.handle, 1)
                    need(dve, gated, (c + 1) * PER_CHUNK)
                    if c:
                        need(dve, h_turned, c)
                    quantise(nc, link, hidden[:].rearrange("p j n -> p (j n)"), hidden_q[:].rearrange("p j n -> p (j n)"), tmp, ready)
                    need(dve, ready, c + 1)
                    if c:
                        add(c - 1)
                add(CHUNKS - 1)
                link.close()
        for tally, n in ((products, TILES), (silu, TILES), (gated, TILES), (ready, CHUNKS), (h_turned, CHUNKS),
                         (h_taken, 3 * CHUNKS), (out_made, CHUNKS), (added, CHUNKS)):
            tally.done += n



def l2_attn(core, area):
    nc, psum, x, y, zt = core.nc, core.psum, core.x, core.y, core.zt
    w = core.weights(area, L2_ATTN)
    H, D, T, W = FA_HEADS, FA_DIM, SEQ_TILES, WA_WIN
    GROUP = 3
    GROUPS = [(g, min(GROUP, H - g)) for g in range(0, H, GROUP)]
    SETS = [GROUPS[:len(GROUPS) // 2], GROUPS[len(GROUPS) // 2:]]
    COLS = 32
    QUADS = H // 4
    chain = core.sem("vector_chain")
    (feature_made, feature_taken, max_scores, tops, tops_turned, rows_ready, rows_stored, rows_placed, scores, probs, v_staged,
     v_used, sums_made, sums_taken, sums_turned, normed, cleared) = (core.sem(n) for n in (
        "wa_feature_product", "wa_feature_taken", "wa_max_scores", "wa_tops", "wa_tops_turned", "wa_rows_split", "wa_rows_stored",
        "wa_rows_placed", "wa_scores", "wa_probs", "wa_values_staged", "wa_values_used", "wa_sums", "wa_sums_taken", "wa_sums_turned", "wa_normed",
        "wa_values_cleared"))
    with ExitStack() as ctx:
        sb = lambda name, shape, dt=F32: ctx.enter_context(nc.sbuf_tensor(core.fresh(name), shape, dt))
        o = sb("wa_tokens", [P, TILES, P])
        normalise_block(core, x, y, 1e-5)
        normalise_block(core, y, o, 1e-5, affine(core, w("gamma"), w("beta")))
        spare = L2_FFN_HELD
        q_t, k_t = (core.areas[0][:, spare + i * TOKENS:spare + (i + 1) * TOKENS] for i in range(2))
        with nc.Block() as block:
            @block.tensor
            def _(pe):
                for n in range(2 * CHUNKS):
                    if n >= 4:
                        need(pe, feature_taken, n - 3)
                    nc.tensor.matmul(psum[:, n % 4, :], w("wq" if n < CHUNKS else "wk"), zt[:, n % CHUNKS * CHUNK:(n % CHUNKS + 1) * CHUNK],
                                     start=True, stop=True).then_inc(feature_made.handle, 1)

            @block.scalar
            def _(act):
                for n in range(2 * CHUNKS):
                    need(act, feature_made, n + 1)
                    to = q_t if n < CHUNKS else k_t
                    nc.scalar.copy(to[:, n % CHUNKS * CHUNK:(n % CHUNKS + 1) * CHUNK], psum[:, n % 4, :]).then_inc(feature_taken.handle, 1)
        feature_made.done += 2 * CHUNKS
        feature_taken.done += 2 * CHUNKS
        v = core.areas[0][:, spare + 2 * TOKENS:spare + 2 * TOKENS + TILES * H * (D + 1)].rearrange("p (t h e) -> p t h e", t=TILES, h=H)
        value_tokens(core, v, w("wv"), None)
        stacks = Stacks(core, ctx, W, W)
        prob = sb("wa_prob", [P, 2, H, BAND])
        tile_v = sb("wa_tile_values", [P, 2, H, COLS])
        sums = sb("wa_sums_copy", [P, CHUNK])
        top = sb("wa_top", [P, H, T])
        rows = sb("wa_rows", [P, 2, P], BF16)
        rec = sb("wa_rec", [P, H])
        max_dram = nc.dram_tensor("wa_max_dram", (2, H, SEQ), BF16).ap()
        with nc.Block() as block:
            @block.gpsimd
            def _(pool):
                nc.gpsimd.memset(tile_v[:], 0.0).then_inc(cleared.handle, 1)
        cleared.done += 1
        q_s, k_s = stacks.q[0:STACK], stacks.k[0:STACK]

        def banded(left, right, at_left, at_right, mask, half, first_bank):
            for g, (head, n) in enumerate(SETS[half]):
                bank = psum[:, first_bank + g, :]
                for h in range(n):
                    nc.tensor.matmul(bank[:, h * BAND:(h + 1) * BAND], left[:, head + h, bass.ds(at_left, P)],
                                     right[:, head + h, bass.ds(at_right, BAND)], start=(h == 0), stop=False, skip_group_check=True)
                last = nc.tensor.matmul(bank[:, 0:n * BAND], core.mask("ident"), mask.unsqueeze(1).to_broadcast([P, n, BAND]),
                                        start=False, stop=True, skip_group_check=True)
            return last

        def whole_and_rest(half):
            head, groups = SETS[half][0][0], SETS[half]
            whole = sum(n == GROUP for _, n in groups)
            parts = [(slice(head, head + whole * GROUP), 0, whole, GROUP)]
            if whole < len(groups):
                parts.append((slice(groups[whole][0], groups[whole][0] + groups[whole][1]), whole, 1, groups[whole][1]))
            return parts

        for b in range(BATCH):
            if b:
                stacks.fill_next(core, b)
            else:
                stacks.fill_first(core, q_t, k_t)
            with nc.Block() as block:
                @block.tensor
                def _(pe):
                    def tile(t, first):
                        for half in range(2):
                            if not first:
                                pe.wait_ge(tops.handle, tops.done + t * 2 + half - 1)
                            banded(q_s[0:MAX_ROWS], k_s[0:MAX_ROWS], t * P, t * P, core.mask("band_q")[:, bass.ds(t * BAND, BAND)],
                                   half, 3 * half).then_inc(max_scores.handle, 1)
                    tile(0, True)
                    with pe.Fori(1, T) as t:
                        tile(t, False)
                    need(pe, tops, 2 * T)
                    nc.tensor.transpose(psum[:, 6, 0:P], top[:].rearrange("p h t -> p (h t)"), core.ident[:]).then_inc(tops_turned.handle, 1)

                @block.vector
                def _(dve):
                    with dve.Fori(0, T) as t:
                        for half in range(2):
                            dve.wait_ge(max_scores.handle, max_scores.done + t * 2 + half + 1)
                            for heads, bank, banks, n in whole_and_rest(half):
                                last = nc.vector.tensor_reduce(top[:, heads, bass.ds(t, 1)].rearrange("p (g h) o -> p g (h o)", g=banks),
                                                               psum[:, 3 * half + bank:3 * half + bank + banks, 0:n * BAND].rearrange("p g (h k) -> p g h k", k=BAND),
                                                               AX.X, ALU.max, negate=True)
                            last.then_inc(tops.handle, 1)
                    link = Steps(dve, chain)
                    need(dve, tops_turned, 1)
                    link(nc.vector.tensor_copy(rows[:, 0, :], psum[:, 6, 0:P]))
                    nc.vector.tensor_tensor(rows[:, 1, :], psum[:, 6, 0:P], rows[:, 0, :], ALU.subtract).then_inc(rows_ready.handle, 1)
                    link.close()

                @block.sync
                def _(sp):
                    need(sp, rows_ready, 1)
                    sp.dma_start(max_dram.rearrange("i h (t p) -> (h t) i p", p=P), rows[:]).then_inc(rows_stored.handle, 16)
                    need(sp, rows_stored, 16)
                    sp.dma_start(stacks.q[MAX_ROWS:MAX_ROWS + 2, :, 0:SEQ], max_dram).then_inc(rows_placed.handle, 16)
                    need(sp, rows_placed, 16)
            for tally, n in ((max_scores, 2 * T), (tops, 2 * T), (tops_turned, 1), (rows_ready, 1), (rows_stored, 16), (rows_placed, 16)):
                tally.done += n
            with nc.Block() as block:
                @block.tensor
                def _(pe):
                    def scores_of(t, first):
                        for half in range(2):
                            if not first:
                                pe.wait_ge(probs.handle, probs.done + t * 2 + half - 1)
                            banded(k_s, q_s, t * P + W, t * P, core.mask("band_k"), half, 3 * half).then_inc(scores.handle, 1)

                    def sums_of(t, p, first, last_tile):
                        pe.wait_ge(v_staged.handle, v_staged.done + t + 1)
                        pe.wait_ge(probs.handle, probs.done + t * 2 + 2)
                        for j in range(QUADS):
                            for c in range(4):
                                last = nc.tensor.matmul(psum[COLS * c:COLS * (c + 1), 6 + p, j * P:(j + 1) * P], tile_v[:, p, 4 * j + c, :],
                                                        prob[:, p, 4 * j + c, 0:P], start=(first and j == 0), stop=(j == QUADS - 1),
                                                        tile_position=(0, COLS * c), skip_group_check=True)
                        last.then_inc(sums_made.handle, 1)
                        if last_tile:
                            return
                        if not first:
                            pe.wait_ge(normed.handle, normed.done + t)
                        for j in range(QUADS):
                            for c in range(4):
                                last = nc.tensor.matmul(psum[COLS * c:COLS * (c + 1), 7 - p, j * P:j * P + W], tile_v[:, p, 4 * j + c, :],
                                                        prob[:, p, 4 * j + c, P:BAND], start=(j == 0), stop=False,
                                                        tile_position=(0, COLS * c), skip_group_check=True)
                        last.then_inc(v_used.handle, 1)

                    def turn(t, p):
                        pe.wait_ge(sums_taken.handle, sums_taken.done + t + 1)
                        for j in range(QUADS):
                            last = nc.tensor.transpose(psum[:, 6 + p, j * P:(j + 1) * P], sums[:, j * P:(j + 1) * P], core.ident[:])
                        last.then_inc(sums_turned.handle, 1)

                    scores_of(0, True)
                    sums_of(0, 0, True, False)
                    scores_of(1, False)
                    turn(0, 0)
                    sums_of(1, 1, False, False)
                    with pe.Fori(1, T // 2 - 1) as i:
                        for p in range(2):
                            scores_of(i * 2 + p, False)
                            turn(i * 2 + p - 1, 1 - p)
                            sums_of(i * 2 + p, p, False, False)
                    for t in (T - 2, T - 1):
                        scores_of(t, False)
                        turn(t - 1, (t - 1) % 2)
                        sums_of(t, t % 2, False, t == T - 1)
                    turn(T - 1, (T - 1) % 2)

                @block.scalar
                def _(act):
                    def exp(t, p, first):
                        for half in range(2):
                            act.wait_ge(scores.handle, scores.done + t * 2 + half + 1)
                            if not first and half == 0:
                                act.wait_ge(v_used.handle, v_used.done + t - 1)
                            for heads, bank, banks, n in whole_and_rest(half):
                                last = nc.scalar.activation(prob[:, p, heads, :].rearrange("p (g h) k -> p g (h k)", g=banks),
                                                            psum[:, 3 * half + bank:3 * half + bank + banks, 0:n * BAND], ACT.Exp,
                                                            scale=float(D) ** -0.5)
                            last.then_inc(probs.handle, 1)

                    def take(t, p, first):
                        act.wait_ge(sums_made.handle, sums_made.done + t + 1)
                        if not first:
                            act.wait_ge(sums_turned.handle, sums_turned.done + t)
                        nc.scalar.copy(sums[:], psum[:, 6 + p, :]).then_inc(sums_taken.handle, 1)

                    exp(0, 0, True)
                    take(0, 0, True)
                    exp(1, 1, True)
                    take(1, 1, False)
                    with act.Fori(1, T // 2) as i:
                        for p in range(2):
                            exp(i * 2 + p, p, False)
                            take(i * 2 + p, p, False)

                @block.vector
                def _(dve):
                    with dve.Fori(0, T // 2) as i:
                        link = Steps(dve, chain, 2, i)
                        for p in range(2):
                            dve.wait_ge(sums_turned.handle, sums_turned.done + i * 2 + p + 1)
                            got = psum[:, 6 + p, :].rearrange("p (h e) -> p h e", e=COLS)
                            link(nc.vector.reciprocal(rec[:], got[:, :, D]))
                            nc.vector.tensor_tensor(o[:].rearrange("p t (h d) -> p t h d", h=H)[:, bass.ds(b * T + i * 2 + p, 1)],
                                                    got[:, :, 0:D].unsqueeze(1),
                                                    rec[:].unsqueeze(1).unsqueeze(3).to_broadcast([P, 1, H, D]), ALU.mult).then_inc(normed.handle, 1)
                            dve.wait_ge(normed.handle, normed.done + i * 2 + p + 1)
                    link.close(T // 2)

                @block.gpsimd
                def _(pool):
                    def stage(t, p):
                        nc.gpsimd.tensor_copy(tile_v[:, p, :, 0:D + 1].unsqueeze(1), v[:, bass.ds(b * T + t, 1), :, :]).then_inc(v_staged.handle, 1)
                    stage(0, 0)
                    stage(1, 1)
                    with pool.Fori(1, T // 2) as i:
                        for p in range(2):
                            pool.wait_ge(v_used.handle, v_used.done + i * 2 + p - 1)
                            stage(i * 2 + p, p)
            for tally, n in ((scores, 2 * T), (probs, 2 * T), (sums_made, T), (v_used, T - 1), (v_staged, T), (sums_taken, T), (sums_turned, T), (normed, T)):
                tally.done += n
        normalise_block(core, x, o, 1e-5, plain(core), only_transpose=True)
        tokens_product(core, w("wout"), add_to_x(core, also=y))



def l3_attn(core, area):
    nc, psum, x, y, zt = core.nc, core.psum, core.x, core.y, core.zt
    w = core.weights(area, L3_ATTN)
    L, S = RA_STEP, RA_SEG
    K = 3
    chain, made, taken = core.sem("vector_chain"), core.sem("ra_product"), core.sem("ra_activated")
    with ExitStack() as ctx:
        sb = lambda name, shape, dt=F32: ctx.enter_context(nc.sbuf_tensor(core.fresh(name), shape, dt))
        normalise_block(core, x, y, 1e-5, plain(core))
        q, k, v, g, beta = (sb(n, [P, TOKENS]) for n in ("ra_q", "ra_k", "ra_v", "ra_g", "ra_beta"))
        decay = sb("ra_decay_gates", [P, 2, TOKENS])
        runs = [("wq", q[:], ACT.Silu, None), ("wk", k[:], ACT.Silu, None), ("wv", v[:], ACT.Silu, None),
                ("wg", g[:], ACT.Sigmoid, None), ("wb", beta[:], ACT.Sigmoid, None),
                ("wfd", decay[:, 0, :], ACT.Sigmoid, "bfd"), ("wsd", decay[:, 1, :], ACT.Sigmoid, "bsd")]
        N = len(runs)
        with nc.Block() as block:
            @block.tensor
            def _(pe):
                for r, (name, _, _, _) in enumerate(runs):
                    for c in range(CHUNKS):
                        n = r * CHUNKS + c
                        if n >= 4:
                            need(pe, taken, n - 3)
                        nc.tensor.matmul(psum[:, n % 4, :], w(name), zt[:, c * CHUNK:(c + 1) * CHUNK],
                                         start=True, stop=True).then_inc(made.handle, 1)

            @block.scalar
            def _(act):
                for r, (_, out, func, bias) in enumerate(runs):
                    for c in range(CHUNKS):
                        n = r * CHUNKS + c
                        need(act, made, n + 1)
                        nc.scalar.activation(out[:, c * CHUNK:(c + 1) * CHUNK], psum[:, n % 4, :], func,
                                             bias=0.0 if bias is None else w(bias)).then_inc(taken.handle, 1)

            @block.vector
            def _(dve):
                link = Steps(dve, chain)
                need(dve, taken, 3 * CHUNKS)
                link(nc.vector.scalar_tensor_tensor(out=k[:], in0=k[:], scalar=1.0 + RA_MIX, in1=v[:], op0=ALU.mult, op1=ALU.mult))
                need(dve, taken, 4 * CHUNKS)
                nc.vector.scalar_tensor_tensor(out=q[:], in0=q[:], scalar=0.5, in1=g[:], op0=ALU.mult, op1=ALU.mult)
                need(dve, taken, 5 * CHUNKS)
                link(nc.vector.tensor_tensor(k[:], k[:], beta[:], ALU.mult))
                link.close()
        made.done += N * CHUNKS
        taken.done += N * CHUNKS

        states = sb("ra_states", [P, 2, K, S])
        faded = sb("ra_faded", [P, 2, 2, K, S])
        read = sb("ra_read", [P, K, S, L])
        starts = sb("ra_starts", [P, 2, S])
        composed = sb("ra_composed", [P, 2, 2, K, S])
        reads_in, reads_made = core.sem("ra_faded"), core.sem("ra_read")
        PER_LOOP = 4
        seg = S // BATCH
        state2 = lambda t: t.rearrange("p a k s -> p a (k s)")
        u = k[:].rearrange("p (s l) -> p s l", l=L)
        fades = decay[:].rearrange("p a (s l) -> p a s l", l=L)
        with nc.Block() as block:
            @block.gpsimd
            def _(pool):
                with pool.Fori(0, L // PER_LOOP) as i:
                    for e in range(PER_LOOP):
                        pool.wait_ge(reads_in.handle, reads_in.done + i * PER_LOOP + e + 1)
                        nc.gpsimd.tensor_tensor(read[:, :, :, bass.ds(i * PER_LOOP + e, 1)].rearrange("p k s l -> p k (s l)"), faded[:, e % 2, 0],
                                                faded[:, e % 2, 1], ALU.add).then_inc(reads_made.handle, 1)

            @block.vector
            def _(dve):
                link = Steps(dve, chain)
                link(nc.vector.memset(states[:], 0.0))
                nc.vector.memset(states[:, 0, 1, :], 1.0)
                nc.vector.memset(starts[:], 0.0)
                link(nc.vector.memset(states[:, 1, 2, :], 1.0))

                def step(t, parity, link):
                    nc.vector.tensor_tensor(faded[:, parity], states[:],
                                            fades[:, :, :, bass.ds(t, 1)].rearrange("p a s l -> p a (s l)").unsqueeze(2)
                                            .to_broadcast([P, 2, K, S]), ALU.mult).then_inc(reads_in.handle, 1)
                    dve.wait_ge(reads_in.handle, reads_in.done + t + 1)
                    link(nc.vector.scalar_tensor_tensor(out=state2(states[:]), in0=state2(faded[:, parity])[:, ::-1, :], scalar=RA_MIX,
                                                        in1=state2(faded[:, parity]), op0=ALU.mult, op1=ALU.add))
                    link(nc.vector.tensor_tensor(states[:, :, 0, :], states[:, :, 0, :],
                                                 u[:, :, bass.ds(t, 1)].rearrange("p s l -> p (s l)").unsqueeze(1).to_broadcast([P, 2, S]),
                                                 ALU.add))
                for t in range(PER_LOOP):
                    if t >= 2:
                        need(dve, reads_made, t - 1)
                    step(t, t % 2, link)
                link.close()
                with dve.Fori(1, L // PER_LOOP) as i:
                    link = Steps(dve, chain, 2 * PER_LOOP, i - 1)
                    for e in range(PER_LOOP):
                        dve.wait_ge(reads_made.handle, reads_made.done + i * PER_LOOP + e - 1)
                        step(i * PER_LOOP + e, e % 2, link)
                link.close(L // PER_LOOP - 1)
                need(dve, reads_made, L)
                link = Steps(dve, chain)
                by_seq = lambda t: t.rearrange("p k (b c) -> p k b c", b=BATCH)
                distance = 1
                while distance < seg:
                    late, early = slice(distance, seg), slice(0, seg - distance)
                    for a in range(2):
                        for e in range(2):
                            last = nc.vector.tensor_tensor(by_seq(composed[:, a, e])[:, :, :, late],
                                                           by_seq(states[:, a, 1 + e:2 + e, :])[:, :, :, late].to_broadcast([P, K, BATCH, seg - distance]),
                                                           by_seq(states[:, e])[:, :, :, early], ALU.mult)
                    link(last)
                    for a in range(2):
                        last = nc.vector.tensor_tensor(by_seq(composed[:, a, 0, 0:1, :])[:, :, :, late], by_seq(composed[:, a, 0, 0:1, :])[:, :, :, late],
                                                       by_seq(states[:, a, 0:1, :])[:, :, :, late], ALU.add)
                    link(last)
                    for a in range(2):
                        last = nc.vector.tensor_tensor(by_seq(states[:, a])[:, :, :, late], by_seq(composed[:, a, 0])[:, :, :, late],
                                                       by_seq(composed[:, a, 1])[:, :, :, late], ALU.add)
                    link(last)
                    distance *= 2
                link(nc.vector.tensor_copy(by_seq(starts[:])[:, :, :, 1:seg], by_seq(states[:, :, 0, :])[:, :, :, 0:seg - 1]))
                link.close()
                link = Steps(dve, chain)
                flat = lambda t: t.rearrange("p s l -> p (s l)")
                for a in range(2):
                    link(nc.vector.tensor_tensor(read[:, 1 + a], read[:, 1 + a], starts[:, a, 0:S].unsqueeze(2).to_broadcast([P, S, L]), ALU.mult))
                link(nc.vector.tensor_tensor(read[:, 0], read[:, 0], read[:, 1], ALU.add))
                link(nc.vector.tensor_tensor(read[:, 0], read[:, 0], read[:, 2], ALU.add))
                link(nc.vector.tensor_tensor(zt[:, 0:TOKENS], flat(read[:, 0]), q[:], ALU.mult))
                link.close()
        reads_in.done += L
        reads_made.done += L
        tokens_product(core, w("wo"), add_to_x(core))


def fetch(core, area, source):
    ready = core.sem(f"weights_{'ab'[area]}_arrived")
    with core.nc.Block() as block:
        @block.sync
        def _(sp):
            sp.dma_start(core.areas[area][:, 0:source.shape[1]], source).then_inc(ready.handle, 16)
    ready.done += 16


def arrived(core, area):
    ready = core.sem(f"weights_{'ab'[area]}_arrived")
    with core.nc.Block() as block:
        @block.sync
        def _(sp):
            sp.wait_ge(ready.handle, ready.done)


STAGES = [("L0_ffn", l0_ffn, 0), ("L0_attn", l0_attn, 1), ("L0_ffn", l0_ffn, 0),
          ("L1_ffn", ternary_ffn, 1), ("L1_attn", l1_attn, 0), ("L1_ffn", ternary_ffn, 1),
          ("L2_ffn", l2_ffn, 0), ("L2_attn", l2_attn, 1), ("L2_ffn", l2_ffn, 0),
          ("L3_ffn", ternary_ffn, 1), ("L3_attn", l3_attn, 0), ("L3_ffn", ternary_ffn, 1)]


def macaron_d4(nc, x_in, blobs, out, stages=STAGES):
    with ExitStack() as ctx:
        core = Core(nc, ctx)
        loaded = core.sem("inputs_arrived")
        stored = core.sem("output_stored")
        half = core.sem("constants_set")
        with nc.Block() as block:
            @block.sync
            def _(sp):
                sp.dma_start(core.x[:], x_in.rearrange("b (i p) d -> p (b i) d", p=P)).then_inc(loaded.handle, 16)
                sp.dma_start(core.ident[:], blobs["constants"]).then_inc(loaded.handle, 16)
                sp.wait_ge(loaded.handle, 32)

            @block.gpsimd
            def _(pool):
                pool.dma_start(core.masks[:], blobs["masks"]).then_inc(core.sem("masks_arrived").handle, 16)
                nc.gpsimd.memset(core.minus_half[:], -0.5).then_inc(half.handle, 1)
                nc.gpsimd.memset(core.zt[:], 0.0).then_inc(half.handle, 1)
                pool.wait_ge(core.sem("masks_arrived").handle, 16)
        held = [None, None]

        def fetch_for(n):
            name, _, area = stages[n]
            if held[area] != name:
                fetch(core, area, blobs[name])
                held[area] = name
        fetch_for(0)
        for n, (_, stage, area) in enumerate(stages):
            if n + 1 < len(stages) and stages[n + 1][2] != area:
                fetch_for(n + 1)
            arrived(core, area)
            stage(core, area)
            if n + 1 < len(stages) and stages[n + 1][2] == area:
                fetch_for(n + 1)
        with nc.Block() as block:
            @block.sync
            def _(sp):
                sp.dma_start(out.rearrange("b (i p) d -> p (b i) d", p=P), core.x[:]).then_inc(stored.handle, 16)
                sp.wait_ge(stored.handle, 16)


def _pack(layout, arrays):
    import numpy as np
    cols = []
    for name, n in layout:
        a = arrays[name]
        a = a.reshape(a.shape[0], -1)
        assert a.shape[1] == n, (name, a.shape, n)
        if a.shape[0] < 128:
            a = np.concatenate([a, np.zeros((128 - a.shape[0], n), a.dtype)])
        cols.append(a)
    return np.ascontiguousarray(np.concatenate(cols, axis=1))


def _rows(w, part=128):
    import numpy as np
    n = -(-w.shape[0] // part)
    w = np.concatenate([w, np.zeros((n * part - w.shape[0], w.shape[1]), w.dtype)])
    return w.reshape(n, part, w.shape[1]).transpose(1, 0, 2).reshape(part, -1)


def _all_rows(v):
    import numpy as np
    return np.broadcast_to(v[None, :], (128, v.shape[0]))


def _tables():
    import numpy as np
    f = np.float32
    out = {}
    t = np.arange(1024, dtype=f)
    hi = np.arange(0, 64, 2, dtype=f)
    inv = (f(1.0) / f(10000.0) ** (hi / f(64))).astype(f)
    fr = (t[:, None] * inv[None, :]).astype(f)
    fr = np.concatenate([fr, fr], -1)
    base = ((hi + f(0.4 * 64)) / f(1.4 * 64)).astype(f)
    power = ((t - 512) / f(32)).astype(f)
    scale = (base[None, :] ** power[:, None]).astype(f)
    scale = np.concatenate([scale, scale], -1)
    cos, sin = np.cos(fr), np.sin(fr)
    sign = np.concatenate([-np.ones(32, f), np.ones(32, f)])
    tok = lambda a: a.astype(f).reshape(8, 128, 64).transpose(1, 0, 2).reshape(128, -1)
    out["xpos"] = {"cq": tok(cos * scale), "sq": tok(sin * scale * sign), "ck": tok(cos / scale), "sk": tok(sin / scale * sign)}
    inv = (f(1.0) / f(10000.0) ** (np.arange(8, dtype=f) / f(8))).astype(f)
    fr = (t[:, None] * inv[None, :]).astype(f)
    c = np.zeros((4, 32, 1024), f)
    s = np.zeros((4, 32, 1024), f)
    c[:, :8] = c[:, 8:16] = np.cos(fr).T
    s[:, :8], s[:, 8:16] = -np.sin(fr).T, np.sin(fr).T
    out["ga"] = (c.reshape(128, 1024), s.reshape(128, 1024))
    inv = (f(1.0) / f(10000.0) ** (np.arange(0, 8, 2, dtype=f) / f(8))).astype(f)
    fr = (t[:, None] * inv[None, :]).astype(f)
    c8 = np.repeat(np.cos(fr), 2, -1).T
    s8 = np.repeat(np.sin(fr), 2, -1).T * np.array([-1] * 4 + [1] * 4, f)[:, None]
    out["fa"] = (np.tile(c8, (16, 1)).astype(f), np.tile(s8, (16, 1)).astype(f))
    off = f(-1e30)
    q, k = np.arange(64)[:, None], np.arange(128)[None, :]
    local = np.where((k >= q) & (k <= q + 64), f(0), off).astype(f)
    first = np.where(k < 64, off, local).astype(f)
    masks = np.zeros((128, 16, 128), f)
    for i in range(16):
        masks[:64, i] = np.roll(first if i % 8 == 0 else local, 64, axis=1)
        masks[64:, i] = local
    j, i = np.arange(128)[:, None], np.arange(128)[None, :]
    causal = np.where(j <= i, f(0), off).astype(f)
    q, k = np.arange(128)[:, None], np.arange(160)[None, :] - 32
    band_q = np.where((k <= q) & (k >= q - 32), f(0), off).astype(f)
    band_q0 = np.where((k <= q) & (k >= q - 32) & (k >= 0), f(0), off).astype(f)
    k, q = np.arange(128)[:, None], np.arange(160)[None, :]
    band_qs = np.concatenate([band_q0] + [band_q] * 7, 1)
    band_k = np.where((k <= q) & (k >= q - 32), f(0), off).astype(f)
    out["masks"] = {"ident": np.eye(128, dtype=f), "local": masks.reshape(128, -1), "causal": causal,
                    "band_q": band_qs, "band_k": band_k}
    out["upper"] = (j <= i).astype(f)
    d = (np.arange(128)[:, None] // 32 == np.arange(64)[None, :] // 16).astype(f)
    out["diag"] = np.concatenate([d, d], 1)
    return out


def _blobs(a):
    import numpy as np
    tb = _tables()
    parts = {}
    r = {}
    for l in range(2):
        w1, w2, b1 = a["L0_ffn_w1"][l], a["L0_ffn_w2"][l], a["L0_ffn_b1"][l]
        col = lambda b: _rows(b[:, None])
        qs, ks = a["L0_ffn_q_scale"][l], a["L0_ffn_k_scale"][l]
        r.update({f"wqkv{l}": a["L0_ffn_wqkv"][l], f"wo{l}": _rows(a["L0_ffn_wo"][l]), f"w1{l}": w1, f"w2{l}": _rows(w2),
                  f"qs{l}": _all_rows(qs), f"ks{l}": _all_rows(ks), f"lg{l}": a["L0_ffn_ln_g"][l][:, None],
                  f"lb{l}": a["L0_ffn_ln_b"][l][:, None], f"b1a{l}": col(b1[:341]), f"b1g{l}": col(b1[341:]),
                  f"b2{l}": _all_rows(a["L0_ffn_b2"][l])})
    r.update(tb["xpos"])
    parts["L0_ffn"] = r

    def spaced(w, swap=False):
        w = w.reshape(8, 16, 128)
        if swap:
            w = np.concatenate([w[:, 8:], w[:, :8]], 1)
        w = np.concatenate([w, np.zeros_like(w)], 1).reshape(256, 128)
        return w.T
    A = "L0_attn_"
    parts["L0_attn"] = {"wq": spaced(a[A + "Wq"]), "wqs": spaced(a[A + "Wq"], True), "wk": spaced(a[A + "Wk"]),
                        "wks": spaced(a[A + "Wk"], True),
                        "wvg": np.concatenate([a[A + "Wv"], a[A + "Wbeta"], a[A + "Wig"], a[A + "Wog"]]).T,
                        "wout": a[A + "Wout"].T, "bg": _all_rows(np.concatenate([a[A + "bbeta"], a[A + "big"], a[A + "bog"]])),
                        "bout": _all_rows(a[A + "bout"]), "nw": a[A + "norm_w"][:, None],
                        "cos": tb["ga"][0], "sin": tb["ga"][1], "upper": tb["upper"], "diag": tb["diag"]}
    for L in ("L1_ffn", "L3_ffn"):
        g = lambda n: a[f"{L}_{n}"]
        col = lambda v: _rows(v[:, None])
        parts[L] = {"w1": g("w1_w").T, "w2": g("w2_w").T, "h1": _rows(g("h1_w").T), "h2": _rows(g("h2_w").T),
                    "w3": _rows(g("w3_w").T), "s1": col(g("w1_s")), "s2": col(g("w2_s")), "t1": col(g("h1_s")),
                    "t2": col(g("h2_s")), "s3": _all_rows(g("w3_s"))}
    swap8 = lambda w: w.reshape(16, 2, 4, -1)[:, ::-1].reshape(128, -1)
    A = "L1_attn_"
    parts["L1_attn"] = {"wq": a[A + "wq"].T, "wqs": swap8(a[A + "wq"]).T, "wk": a[A + "wk"].T, "wks": swap8(a[A + "wk"]).T,
                        "wv": a[A + "wv"].T, "wo": a[A + "wo"].T, "bq": a[A + "bq"][:, None], "bqs": swap8(a[A + "bq"]),
                        "bk": a[A + "bk"][:, None], "bks": swap8(a[A + "bk"]), "bv": _all_rows(a[A + "bv"]),
                        "bo": _all_rows(a[A + "bo"]), "cos": tb["fa"][0], "sin": tb["fa"][1]}
    parts["L2_ffn"] = {"wg": _rows(a["L2_ffn_w_gate"]), "wu": _rows(a["L2_ffn_w_up"]), "wd": a["L2_ffn_w_down"]}
    W = a["L2_attn_W_qkv"]
    parts["L2_attn"] = {"wq": W[:128].T, "wk": W[128:256].T, "wv": W[256:].T, "wout": a["L2_attn_W_out"].T,
                        "gamma": a["L2_attn_gamma"][:, None], "beta": a["L2_attn_beta"][:, None]}
    A = "L3_attn_"
    rep = lambda w: np.repeat(w, 8, axis=0)
    parts["L3_attn"] = {"wq": a[A + "Wq"].T, "wk": a[A + "Wk"].T, "wv": a[A + "Wv"].T, "wg": a[A + "Wg"].T,
                        "wb": rep(a[A + "Wb"]).T, "wfd": rep(a[A + "Wfd"]).T, "wsd": rep(a[A + "Wsd"]).T,
                        "wo": a[A + "Wo"].T, "bfd": rep(a[A + "bfd"])[:, None], "bsd": rep(a[A + "bsd"])[:, None]}
    blobs = {name: _pack(LAYOUTS[name], parts[name]) for name in LAYOUTS}
    blobs["constants"] = np.eye(128, dtype=np.float32)
    blobs["masks"] = _pack(MASKS, tb["masks"])
    return blobs


def kernel(**inputs):
    import numpy as _np
    import concourse.bacc as _bacc
    from concourse import mybir as _mybir
    from concourse.bass_utils import run_bass_kernel_spmd as _run

    nc = _bacc.Bacc("TRN2", target_bir_lowering=False, num_devices=1)
    given = {k: _np.asarray(v) for k, v in inputs.items()}
    arrays = {"in_x": _np.ascontiguousarray(given["L0_attn_x"])}
    arrays.update({f"in_{k}": v for k, v in _blobs(given).items()})
    args = {k: nc.dram_tensor(k, v.shape, _mybir.dt.from_np(v.dtype), kind="ExternalInput").ap() for k, v in arrays.items()}
    out = nc.dram_tensor("out_x", (BATCH, SEQ, P), F32, kind="ExternalOutput").ap()
    macaron_d4(nc, args["in_x"], {k[3:]: v for k, v in args.items()}, out)
    r = _run(nc, [arrays], core_ids=[0])
    return r.results[0]["out_x"]
```
